# Optimizing a Trainium2 kernel written in Bass

```python
import numpy as np
import jax
import jax.numpy as jnp

def _softmax(x, axis=-1):
    return jax.nn.softmax(x, axis=axis)

def _gelu(x):
    return jax.nn.gelu(x, approximate=True)

def _silu(x):
    return jax.nn.silu(x)

def _sigmoid(x):
    return jax.nn.sigmoid(x)

def _layernorm(x, axis=-1, eps=1e-05):
    m = jnp.mean(x, axis=axis, keepdims=True)
    v = jnp.var(x, axis=axis, keepdims=True)
    return (x - m) / jnp.sqrt(v + eps)

def _scatter_add(tgt, idx, src, axis=0):
    return tgt.at[idx].add(src)

def _segment_sum(src, seg, n):
    return jax.ops.segment_sum(src, seg, n)
kernel_name = 'mk_gnn_resnorm_d4_gnn_r64_220398'

def setup_inputs(seed: int=0):
    np.random.seed(seed)
    _w = jnp.asarray

    def _rec_inputs():
        import jax
        import jax.numpy as jnp
        _gk = jax.random.key(seed)
        x = -0.0003713 + 1 * jax.random.normal(jax.random.fold_in(_gk, 1), (50000, 128), jnp.float32)
        _s = jax.random.randint(jax.random.fold_in(_gk, 2), (6250,), 0, 50000, jnp.int32)
        _d = jax.random.randint(jax.random.fold_in(_gk, 3), (6250,), 0, 50000, jnp.int32)
        _loop = jnp.arange(50000, dtype=jnp.int32)
        src = jnp.concatenate([_s, _d, _loop])
        dst = jnp.concatenate([_d, _s, _loop])
        _o = jnp.argsort(dst, stable=True)
        src = src[_o]
        dst = dst[_o]
        return (x, src, dst)
    x, src, dst = _rec_inputs()

    def _L0_gnn_setup():
        import jax, jax.numpy as jnp
        import numpy as np
        N = 100000
        E = 12500
        D = 128
        OUT = 128
        key = jax.random.key(seed)
        k = jax.random.split(key, 6)
        x = jax.random.normal(k[0], (N, D), dtype=jnp.float32)
        edge_index = jax.random.randint(k[1], (2, E), 0, N, dtype=jnp.int64)
        Wl = jax.random.normal(k[2], (D, OUT), dtype=jnp.float32) / np.sqrt(D)
        bl = jax.random.normal(k[3], (OUT,), dtype=jnp.float32) * 0.01
        Wr = jax.random.normal(k[4], (D, OUT), dtype=jnp.float32) / np.sqrt(D)
        br = jax.random.normal(k[5], (OUT,), dtype=jnp.float32) * 0.01
        return {'x': x, 'edge_index': edge_index, 'Wl': Wl, 'bl': bl, 'Wr': Wr, 'br': br}
    _L0_gnn_all = _L0_gnn_setup()
    _L0_gnn_in = {k: v for k, v in _L0_gnn_all.items() if k in ('Wl', 'bl', 'Wr', 'br')}
    del _L0_gnn_all

    def _L1_gnn_setup():
        import jax, jax.numpy as jnp
        import numpy as np
        N_NODES = 50000
        N_EDGES = 9375
        DIM_H = 128
        LN_EPS = 1e-05

        def _layer_norm(x, gamma, beta):
            mu = jnp.mean(x, axis=-1, keepdims=True)
            var = jnp.mean(jnp.square(x - mu), axis=-1, keepdims=True)
            return gamma * (x - mu) * jax.lax.rsqrt(var + LN_EPS) + beta
        key = jax.random.key(seed)
        ks = jax.random.split(key, 8)
        s = 1.0 / np.sqrt(DIM_H)
        return {'nodes': jax.random.normal(ks[0], (N_NODES, DIM_H), jnp.float32), 'W_msg': jax.random.normal(ks[1], (DIM_H, DIM_H), jnp.float32) * s, 'b_msg': jnp.zeros((DIM_H,), jnp.float32), 'w_ih': jax.random.normal(ks[2], (3 * DIM_H, DIM_H), jnp.float32) * s, 'w_hh': jax.random.normal(ks[3], (3 * DIM_H, DIM_H), jnp.float32) * s, 'b_ih': jnp.zeros((3 * DIM_H,), jnp.float32), 'b_hh': jnp.zeros((3 * DIM_H,), jnp.float32), 'ln_gamma': jnp.ones((DIM_H,), jnp.float32), 'ln_beta': jnp.zeros((DIM_H,), jnp.float32), 'edge_src': jax.random.randint(ks[4], (N_EDGES,), 0, N_NODES, jnp.int32), 'edge_dst': jax.random.randint(ks[5], (N_EDGES,), 0, N_NODES, jnp.int32)}
    _L1_gnn_all = _L1_gnn_setup()
    _L1_gnn_in = {k: v for k, v in _L1_gnn_all.items() if k in ('W_msg', 'b_msg', 'w_ih', 'w_hh', 'b_ih', 'b_hh', 'ln_gamma', 'ln_beta')}
    del _L1_gnn_all

    def _L2_gnn_setup():
        import jax, jax.numpy as jnp
        import numpy as np
        N = 50000
        E = 12500
        IN_DIM = 128
        OUT_DIM = 128
        key = jax.random.key(seed)
        k1, k2, k3, k4, k5, k6 = jax.random.split(key, 6)
        x = jax.random.normal(k1, (N, IN_DIM), dtype=jnp.float32)
        edge_index = jax.random.randint(k2, (2, E), 0, N, dtype=jnp.int64)
        bound = 1.0 / np.sqrt(IN_DIM)
        w_self = jax.random.uniform(k3, (OUT_DIM, IN_DIM), minval=-bound, maxval=bound, dtype=jnp.float32)
        b_self = jax.random.uniform(k4, (OUT_DIM,), minval=-bound, maxval=bound, dtype=jnp.float32)
        w_neigh = jax.random.uniform(k5, (OUT_DIM, IN_DIM), minval=-bound, maxval=bound, dtype=jnp.float32)
        b_neigh = jax.random.uniform(k6, (OUT_DIM,), minval=-bound, maxval=bound, dtype=jnp.float32)
        return {'x': x, 'edge_index': edge_index, 'w_self': w_self, 'b_self': b_self, 'w_neigh': w_neigh, 'b_neigh': b_neigh}
    _L2_gnn_all = _L2_gnn_setup()
    _L2_gnn_in = {k: v for k, v in _L2_gnn_all.items() if k in ('w_self', 'b_self', 'w_neigh', 'b_neigh')}
    del _L2_gnn_all

    def _L3_gnn_setup():
        import jax, jax.numpy as jnp
        import numpy as np
        N = 10000
        E = 10000
        D = 128
        EPS = 1e-08

        def _gcn_conv(x, src, dst, deg_isqrt, W, b, n):
            h = x @ W
            norm = deg_isqrt[src] * deg_isqrt[dst]
            msgs = h[src] * norm[:, None]
            out = jax.ops.segment_sum(msgs, dst, num_segments=n)
            return out + b

        def _pairnorm_pn(x):
            norm = jnp.sqrt(jnp.sum(x * x, axis=1, keepdims=True)) + EPS
            return x / norm
        key = jax.random.key(seed)
        ks = jax.random.split(key, 8)
        x = jax.random.normal(ks[0], (N, D), dtype=jnp.float32)
        edge_index = jax.random.randint(ks[1], (2, E), 0, N, dtype=jnp.int64)
        scale = 1.0 / np.sqrt(D)
        W1 = jax.random.normal(ks[2], (D, D), dtype=jnp.float32) * scale
        b1 = jnp.zeros((D,), dtype=jnp.float32)
        W2 = jax.random.normal(ks[3], (D, D), dtype=jnp.float32) * scale
        b2 = jnp.zeros((D,), dtype=jnp.float32)
        W3 = jax.random.normal(ks[4], (D, D), dtype=jnp.float32) * scale
        b3 = jnp.zeros((D,), dtype=jnp.float32)
        return {'x': x, 'edge_index': edge_index, 'W1': W1, 'b1': b1, 'W2': W2, 'b2': b2, 'W3': W3, 'b3': b3}
    _L3_gnn_all = _L3_gnn_setup()
    _L3_gnn_in = {k: v for k, v in _L3_gnn_all.items() if k in ('W1', 'b1', 'W2', 'b2', 'W3', 'b3')}
    del _L3_gnn_all
    return {'x': x, 'src': src, 'dst': dst, 'L0_gnn_Wl': _L0_gnn_in['Wl'], 'L0_gnn_bl': _L0_gnn_in['bl'], 'L0_gnn_Wr': _L0_gnn_in['Wr'], 'L0_gnn_br': _L0_gnn_in['br'], 'L1_gnn_W_msg': _L1_gnn_in['W_msg'], 'L1_gnn_b_msg': _L1_gnn_in['b_msg'], 'L1_gnn_w_ih': _L1_gnn_in['w_ih'], 'L1_gnn_w_hh': _L1_gnn_in['w_hh'], 'L1_gnn_b_ih': _L1_gnn_in['b_ih'], 'L1_gnn_b_hh': _L1_gnn_in['b_hh'], 'L1_gnn_ln_gamma': _L1_gnn_in['ln_gamma'], 'L1_gnn_ln_beta': _L1_gnn_in['ln_beta'], 'L2_gnn_w_self': _L2_gnn_in['w_self'], 'L2_gnn_b_self': _L2_gnn_in['b_self'], 'L2_gnn_w_neigh': _L2_gnn_in['w_neigh'], 'L2_gnn_b_neigh': _L2_gnn_in['b_neigh'], 'L3_gnn_W1': _L3_gnn_in['W1'], 'L3_gnn_b1': _L3_gnn_in['b1'], 'L3_gnn_W2': _L3_gnn_in['W2'], 'L3_gnn_b2': _L3_gnn_in['b2'], 'L3_gnn_W3': _L3_gnn_in['W3'], 'L3_gnn_b3': _L3_gnn_in['b3']}

def reference(x, src, dst, L0_gnn_Wl, L0_gnn_bl, L0_gnn_Wr, L0_gnn_br, L1_gnn_W_msg, L1_gnn_b_msg, L1_gnn_w_ih, L1_gnn_w_hh, L1_gnn_b_ih, L1_gnn_b_hh, L1_gnn_ln_gamma, L1_gnn_ln_beta, L2_gnn_w_self, L2_gnn_b_self, L2_gnn_w_neigh, L2_gnn_b_neigh, L3_gnn_W1, L3_gnn_b1, L3_gnn_W2, L3_gnn_b2, L3_gnn_W3, L3_gnn_b3):
    import jax
    import jax.numpy as jnp

    def _L0_gnn_ref(x, edge_index, Wl, bl, Wr, br):
        import jax, jax.numpy as jnp
        import numpy as np
        N = 100000
        E = 12500
        D = 128
        OUT = 128
        n = x.shape[0]
        tgt = edge_index[0]
        nbr = edge_index[1]
        agg_sum = jax.ops.segment_sum(x[nbr], tgt, num_segments=n)
        deg = jax.ops.segment_sum(jnp.ones((edge_index.shape[1],), x.dtype), tgt, num_segments=n)
        agg = agg_sum / jnp.maximum(deg, 1.0)[:, None]
        out = jax.nn.relu(x @ Wl + bl + agg @ Wr + br)
        norm = jnp.linalg.norm(out, axis=1, keepdims=True) + 1e-06
        return out / norm

    def _L1_gnn_ref(nodes, W_msg, b_msg, w_ih, w_hh, b_ih, b_hh, ln_gamma, ln_beta, edge_src, edge_dst):
        import jax, jax.numpy as jnp
        import numpy as np
        N_NODES = 50000
        N_EDGES = 9375
        DIM_H = 128
        LN_EPS = 1e-05

        def _layer_norm(x, gamma, beta):
            mu = jnp.mean(x, axis=-1, keepdims=True)
            var = jnp.mean(jnp.square(x - mu), axis=-1, keepdims=True)
            return gamma * (x - mu) * jax.lax.rsqrt(var + LN_EPS) + beta
        n_nodes = nodes.shape[0]
        msg_e = nodes[edge_src] @ W_msg.T + b_msg
        messages = jax.ops.segment_sum(msg_e, edge_dst, num_segments=n_nodes)
        msg = messages + jnp.mean(nodes, axis=0)
        gi = msg @ w_ih.T + b_ih
        gh = nodes @ w_hh.T + b_hh
        i_r, i_z, i_n = jnp.split(gi, 3, axis=-1)
        h_r, h_z, h_n = jnp.split(gh, 3, axis=-1)
        r = jax.nn.sigmoid(i_r + h_r)
        z = jax.nn.sigmoid(i_z + h_z)
        n = jnp.tanh(i_n + r * h_n)
        h_next = (1.0 - z) * n + z * nodes
        out = _layer_norm(h_next, ln_gamma, ln_beta)
        out = out + messages
        return out

    def _L2_gnn_ref(x, edge_index, w_self, b_self, w_neigh, b_neigh):
        import jax, jax.numpy as jnp
        import numpy as np
        N = 50000
        E = 12500
        IN_DIM = 128
        OUT_DIM = 128
        src = edge_index[0]
        dst = edge_index[1]
        n = x.shape[0]
        agg = jax.ops.segment_sum(x[src], dst, num_segments=n)
        deg = jax.ops.segment_sum(jnp.ones((src.shape[0],), dtype=x.dtype), dst, num_segments=n)
        deg = jnp.maximum(deg, 1.0)[:, None]
        mean_neigh = agg / deg
        return x @ w_self.T + b_self + mean_neigh @ w_neigh.T + b_neigh

    def _L3_gnn_ref(x, edge_index, W1, b1, W2, b2, W3, b3):
        import jax, jax.numpy as jnp
        import numpy as np
        N = 10000
        E = 10000
        D = 128
        EPS = 1e-08

        def _gcn_conv(x, src, dst, deg_isqrt, W, b, n):
            h = x @ W
            norm = deg_isqrt[src] * deg_isqrt[dst]
            msgs = h[src] * norm[:, None]
            out = jax.ops.segment_sum(msgs, dst, num_segments=n)
            return out + b

        def _pairnorm_pn(x):
            norm = jnp.sqrt(jnp.sum(x * x, axis=1, keepdims=True)) + EPS
            return x / norm
        n = x.shape[0]
        loops = jnp.arange(n, dtype=edge_index.dtype)
        src = jnp.concatenate([edge_index[0], loops])
        dst = jnp.concatenate([edge_index[1], loops])
        deg = jax.ops.segment_sum(jnp.ones_like(dst, dtype=x.dtype), dst, num_segments=n)
        deg_isqrt = jnp.where(deg > 0, jax.lax.rsqrt(jnp.maximum(deg, 1.0)), 0.0)
        prev = x
        for W, b in ((W1, b1), (W2, b2)):
            x = _gcn_conv(x, src, dst, deg_isqrt, W, b, n)
            x = _pairnorm_pn(x)
            x = x + prev
            prev = x
            x = jax.nn.gelu(x, approximate=False)
        return _gcn_conv(x, src, dst, deg_isqrt, W3, b3, n)
    edge_index = jnp.stack([src, dst])
    x = _layernorm(x + _L0_gnn_ref(x, edge_index, L0_gnn_Wl, L0_gnn_bl, L0_gnn_Wr, L0_gnn_br), axis=-1)
    x = _layernorm(x + _L1_gnn_ref(x, L1_gnn_W_msg, L1_gnn_b_msg, L1_gnn_w_ih, L1_gnn_w_hh, L1_gnn_b_ih, L1_gnn_b_hh, L1_gnn_ln_gamma, L1_gnn_ln_beta, src, dst), axis=-1)
    x = _layernorm(x + _L2_gnn_ref(x, edge_index, L2_gnn_w_self, L2_gnn_b_self, L2_gnn_w_neigh, L2_gnn_b_neigh), axis=-1)
    x = _layernorm(x + _L3_gnn_ref(x, edge_index, L3_gnn_W1, L3_gnn_b1, L3_gnn_W2, L3_gnn_b2, L3_gnn_W3, L3_gnn_b3), axis=-1)
    return x

_drawn_inputs = setup_inputs


def setup_inputs(seed=0):
    import zlib

    import numpy as np

    out = dict(_drawn_inputs(seed))
    spreads = {'L1_gnn_b_msg': (0.0, 0.1),
     'L1_gnn_b_ih': (0.0, 0.27),
     'L1_gnn_b_hh': (0.0, 0.402),
     'L1_gnn_ln_gamma': (1.0, 0.2),
     'L1_gnn_ln_beta': (0.0, 0.1),
     'L3_gnn_b1': (0.0, 2.0),
     'L3_gnn_b2': (0.0, 0.8),
     'L3_gnn_b3': (0.0, 0.1)}
    factors = {'L0_gnn_bl': 64.0, 'L0_gnn_br': 64.0}
    for name, (base, spread) in spreads.items():
        noise = np.random.default_rng([zlib.crc32(name.encode()), seed]).standard_normal(out[name].shape)
        drawn = base * np.exp(spread * noise) if base else spread * noise
        out[name] = jnp.asarray(drawn.astype(out[name].dtype))
    for name, factor in factors.items():
        out[name] = (out[name] * factor).astype(out[name].dtype)
    return out
```

```python
from contextlib import ExitStack

import concourse.bass as bass
from concourse import mybir

ALU = mybir.AluOpType
ACT = mybir.ActivationFunctionType
AX = mybir.AxisListType
F32 = mybir.dt.float32
F16 = mybir.dt.float16
BF16 = mybir.dt.bfloat16
I32 = mybir.dt.int32

P = 128
D = 128
N = 50000
E = 62500
A = 4
BLK = P * A
NB = -(-N // BLK)
LAST = N - BLK
SHIFT = ((NB - 1) * BLK - LAST) // A
COLS = NB * A
R = 6
S = 3

EP = 125
EJ = E // EP
C = 4
G2 = 2 * C
MAXT = -(-EJ // G2)
KC = MAXT * G2
TRASH = N
ZROWS = 6
ROWS = 396 * P
BIG = float(1 << 24)
FILL = -2.0 * BIG
HOT = 5
HJ = 10

L0, L1, L2, CV1, CV2, CV3 = range(6)
PHASES = 6

LN_EPS = 1e-5
NORM_EPS = {L0: 1e-6, CV1: 1e-8, CV2: 1e-8}

STAGES = {
    "own_added": (L0,),
    "prescaled": (L0, L2, CV1, CV2, CV3),
    "own_scaled": (CV3,),
    "own_ready": (L1, L2, CV1, CV3),
    "turned": tuple(range(6)),
    "turned_out": tuple(range(6)),
    "product": tuple(range(6)),
    "biased": (L0, CV1, CV2),
    "relued": (L0,),
    "squared": (L0, CV1, CV2),
    "norm": (L0, CV1, CV2),
    "norm_eps": (L0, CV1, CV2),
    "norm_inv": (L0, CV1, CV2),
    "residual": tuple(range(6)),
    "stats": (L0, L1, L2, CV3),
    "aggr": (L0, L1, L2, CV3),
    "var_eps": (L0, L1, L2, CV3),
    "rstd": (L0, L1, L2, CV3),
    "rstd_dis": (L2,),
    "shifted": (L0, L1, L2, CV3),
    "gelued": (CV1, CV2),
    "result": tuple(range(6)),
    "seeded": (L0, L1, L2, CV1, CV2),
    "summed": (L0,),
    "message": (L1,),
    "own_message": (L1,),
    "msg_turned": (L1,),
    "msg_out": (L1,),
    "gates_rh": (L1,),
    "gates_zn": (L1,),
    "reset": (L1,),
    "update": (L1,),
    "reset_hidden": (L1,),
    "candidate_in": (L1,),
    "candidate": (L1,),
    "old_less_new": (L1,),
    "kept": (L1,),
    "state": (L1,),
    "state_turned": (L1,),
    "state_out": (L1,),
    "stats1": (L1,), "aggr1": (L1,), "var_eps1": (L1,),
    "rstd1": (L1,),
    "shifted1": (L1,), "normed1": (L1,), "scaled1": (L1,),
}


def base(stage, ph):
    return NB * sum(q < ph for q in STAGES[stage])


STORES = {L0: 2, L1: 2, L2: 2, CV1: 3, CV2: 2, CV3: 1}
NORMED = (L0, L1, L2, CV3)
FINAL = {ph: 8 if ph == L1 else 5 for ph in range(PHASES)}


def stores_before(ph, slot):
    return 16 * sum(STORES[q] for q in range(ph)) * len(range(slot, NB, R))


def build(nc, x, src, dst, Wl, bl, Wr, br, W_msg, b_msg, w_ih, w_hh, b_ih, b_hh, gamma, beta,
          w_self, b_self, w_neigh, b_neigh, W1, b1, W2, b2, W3, b3, out):
    with ExitStack() as ctx:
        def sb(name, shape, dt=F32):
            return ctx.enter_context(nc.sbuf_tensor(name, shape, dt))

        def sem(name):
            return ctx.enter_context(nc.semaphore(name))

        def table(name, rows):
            return nc.dram_tensor(name, [rows, D], F32, kind="Internal").ap()

        x1, x2, y3, h1, y4, y5 = (table(n, N) for n in ("x1", "x2", "y3", "h1", "y4", "y5"))
        sums = [table("sum_even", ROWS), table("sum_odd", ROWS)]
        OWN = [x, x1, x2, y3, h1, y3]
        SOURCE = [x, x1, x2, y3, y4, y5]
        RESULT = [x1, x2, y3, y4, y5, out]

        ident = sb("ident", [P, P])
        zeros = sb("zeros", [P, ZROWS * D])
        ones = sb("ones", [P, P])
        inv_n = sb("inv_n", [P, 2])
        powers = sb("powers", [P, 2, A])
        earlier = sb("earlier", [P, C, C * P])
        lane_f = sb("lane_f", [P, P], F16)
        col_f = sb("col_f", [P, COLS], F16)
        trash_f = sb("trash_f", [P, C])

        weights_T = sb("weights_T", [P, 9, D])
        straight = sb("straight", [P, 5, D])
        rows_bc = sb("rows_bc", [P, 10, D])
        bl_, br_, bmsg_, gamma_, beta_, bself_, bneigh_, bc1_, bc2_, bc3_ = range(10)
        gate_b = sb("gate_b", [P, 2, 3])
        gate_c = sb("gate_c", [P, 3])
        mean_col = sb("mean_col", [P, 1])
        BIAS = {L0: bl_, L2: bself_, CV1: bc1_, CV2: bc2_, CV3: bc3_}

        own_n = sb("own_n", [P, COLS])
        own_n1 = sb("own_n1", [P, COLS])
        deg_s = sb("deg_s", [P, COLS])
        deg_d = sb("deg_d", [P, COLS])
        inv_s = sb("inv_s", [P, COLS])
        inv_d = sb("inv_d", [P, COLS])
        dis = sb("dis", [P, COLS])
        dis_inv = sb("dis_inv", [P, COLS])
        deg_gcn = sb("deg_gcn", [P, COLS])
        SCALE = {L0: inv_s, L2: inv_d, CV1: dis, CV2: dis, CV3: dis}
        SEED = {L0: own_n, L1: own_n, L2: own_n1, CV1: own_n1, CV2: own_n1}

        key_f = sb("key_f", [P, 2, KC])
        gidx = sb("gidx", [P, 2, KC], I32)
        trips = sb("trips", [1, 4], I32)
        trips_f = sb("trips_f", [1, 4])

        ROOMS = 3 * R + 13 * S
        arena = sb("arena", [P, ROOMS, BLK])
        at = [0]

        def ring(n):
            at[0] += n
            return arena[:, at[0] - n:at[0], :]

        own, own_T, extra = ring(R), ring(R), ring(R)
        sm, scaled, gT = ring(S), ring(S), ring(S)
        u, r, res = ring(S), ring(S), ring(S)
        result, seed, update = ring(S), ring(S), ring(S)
        new, kept, state, cand = ring(S), ring(S), ring(S), ring(S)
        at[0] = 0

        def prep(k):
            at[0] += 1
            assert at[0] <= ROOMS
            return arena[:, at[0] - 1, 0:k]

        raw = arena[:, ROOMS - 3:ROOMS, :].rearrange("p a k -> p (a k)")[:, 0:9 * D].rearrange("p (i d) -> p i d", d=D)
        src_i, dst_i = prep(EJ).bitcast(I32), prep(EJ).bitcast(I32)
        src_f, dst_f, differ, place_f = prep(EJ), prep(EJ), prep(EJ), prep(EJ)
        pack = [prep(EJ), prep(EJ)]
        packed = [prep(KC), prep(KC)]
        packed_i = [prep(KC).bitcast(I32), prep(KC).bitcast(I32)]
        empty, trash_kf, trash_k, place_i = prep(KC), prep(KC), prep(KC).bitcast(I32), prep(EJ).bitcast(I32)
        own_lane, own_col = prep(EJ), prep(EJ)
        own_i = [prep(EJ).bitcast(I32), prep(EJ).bitcast(I32), prep(EJ).bitcast(I32)]
        key_lane = [prep(KC), prep(KC)]
        key_col = [prep(KC), prep(KC)]
        key_i = [prep(KC).bitcast(I32) for _ in range(3)]
        hist = [prep(COLS), prep(COLS), prep(COLS)]
        top8 = sb("top8", [P, 2, 8])
        row_n = sb("row_n", [P, 1])
        hot_lane = sb("hot_lane", [P, HOT, P], F16)
        hot_col = sb("hot_col", [P, HOT, COLS], F16)

        idx_now = sb("idx_now", [P, 2, C], I32)
        key_now = sb("key_now", [P, 2, C])
        to_now = sb("to_now", [P, 2, C], I32)
        rows_in = sb("rows_in", [P, 2, C, D])
        rows_sum = sb("rows_sum", [P, 2, C, D])
        equal = sb("equal", [P, 2, C, C * P])
        junk = sb("junk", [P, C, C * P], BF16)
        pass_mark = sb("pass_mark", [P, 1])
        pass_mark_dve = sb("pass_mark_dve", [P, 1])
        n_earlier = sb("n_earlier", [P, 2, C])
        pick = sb("pick", [P, 2, 3, C])

        ss = sb("ss", [P, R, A])
        nrm = sb("nrm", [P, R, A])
        nrm_e = sb("nrm_e", [P, R, A])
        nrm_inv = sb("nrm_inv", [P, R, A])
        bn6 = sb("bn6", [P, R, A, 6])
        mv = sb("mv", [P, R, A, 2])
        ve = sb("ve", [P, R, A])
        rs = sb("rs", [P, R, A])
        rsd = sb("rsd", [P, R, A])
        nb = sb("nb", [P, R, A])
        bn6_1 = sb("bn6_1", [P, R, A, 6])
        mv_1 = sb("mv_1", [P, R, A, 2])
        ve_1 = sb("ve_1", [P, R, A])
        rs_1 = sb("rs_1", [P, R, A])
        nb_1 = sb("nb_1", [P, R, A])
        junk_sq = sb("junk_sq", [P, S, A, D], BF16)

        bank = [ctx.enter_context(nc.psum_tensor(f"bank{i}", [P, BLK], F32)) for i in range(8)]

        stage = {n: sem(n) for n in STAGES}
        loaded = [sem(f"loaded{i}") for i in range(R)]
        stored = [sem(f"stored{i}") for i in range(R)]
        (s_edges, s_weights, s_zero_tile, s_zeroed, s_shift, s_const, s_dve, s_pool, s_row_n, s_row_turned, s_trips,
         s_weights_turned, s_weights_out, s_top, s_own_hot, s_own_hist, s_key_hot, s_key_hist, s_hist_out, s_nodes,
         s_roots, s_biases, s_mean, s_gate_mm, s_gate_c, s_pass_done, s_alone) = (sem(n) for n in (
             "edges_loaded", "weights_loaded", "zero_tile", "sums_zeroed", "last_block_shifted", "constants",
             "dve_step", "pool_step", "rows_counted", "row_counts_turned", "trips_known", "weights_turned",
             "weights_out", "top8_step", "own_hot", "own_hist", "key_hot", "key_hist", "hist_out", "degrees",
             "roots", "biases", "mean_column", "gate_product", "gate_constants", "pass_done", "wait_alone"))
        staged, keys_turned, matched, counted, picked, to_ready, summed_eq, rows_out, added = (
            [sem(f"{n}{ph}") for ph in range(PHASES)] for n in
            ("staged", "keys_turned", "matched", "counted", "picked", "to_ready",
             "summed_eq", "rows_out", "added"))

        class Blk:

            def __init__(self, b, slot, turn):
                self.b, self.slot, self.turn = b, slot % R, turn
                self.s3 = self.slot % S
                self.two = self.slot % 2

            def back(self, n):
                return Blk(self.b - n, self.slot - n, self.turn + (self.slot - n) // R)

            def exists(self):
                return not isinstance(self.b, int) or 0 <= self.b < NB

            def last(self):
                return isinstance(self.b, int) and self.b == NB - 1

        landed = [[sem(f"landed{ph}_{g}") for g in range(2)] for ph in range(PHASES)]

        def after(eng, name, ph, k):
            if k.exists():
                eng.wait_ge(stage[name], k.b + (base(name, ph) + 1))

        def after_stores(eng, ph, k):
            if k.exists():
                eng.wait_ge(stored[k.slot], (k.turn + 1) * (16 * STORES[ph]) + stores_before(ph, k.slot))

        def after_loads(eng, ph, k):
            eng.wait_ge(loaded[k.slot], (k.turn + 1) * 32 + 32 * ph * len(range(k.slot, NB, R)))

        def alone(eng):
            eng.sem_inc(s_alone, 1)

        def rows_of(t, k):
            first = LAST if k.last() else k.b * BLK
            return t[bass.ds(first, BLK), :].rearrange("(p a) d -> p (a d)", a=A)

        def col(t, k, a):
            return t[:, bass.ds(k.b * A + a, 1)]

        def cols(t, k):
            return t[:, bass.ds(k.b * A, A)].unsqueeze(2).to_broadcast([P, A, D])

        def each(i):
            return rows_bc[:, i, :].unsqueeze(1).to_broadcast([P, A, D])

        def sub(t, a):
            return t[:, a * D:(a + 1) * D]

        def v3(t):
            return t.rearrange("p (a d) -> p a d", a=A)

        def steps(eng, body, depth):
            first = -(-(depth + S) // R)
            whole = (NB - 2) // R
            for n in range(first * R):
                body(Blk(n, n, n // R))
            with eng.Fori(first, whole) as q:
                for slot in range(R):
                    body(Blk(q * R + slot, slot, q))
            for n in range(whole * R, NB + depth):
                body(Blk(n, n, n // R))

        block = ctx.enter_context(nc.Block())

        @block.sync
        def _(sp):
            sp.dma_start(src_i[0:EP, :], src.rearrange("(p j) -> p j", j=EJ)).then_inc(s_edges, 16)
            sp.dma_start(dst_i[0:EP, :], dst.rearrange("(p j) -> p j", j=EJ)).then_inc(s_edges, 16)
            sp.dma_start(raw[:, 0, :], W_msg).then_inc(s_weights, 16)
            sp.dma_start(raw[:, 1:4, :], w_ih.rearrange("(g p) d -> p g d", p=P)).then_inc(s_weights, 16)
            sp.dma_start(raw[:, 4:7, :], w_hh.rearrange("(g p) d -> p g d", p=P)).then_inc(s_weights, 16)
            sp.dma_start(raw[:, 7, :], w_self).then_inc(s_weights, 16)
            sp.dma_start(raw[:, 8, :], w_neigh).then_inc(s_weights, 16)
            for i, w in enumerate((Wl, Wr, W1, W2, W3)):
                sp.dma_start(straight[:, i, :], w).then_inc(s_weights, 16)
            for i, v in enumerate((bl, br, b_msg, gamma, beta, b_self, b_neigh, b1, b2, b3)):
                sp.dma_start(rows_bc[:, i, :], v.rearrange("(o d) -> o d", o=1).to_broadcast([P, D])).then_inc(s_weights, 16)
            with nc.allow_non_contiguous_dma(reason="three numbers a partition, once"):
                sp.dma_start(gate_b[:, 0, :], b_ih.rearrange("(g p) -> p g", p=P)).then_inc(s_weights, 16)
                sp.dma_start(gate_b[:, 1, :], b_hh.rearrange("(g p) -> p g", p=P)).then_inc(s_weights, 16)
            sp.wait_ge(s_zero_tile, 1)
            sp.dma_start(sums[0].rearrange("(p c r) d -> p c (r d)", p=P, r=ZROWS),
                         zeros[:, :].unsqueeze(1).to_broadcast([P, ROWS // P // ZROWS, ZROWS * D])).then_inc(s_zeroed, 16)
            sp.dma_start(sums[1][TRASH:TRASH + BLK, :].rearrange("(p a) d -> p (a d)", a=A),
                         zeros[:, 0:A * D]).then_inc(s_zeroed, 16)
            sp.wait_ge(s_hist_out, 1)
            for t, h in ((own_n, hist[0]), (deg_s, hist[1]), (deg_d, hist[2])):
                sp.dma_start(t[0:SHIFT, COLS - A:COLS], h[P - SHIFT:P, COLS - 2 * A:COLS - A]).then_inc(s_shift, 16)
                sp.dma_start(t[SHIFT:P, COLS - A:COLS], h[0:P - SHIFT, COLS - A:COLS]).then_inc(s_shift, 16)

            def load(ph, k):
                for name in {L0: ("residual",), L1: ("turned", "own_message"), L2: ("turned", "own_ready"),
                             CV1: ("own_ready",), CV2: ("residual",), CV3: ("own_ready",)}[ph]:
                    after(sp, name, ph, k.back(R))
                    alone(sp)
                sp.dma_start(own[:, k.slot, :], rows_of(OWN[ph], k)).then_inc(loaded[k.slot], 16)
                after(sp, "turned" if ph == L1 else "prescaled", ph, k.back(S))
                alone(sp)
                sp.dma_start(sm[:, k.s3, :], rows_of(sums[ph % 2], k)).then_inc(loaded[k.slot], 16)

            def store(ph, k):
                if k.last():
                    after_stores(sp, ph, k.back(1))
                after(sp, "result", ph, k)
                alone(sp)
                sp.dma_start(rows_of(RESULT[ph], k), result[:, k.s3, :]).then_inc(stored[k.slot], 16)
                if ph == CV1:
                    sp.dma_start(rows_of(h1, k), res[:, k.s3, :]).then_inc(stored[k.slot], 16)
                if ph in SEED:
                    after(sp, "seeded", ph, k)
                    alone(sp)
                    sp.dma_start(rows_of(sums[(ph + 1) % 2], k), seed[:, k.s3, :]).then_inc(stored[k.slot], 16)

            def dense(ph):
                sp.wait_ge(s_pass_done, ph + 1)
                load(ph, Blk(0, 0, 0))

                def step(k):
                    if not isinstance(k.b, int) or k.b + 1 < NB:
                        load(ph, k.back(-1))
                    if k.back(FINAL[ph]).exists():
                        store(ph, k.back(FINAL[ph]))

                steps(sp, step, FINAL[ph] + 1)

            for ph in range(PHASES):
                dense(ph)
            for slot in range(R):
                sp.wait_ge(stored[slot], stores_before(PHASES, slot))

        @block.gpsimd
        def _(pool):
            pool.memset(zeros[:, :], 0.0).then_inc(s_zero_tile, 1)
            pool.memset(ones[:, :], 1.0)
            pool.memset(ident[:, :], 0.0)
            pool.memset(earlier[:, :, :], 0.0)
            pool.memset(inv_n[:, :], 1.0 / N)
            pool.memset(powers[:, 0, :], -0.5)
            pool.memset(powers[:, 1, :], 0.5)
            pool.iota(lane_f[:, :], [[1, P]], base=0, channel_multiplier=0, allow_small_or_imprecise_dtypes=True)
            pool.iota(col_f[:, :], [[1, COLS]], base=0, channel_multiplier=0, allow_small_or_imprecise_dtypes=True)
            pool.iota(place_i[:, :], [[1, EJ]], base=0, channel_multiplier=0)
            pool.iota(trash_k[:, :], [[0, KC // C], [P, C]], base=TRASH, channel_multiplier=1).then_inc(s_pool, 1)
            pool.wait_ge(s_pool, 1)
            pool.affine_select(out=ident[:, :], in_=ident[:, :], compare_op=ALU.not_equal, fill=1.0, base=0,
                               pattern=[[-1, P]], channel_multiplier=1)
            pool.affine_select(out=inv_n[:, 1:2], in_=inv_n[:, 1:2], compare_op=ALU.is_ge, fill=0.0, base=-SHIFT,
                               pattern=[[0, 1]], channel_multiplier=1)
            for c in range(C):
                if c:
                    pool.memset(earlier[:, c, 0:c * P], 1.0)
                pool.affine_select(out=earlier[:, c, c * P:(c + 1) * P], in_=ones[:, :], compare_op=ALU.is_ge, fill=0.0,
                                   base=-1, pattern=[[-1, P]], channel_multiplier=1)
            pool.tensor_copy(trash_f[:, :], trash_k[:, 0:C]).then_inc(s_const, 1)
            pool.wait_ge(s_nodes, 1)
            pool.tensor_tensor(dis[:, :], deg_gcn[:, :], powers[:, 0, 0:1].to_broadcast([P, COLS]), ALU.pow)
            pool.tensor_tensor(dis_inv[:, :], deg_gcn[:, :], powers[:, 1, 0:1].to_broadcast([P, COLS]), ALU.pow).then_inc(s_roots, 1)
            pool.wait_ge(s_trips, 1)
            turns = pool.value_load(trips[0:1, 0:1], min_val=2, max_val=MAXT)
            last_turn = pool.value_load(trips[0:1, 1:2], min_val=1, max_val=MAXT - 1)

            def gather(ph, q, g):
                pool.wait_ge(staged[ph], q * 2 + (g + 1))
                alone(pool)
                if not (isinstance(q, int) and q == 0):
                    pool.wait_ge(summed_eq[ph], q * 2 + (g - 1))
                    alone(pool)
                for c in range(C):
                    pool.indirect_dma_start(rows_in[:, g, c, :], None, SOURCE[ph],
                                            bass.IndirectOffsetOnAxis(ap=idx_now[:, g, c:c + 1], axis=0)
                                            ).then_inc(landed[ph][g], 16)

            def add(ph, q, g, first=False):
                room = g % 2
                pool.wait_ge(rows_out[ph], q * 2 + (g + 1))
                alone(pool)
                pool.wait_ge(to_ready[ph], q * 2 + (g + 1))
                alone(pool)
                if not first:
                    pool.wait_ge(added[ph], q * (32 * C) + 16 * C * g)
                    alone(pool)
                for c in range(C):
                    pool.indirect_dma_start(sums[ph % 2], bass.IndirectOffsetOnAxis(ap=to_now[:, room, c:c + 1], axis=0),
                                            rows_sum[:, room, c, :], None, compute_op=ALU.add).then_inc(added[ph], 16)

            def aggregate(ph):
                if ph == L0:
                    pool.wait_ge(s_zeroed, 32)
                else:
                    for slot in range(R):
                        pool.wait_ge(stored[slot], stores_before(ph, slot))
                gather(ph, 0, 0)
                gather(ph, 0, 1)
                add(ph, 0, 0, first=True)
                with pool.Fori(1, turns) as q:
                    gather(ph, q, 0)
                    add(ph, q, -1)
                    gather(ph, q, 1)
                    add(ph, q, 0)
                add(ph, last_turn, 1)
                pool.wait_ge(added[ph], turns * (32 * C))
                alone(pool)
                pool.memset(pass_mark[:, :], 0.0).then_inc(s_pass_done, 1)

            def power(ph, k, out_, in_, i, needs, gives):
                after(pool, needs, ph, k)
                pool.tensor_tensor(out_[:, k.slot, :], in_[:, k.slot, :], powers[:, i, :], ALU.pow).then_inc(stage[gives], 1)

            def operands(ph, k):
                after_loads(pool, ph, k)
                if ph == L0:
                    after(pool, "own_added", ph, k)
                after(pool, "turned", ph, k.back(S))
                pool.tensor_tensor(v3(scaled[:, k.s3, :]), v3(sm[:, k.s3, :]), cols(SCALE[ph], k),
                                   ALU.mult).then_inc(stage["prescaled"], 1)
                if ph == L2:
                    after(pool, "residual", ph, k.back(R))
                    pool.tensor_tensor(v3(extra[:, k.slot, :]), v3(own[:, k.slot, :]), each(BIAS[L2]),
                                       ALU.add).then_inc(stage["own_ready"], 1)
                if ph in (CV1, CV3):
                    after(pool, "residual", ph, k.back(R))
                    last = pool.tensor_tensor(v3(extra[:, k.slot, :]), v3(own[:, k.slot, :]), cols(dis_inv, k), ALU.mult)
                    if ph == CV1:
                        last.then_inc(stage["own_ready"], 1)
                    else:
                        last.then_inc(stage["own_scaled"], 1)
                        after(pool, "own_scaled", ph, k)
                        pool.tensor_tensor(v3(extra[:, k.slot, :]), v3(extra[:, k.slot, :]), each(BIAS[CV3]),
                                           ALU.add).then_inc(stage["own_ready"], 1)

            def seeds(ph, k):
                after(pool, "result", ph, k)
                after_stores(pool, ph, k.back(S))
                pool.tensor_tensor(v3(seed[:, k.s3, :]), v3(result[:, k.s3, :]), cols(SEED[ph], k),
                                   ALU.mult).then_inc(stage["seeded"], 1)

            def dense(ph):
                def step(k):
                    if k.exists():
                        operands(ph, k)
                    if ph in SEED and k.back(5).exists():
                        seeds(ph, k.back(5))
                    if ph in NORM_EPS and k.back(3).exists():
                        power(ph, k.back(3), nrm, ss, 1, "squared", "norm")
                    if ph in NORMED and k.back(4).exists():
                        power(ph, k.back(4), rs, ve, 0, "var_eps", "rstd")

                steps(pool, step, FINAL[ph] + 1)

            def dense_gru(k):
                if k.back(8).exists():
                    seeds(L1, k.back(8))
                j = k.back(2)
                if j.exists():
                    after_loads(pool, L1, j)
                    after(pool, "message", L1, j)
                    after(pool, "residual", L1, j.back(R))
                    pool.tensor_tensor(extra[:, j.slot, :], own[:, j.slot, :], scaled[:, j.s3, :],
                                       ALU.add).then_inc(stage["own_message"], 1)
                    after(pool, "own_message", L1, j)
                    pool.tensor_tensor(v3(extra[:, j.slot, :]), v3(extra[:, j.slot, :]), each(beta_),
                                       ALU.add).then_inc(stage["own_ready"], 1)
                j = k.back(4)
                if j.exists():
                    after(pool, "candidate", L1, j)
                    after(pool, "update", L1, j)
                    after(pool, "turned_out", L1, j)
                    after(pool, "state_turned", L1, j.back(S))
                    pool.tensor_tensor(kept[:, j.s3, :], own_T[:, j.slot, :], new[:, j.s3, :],
                                       ALU.subtract).then_inc(stage["old_less_new"], 1)
                    after(pool, "old_less_new", L1, j)
                    pool.tensor_tensor(kept[:, j.s3, :], kept[:, j.s3, :], update[:, j.s3, :],
                                       ALU.mult).then_inc(stage["kept"], 1)
                if k.back(6).exists():
                    power(L1, k.back(6), rs_1, ve_1, 0, "var_eps1", "rstd1")
                if k.back(7).exists():
                    power(L1, k.back(7), rs, ve, 0, "var_eps", "rstd")

            for ph in range(PHASES):
                aggregate(ph)
                if ph == L1:
                    steps(pool, dense_gru, FINAL[ph] + 1)
                else:
                    dense(ph)

        @block.tensor
        def _(pe):
            pe.wait_ge(s_const, 1)
            pe.wait_ge(s_row_n, 1)
            nc.tensor.transpose(bank[3][0:1, 0:P], row_n[:, :], ident[:, :]).then_inc(s_row_turned, 1)
            pe.wait_ge(s_weights, 16 * 22)
            for i in range(9):
                last = nc.tensor.transpose(bank[4 + i // 4][:, i % 4 * D:(i % 4 + 1) * D], raw[:, i, :], ident[:, :])
            last.then_inc(s_weights_turned, 1)

            def own_hist(j, slot, first=False):
                pe.wait_ge(s_own_hot, j + 1)
                nc.tensor.matmul(bank[0][:, 0:COLS], hot_lane[:, slot, :], hot_col[:, slot, :], start=first, stop=True,
                                 skip_group_check=True).then_inc(s_own_hist, 1)

            for j in range(HJ):
                own_hist(j, j % HOT, first=j == 0)
            with pe.Fori(1, EJ // HJ) as q:
                for j in range(HJ):
                    own_hist(q * HJ + j, j % HOT)

            def key_hist(c, slot, first=False):
                pe.wait_ge(s_key_hot, c + 1)
                for d in range(2):
                    last = nc.tensor.matmul(bank[1 + d][:, 0:COLS], hot_lane[:, 2 * slot + d, :], hot_col[:, 2 * slot + d, :],
                                            start=first, stop=True, skip_group_check=True)
                last.then_inc(s_key_hist, 1)

            pe.wait_ge(s_trips, 1)
            turns = pe.value_load(trips[0:1, 0:1], min_val=2, max_val=MAXT)
            for c in range(G2):
                key_hist(c, c % 2, first=c == 0)
            with pe.Fori(1, turns) as q:
                for c in range(G2):
                    key_hist(q * G2 + c, c % 2)

            def group(ph, q, g, first=False):
                pe.wait_ge(staged[ph], q * 2 + (g + 1))
                if not (first and g == 0):
                    pe.wait_ge(matched[ph], q * 2 + g)
                for c in range(C):
                    last = nc.tensor.transpose(sub(bank[0], c), key_now[:, g, c:c + 1].to_broadcast([P, P]), ident[:, :])
                last.then_inc(keys_turned[ph], 1)
                pe.wait_ge(matched[ph], q * 2 + (g + 1))
                pe.wait_ge(landed[ph][g], q * (16 * C) + 16 * C)
                if not first:
                    pe.wait_ge(rows_out[ph], q * 2 + (g - 1))
                for c in range(C):
                    for e in range(C):
                        last = nc.tensor.matmul(sub(bank[1 + g], c), equal[:, g, e, c * P:(c + 1) * P], rows_in[:, g, e, :],
                                                start=e == 0, stop=e == C - 1)
                last.then_inc(summed_eq[ph], 1)

            def aggregate(ph):
                group(ph, 0, 0, first=True)
                group(ph, 0, 1, first=True)
                with pe.Fori(1, turns) as q:
                    group(ph, q, 0)
                    group(ph, q, 1)

            def turn(ph, k):
                after_loads(pe, ph, k)
                after(pe, "prescaled", ph, k)
                after(pe, "turned_out", ph, k.back(2))
                for a in range(A):
                    if ph in (L0, L2):
                        nc.tensor.transpose(sub(bank[k.two], a), sub(own[:, k.slot, :], a), ident[:, :])
                    last = nc.tensor.transpose(sub(bank[2 + k.two], a), sub(scaled[:, k.s3, :], a), ident[:, :])
                last.then_inc(stage["turned"], 1)

            def multiply(ph, k):
                after(pe, "turned_out", ph, k)
                after(pe, "biased" if ph in NORM_EPS else "residual", ph, k.back(2))
                w_sum = {L0: straight[:, 1, :], L2: weights_T[:, 8, :], CV1: straight[:, 2, :], CV2: straight[:, 3, :],
                         CV3: straight[:, 4, :]}[ph]
                w_own = {L0: straight[:, 0, :], L2: weights_T[:, 7, :]}.get(ph)
                for a in range(A):
                    if w_own is not None:
                        nc.tensor.matmul(sub(bank[4 + k.two], a), sub(own_T[:, k.slot, :], a), w_own, start=True, stop=False)
                    last = nc.tensor.matmul(sub(bank[4 + k.two], a), sub(gT[:, k.s3, :], a), w_sum,
                                            start=w_own is None, stop=True)
                last.then_inc(stage["product"], 1)

            def column_sums(k):
                after(pe, "result", L0, k)
                w = inv_n[:, 1:2] if k.last() else inv_n[:, 0:1]
                for a in range(A):
                    last = nc.tensor.matmul(bank[6][:, 0:1], sub(result[:, k.s3, :], a), w,
                                            start=isinstance(k.b, int) and k.b == 0 and a == 0, stop=True,
                                            skip_group_check=True)
                last.then_inc(stage["summed"], 1)

            def dense(ph):
                def step(k):
                    if k.back(1).exists():
                        turn(ph, k.back(1))
                    if k.back(2).exists():
                        multiply(ph, k.back(2))
                    if ph == L0 and k.back(6).exists():
                        column_sums(k.back(6))

                steps(pe, step, FINAL[ph] + 2)

            def dense_gru(k):
                if k.exists():
                    after_loads(pe, L1, k)
                    after(pe, "turned_out", L1, k.back(1))
                    for a in range(A):
                        nc.tensor.transpose(sub(bank[0], a), sub(own[:, k.slot, :], a), ident[:, :])
                        last = nc.tensor.transpose(sub(bank[1], a), sub(sm[:, k.s3, :], a), ident[:, :])
                    last.then_inc(stage["turned"], 1)
                j = k.back(5)
                if j.exists():
                    after(pe, "state", L1, j)
                    ahead = j.back(-2)
                    after(pe, "msg_out", L1, ahead if ahead.exists() else Blk(NB - 1, NB - 1, (NB - 1) // R))
                    for a in range(A):
                        last = nc.tensor.transpose(sub(bank[3], a), sub(kept[:, j.s3, :], a), ident[:, :])
                    last.then_inc(stage["state_turned"], 1)
                j = k.back(1)
                if j.exists():
                    after(pe, "turned_out", L1, j)
                    after(pe, "message", L1, j.back(1))
                    for a in range(A):
                        last = nc.tensor.matmul(sub(bank[2], a), sub(gT[:, j.s3, :], a), weights_T[:, 0, :],
                                                start=True, stop=True)
                    last.then_inc(stage["product"], 1)
                j = k.back(3)
                if j.exists():
                    after(pe, "msg_out", L1, j)
                    x_T, m_T = own_T[:, j.slot, :], u[:, j.s3, :]
                    after(pe, "reset", L1, j.back(1))
                    nc.tensor.matmul(bank[4][:, :], weights_T[:, 1, :], m_T, start=True, stop=False)
                    nc.tensor.matmul(bank[4][:, :], weights_T[:, 4, :], x_T, start=False, stop=True)
                    after(pe, "reset_hidden", L1, j.back(1))
                    nc.tensor.matmul(bank[5][:, :], weights_T[:, 6, :], x_T, start=True, stop=True
                                     ).then_inc(stage["gates_rh"], 1)
                    after(pe, "candidate_in", L1, j.back(1))
                    nc.tensor.matmul(bank[7][:, :], weights_T[:, 3, :], m_T, start=True, stop=True)
                    after(pe, "update", L1, j.back(1))
                    nc.tensor.matmul(bank[6][:, :], weights_T[:, 2, :], m_T, start=True, stop=False)
                    nc.tensor.matmul(bank[6][:, :], weights_T[:, 5, :], x_T, start=False, stop=True
                                     ).then_inc(stage["gates_zn"], 1)
                j = k.back(2)
                if j.exists():
                    after(pe, "message", L1, j)
                    after(pe, "state_out", L1, j.back(3))
                    for a in range(A):
                        last = nc.tensor.transpose(sub(bank[3], a), sub(scaled[:, j.s3, :], a), ident[:, :])
                    last.then_inc(stage["msg_turned"], 1)

            for ph in range(PHASES):
                aggregate(ph)
                if ph == L1:
                    pe.wait_ge(s_mean, 1)
                    for g in range(3):
                        last = nc.tensor.matmul(bank[7][:, g:g + 1], weights_T[:, 1 + g, :], mean_col[:, :], start=True,
                                                stop=True, skip_group_check=True)
                    last.then_inc(s_gate_mm, 1)
                    pe.wait_ge(s_gate_c, 1)
                    steps(pe, dense_gru, FINAL[ph] + 1)
                else:
                    dense(ph)

        @block.scalar
        def _(act):
            act.wait_ge(s_weights_turned, 1)
            for i in range(3):
                n = min(4, 9 - 4 * i) * D
                last = nc.scalar.copy(weights_T[:, 4 * i:4 * i + n // D, :].rearrange("p i d -> p (i d)"), bank[4 + i][:, 0:n])
            last.then_inc(s_weights_out, 1)
            act.wait_ge(s_trips, 1)
            turns = act.value_load(trips[0:1, 0:1], min_val=2, max_val=MAXT)

            def group(ph, q, g, first=False):
                act.wait_ge(summed_eq[ph], q * 2 + (g + 1))
                if not first:
                    act.wait_ge(added[ph], q * (32 * C) + 16 * C * (g - 1))
                nc.scalar.copy(rows_sum[:, g, :, :].rearrange("p c d -> p (c d)"), bank[1 + g][:, :]).then_inc(rows_out[ph], 1)

            def aggregate(ph):
                group(ph, 0, 0, first=True)
                group(ph, 0, 1, first=True)
                with act.Fori(1, turns) as q:
                    group(ph, q, 0)
                    group(ph, q, 1)

            def turned_out(ph, k):
                after(act, "turned", ph, k)
                if ph in (L0, L2):
                    after(act, "product", ph, k.back(R))
                    nc.scalar.copy(own_T[:, k.slot, :], bank[k.two][:, :])
                after(act, "product", ph, k.back(S))
                nc.scalar.copy(gT[:, k.s3, :], bank[2 + k.two][:, :]).then_inc(stage["turned_out"], 1)

            def squares(ph, k):
                after(act, "biased", ph, k)
                rows = u
                if ph == L0:
                    after(act, "residual", ph, k.back(S))
                    nc.scalar.activation(r[:, k.s3, :], u[:, k.s3, :], ACT.Relu).then_inc(stage["relued"], 1)
                    after(act, "relued", ph, k)
                    rows = r
                for a in range(A):
                    last = nc.scalar.activation(junk_sq[:, k.s3, a, :], sub(rows[:, k.s3, :], a), ACT.Square,
                                                accum_out=ss[:, k.slot, a:a + 1])
                last.then_inc(stage["squared"], 1)

            def gelu(ph, k):
                after(act, "residual", ph, k)
                after(act, "result", ph, k.back(S))
                nc.scalar.activation(r[:, k.s3, :], res[:, k.s3, :], ACT.Gelu).then_inc(stage["gelued"], 1)

            def dense(ph):
                def step(k):
                    if k.back(1).exists():
                        turned_out(ph, k.back(1))
                    if ph in (CV1, CV2) and k.back(4).exists():
                        gelu(ph, k.back(4))
                    if ph in NORM_EPS and k.back(3).exists():
                        squares(ph, k.back(3))

                if ph in (CV1, CV2):
                    nc.scalar.preload_act_table(ACT.Gelu)
                steps(act, step, FINAL[ph] + 1)

            def dense_gru(k):
                if k.exists():
                    after(act, "turned", L1, k)
                    after(act, "gates_zn", L1, k.back(R))
                    after(act, "old_less_new", L1, k.back(R))
                    nc.scalar.copy(own_T[:, k.slot, :], bank[0][:, :])
                    after(act, "product", L1, k.back(S))
                    nc.scalar.copy(gT[:, k.s3, :], bank[1][:, :]).then_inc(stage["turned_out"], 1)
                j = k.back(5)
                if j.exists():
                    after(act, "state_turned", L1, j)
                    after(act, "normed1", L1, j.back(S))
                    nc.scalar.copy(state[:, j.s3, :], bank[3][:, :]).then_inc(stage["state_out"], 1)
                j = k.back(4)
                if j.exists():
                    after(act, "candidate_in", L1, j)
                    after(act, "state", L1, j.back(S))
                    nc.scalar.activation(new[:, j.s3, :], cand[:, j.s3, :], ACT.Tanh, bias=gate_c[:, 2:3]
                                         ).then_inc(stage["candidate"], 1)
                j = k.back(3)
                if j.exists():
                    after(act, "gates_rh", L1, j)
                    after(act, "reset_hidden", L1, j.back(S))
                    nc.scalar.activation(r[:, j.s3, :], bank[4][:, :], ACT.Sigmoid, bias=gate_c[:, 0:1]
                                         ).then_inc(stage["reset"], 1)
                    after(act, "gates_zn", L1, j)
                    after(act, "kept", L1, j.back(S))
                    nc.scalar.activation(update[:, j.s3, :], bank[6][:, :], ACT.Sigmoid, bias=gate_c[:, 1:2]
                                         ).then_inc(stage["update"], 1)
                j = k.back(2)
                if j.exists():
                    after(act, "msg_turned", L1, j)
                    after(act, "gates_zn", L1, j.back(S))
                    nc.scalar.copy(u[:, j.s3, :], bank[3][:, :]).then_inc(stage["msg_out"], 1)

            for ph in range(PHASES):
                aggregate(ph)
                if ph == L1:
                    act.wait_ge(s_gate_c, 1)
                    nc.scalar.preload_act_table(ACT.Sigmoid)
                    steps(act, dense_gru, FINAL[ph] + 1)
                else:
                    dense(ph)

        @block.vector
        def _(dve):
            done = [0]

            def link(ins):
                done[0] += 1
                ins.then_inc(s_dve, 1)
                dve.wait_ge(s_dve, done[0])

            V = nc.vector
            V.memset(row_n[:, :], 0.0)
            for i in range(2):
                V.memset(pack[i], FILL)
                V.memset(packed[i], FILL)
            V.memset(own_col, 0.0)
            link(V.memset(own_lane, -1.0))
            dve.wait_ge(s_edges, 32)
            ends_i, ends_f = (src_i, dst_i), (src_f, dst_f)
            for i in range(2):
                last = V.tensor_copy(ends_f[i][0:EP, :], ends_i[i][0:EP, :])
            link(last)
            link(V.tensor_tensor(differ[0:EP, :], src_f[0:EP, :], dst_f[0:EP, :], ALU.not_equal))
            V.reduce_sum(row_n[0:EP, :], differ[0:EP, :], AX.X).then_inc(s_row_n, 1)
            dve.wait_ge(s_row_turned, 1)
            link(V.reduce_max(trips_f[:, 0:1], bank[3][0:1, 0:P], AX.X))
            link(V.tensor_scalar(trips_f[:, 1:2], trips_f[:, 0:1], float(G2 - 1), float(2 * G2), ALU.add, ALU.max))
            link(V.tensor_copy(trips[:, 2:3], trips_f[:, 1:2]))
            link(V.tensor_scalar(trips[:, 0:1], trips[:, 2:3], G2.bit_length() - 1, None, ALU.logical_shift_right))
            V.tensor_scalar(trips[:, 1:2], trips[:, 0:1], -1.0, None, ALU.add).then_inc(s_trips, 1)
            dve.wait_ge(s_const, 1)
            link(V.tensor_scalar(place_f[0:EP, :], place_i[0:EP, :], 65536.0, -BIG, ALU.mult, ALU.add))
            for i in range(2):
                last = V.tensor_tensor(pack[i][0:EP, :], place_f[0:EP, :], ends_f[i][0:EP, :], ALU.add)
            link(last)
            for i in range(2):
                last = V.tensor_tensor(pack[i][0:EP, :], pack[i][0:EP, :], differ[0:EP, :], ALU.mult)
            link(last)
            link(V.tensor_scalar(place_f[0:EP, :], differ[0:EP, :], -FILL, FILL, ALU.mult, ALU.add))
            for i in range(2):
                last = V.tensor_tensor(pack[i][0:EP, :], pack[i][0:EP, :], place_f[0:EP, :], ALU.add)
            link(last)
            dve.wait_ge(s_trips, 1)
            turns = dve.value_load(trips[0:1, 0:1], min_val=2, max_val=MAXT)
            with dve.Fori(0, turns) as q:
                for i in range(2):
                    last = V.max(top8[:, i, :], pack[i])
                last.then_inc(s_top, 1)
                dve.wait_ge(s_top, q * 2 + 1)
                for i in range(2):
                    V.tensor_copy(packed[i][:, bass.ds(q * G2, G2)], top8[:, i, :])
                for i in range(2):
                    last = V.match_replace(pack[i], top8[:, i, :], pack[i], FILL)
                last.then_inc(s_top, 1)
                dve.wait_ge(s_top, q * 2 + 2)
                alone(dve)
            link(V.tensor_scalar(empty, packed[0], -BIG, None, ALU.is_lt))
            link(V.tensor_copy(trash_kf, trash_k[:, :]))
            link(V.tensor_tensor(empty, empty, trash_kf, ALU.mult))
            for i in range(2):
                last = V.tensor_copy(packed_i[i], packed[i])
            link(last)
            for i in range(2):
                last = V.tensor_scalar(gidx[:, 1 - i, :], packed_i[i], 0xFFFF, None, ALU.bitwise_and)
            link(last)
            for i in range(2):
                last = V.tensor_copy(packed[i], gidx[:, 1 - i, :])
            link(last)
            for i in range(2):
                last = V.tensor_tensor(key_f[:, i, :], packed[i], empty, ALU.add)
            link(last)

            def grid(lane, column, nodes, t1, t2, t3):
                V.tensor_scalar(t1, nodes, 2, P - 1, ALU.logical_shift_right, ALU.bitwise_and)
                V.tensor_scalar(t2, nodes, 9, 2, ALU.logical_shift_right, ALU.logical_shift_left)
                link(V.tensor_scalar(t3, nodes, A - 1, None, ALU.bitwise_and))
                V.tensor_copy(lane, t1)
                link(V.tensor_tensor(column, t2, t3, ALU.add))

            for i in range(2):
                link(V.tensor_copy(packed_i[i], key_f[:, i, :]))
                grid(key_lane[i], key_col[i], packed_i[i], *key_i)
            grid(own_lane[0:EP, :], own_col[0:EP, :], src_i[0:EP, :], *(t[0:EP, :] for t in own_i))
            link(V.tensor_scalar(place_f[0:EP, :], differ[0:EP, :], -1.0, 1.0, ALU.mult, ALU.add))
            link(V.tensor_tensor(own_lane[0:EP, :], own_lane[0:EP, :], place_f[0:EP, :], ALU.mult))
            link(V.tensor_tensor(own_lane[0:EP, :], own_lane[0:EP, :], differ[0:EP, :], ALU.subtract))

            def own_hot(j, slot, first=False):
                if not first:
                    dve.wait_ge(s_own_hist, j - (HOT - 1))
                V.tensor_scalar(hot_lane[:, slot, :], lane_f[:, :], own_lane[:, bass.ds(j, 1)], None, ALU.is_equal)
                V.tensor_scalar(hot_col[:, slot, :], col_f[:, :], own_col[:, bass.ds(j, 1)], None,
                                ALU.is_equal).then_inc(s_own_hot, 1)

            for j in range(HJ):
                own_hot(j, j % HOT, first=j < HOT)
            with dve.Fori(1, EJ // HJ) as q:
                for j in range(HJ):
                    own_hot(q * HJ + j, j % HOT)
            dve.wait_ge(s_own_hist, EJ)

            def key_hot(c, slot, first=False):
                if not first:
                    dve.wait_ge(s_key_hist, c - 1)
                for d in range(2):
                    V.tensor_scalar(hot_lane[:, 2 * slot + d, :], lane_f[:, :], key_lane[d][:, bass.ds(c, 1)], None, ALU.is_equal)
                    last = V.tensor_scalar(hot_col[:, 2 * slot + d, :], col_f[:, :], key_col[d][:, bass.ds(c, 1)], None,
                                           ALU.is_equal)
                last.then_inc(s_key_hot, 1)

            for c in range(G2):
                key_hot(c, c % 2, first=c < 2)
            with dve.Fori(1, turns) as q:
                for c in range(G2):
                    key_hot(q * G2 + c, c % 2)
            dve.wait_ge(s_key_hist, turns * G2)
            link(V.tensor_copy(hist[0], bank[0][:, 0:COLS]))
            V.tensor_tensor(hist[1], bank[1][:, 0:COLS], hist[0], ALU.add)
            link(V.tensor_tensor(hist[2], bank[2][:, 0:COLS], hist[0], ALU.add))
            on_grid = COLS - A
            V.tensor_copy(own_n[:, 0:on_grid], hist[0][:, 0:on_grid])
            V.tensor_copy(deg_s[:, 0:on_grid], hist[1][:, 0:on_grid])
            V.tensor_copy(deg_d[:, 0:on_grid], hist[2][:, 0:on_grid]).then_inc(s_hist_out, 1)
            dve.wait_ge(s_hist_out, 1)
            dve.wait_ge(s_shift, 96)
            V.tensor_scalar(own_n1[:, :], own_n[:, :], 1.0, None, ALU.add)
            V.tensor_scalar(deg_gcn[:, :], deg_d[:, :], 1.0, None, ALU.add).then_inc(s_nodes, 1)
            V.tensor_scalar(inv_s[:, :], deg_s[:, :], 1.0, None, ALU.max)
            link(V.tensor_scalar(inv_d[:, :], deg_d[:, :], 1.0, None, ALU.max))
            V.reciprocal(inv_s[:, :], inv_s[:, :])
            link(V.reciprocal(inv_d[:, :], inv_d[:, :]))
            dve.wait_ge(s_weights, 16 * 22)
            V.tensor_tensor(rows_bc[:, bl_, :], rows_bc[:, bl_, :], rows_bc[:, br_, :], ALU.add)
            link(V.tensor_tensor(rows_bc[:, bself_, :], rows_bc[:, bself_, :], rows_bc[:, bneigh_, :], ALU.add))
            V.memset(pass_mark_dve[:, :], 0.0).then_inc(s_biases, 1)

            def group(ph, q, g, first=False):
                key = 0 if ph == L0 else 1
                at_ = bass.ds(q * G2 + g * C, C)
                if not first:
                    dve.wait_ge(landed[ph][g], q * (16 * C))
                V.tensor_copy(idx_now[:, g, :], gidx[:, key, at_])
                V.tensor_copy(key_now[:, g, :], key_f[:, key, at_]).then_inc(staged[ph], 1)
                dve.wait_ge(keys_turned[ph], q * 2 + (g + 1))
                if not first:
                    dve.wait_ge(summed_eq[ph], q * 2 + (g - 1))
                for c in range(C):
                    last = V.tensor_scalar(equal[:, g, c, :], bank[0][:, :], key_now[:, g, c:c + 1], None, ALU.is_equal)
                last.then_inc(matched[ph], 1)
                dve.wait_ge(matched[ph], q * 2 + (g + 1))
                for c in range(C):
                    n = (c + 1) * P
                    last = V.scalar_tensor_tensor(out=junk[:, c, 0:n], in0=equal[:, g, c, 0:n], scalar=1.0,
                                                  in1=earlier[:, c, 0:n], op0=ALU.mult, op1=ALU.mult,
                                                  accum_out=n_earlier[:, g, c:c + 1])
                last.then_inc(counted[ph], 1)
                V.tensor_tensor(pick[:, g, 0, :], trash_f[:, :], key_now[:, g, :], ALU.subtract)
                dve.wait_ge(counted[ph], q * 2 + (g + 1))
                V.tensor_scalar(pick[:, g, 1, :], n_earlier[:, g, :], 1.0, None, ALU.min).then_inc(picked[ph], 1)
                dve.wait_ge(picked[ph], q * 6 + (3 * g + 1))
                V.tensor_tensor(pick[:, g, 2, :], pick[:, g, 0, :], pick[:, g, 1, :], ALU.mult).then_inc(picked[ph], 1)
                dve.wait_ge(picked[ph], q * 6 + (3 * g + 2))
                V.tensor_tensor(pick[:, g, 0, :], pick[:, g, 2, :], key_now[:, g, :], ALU.add).then_inc(picked[ph], 1)
                dve.wait_ge(picked[ph], q * 6 + (3 * g + 3))
                if not first:
                    dve.wait_ge(added[ph], q * (32 * C) + 16 * C * (g - 1))
                V.tensor_copy(to_now[:, g, :], pick[:, g, 0, :]).then_inc(to_ready[ph], 1)

            def aggregate(ph):
                group(ph, 0, 0, first=True)
                group(ph, 0, 1, first=True)
                with dve.Fori(1, turns) as q:
                    group(ph, q, 0)
                    group(ph, q, 1)

            def statistics(ph, k, rows, bn6, mv, ve, tag=""):
                for a in range(A):
                    last = V.bn_stats(bn6[:, k.slot, a, :], sub(rows, a))
                last.then_inc(stage["stats" + tag], 1)
                after(dve, "stats" + tag, ph, k)
                alone(dve)
                for a in range(A):
                    last = V.bn_aggr(mv[:, k.slot, a, :], bn6[:, k.slot, a, :])
                last.then_inc(stage["aggr" + tag], 1)
                after(dve, "aggr" + tag, ph, k)
                V.tensor_scalar(ve[:, k.slot, :], mv[:, k.slot, :, 1], LN_EPS, None, ALU.add).then_inc(stage["var_eps" + tag], 1)

            def shift(ph, k, mv, rs, nb, tag=""):
                V.scalar_tensor_tensor(out=nb[:, k.slot, :], in0=mv[:, k.slot, :, 0], scalar=-1.0, in1=rs,
                                       op0=ALU.mult, op1=ALU.mult).then_inc(stage["shifted" + tag], 1)
                after(dve, "shifted" + tag, ph, k)

            def residual(ph, k):
                x_ = own[:, k.slot, :] if ph in (L0, CV2) else extra[:, k.slot, :]
                if ph in NORM_EPS:
                    after(dve, "norm", ph, k)
                    V.tensor_scalar(nrm_e[:, k.slot, :], nrm[:, k.slot, :], NORM_EPS[ph], None, ALU.add).then_inc(stage["norm_eps"], 1)
                    after(dve, "norm_eps", ph, k)
                    V.reciprocal(nrm_inv[:, k.slot, :], nrm_e[:, k.slot, :]).then_inc(stage["norm_inv"], 1)
                    after(dve, "norm_inv", ph, k)
                    if ph != L0:
                        after(dve, "gelued", ph, k.back(S))
                    if ph == CV1:
                        after(dve, "own_ready", ph, k)
                        after_stores(dve, ph, k.back(S))
                    rows = r if ph == L0 else u
                    for a in range(A):
                        last = V.scalar_tensor_tensor(out=sub(res[:, k.s3, :], a), in0=sub(rows[:, k.s3, :], a),
                                                      scalar=nrm_inv[:, k.slot, a:a + 1], in1=sub(x_, a),
                                                      op0=ALU.mult, op1=ALU.add)
                else:
                    after(dve, "product", ph, k)
                    after(dve, "own_ready", ph, k)
                    last = V.tensor_tensor(res[:, k.s3, :], bank[4 + k.two][:, :], x_, ALU.add)
                last.then_inc(stage["residual"], 1)
                if ph in NORMED:
                    after(dve, "residual", ph, k)
                    statistics(ph, k, res[:, k.s3, :], bn6, mv, ve)

            def finish(ph, k):
                if ph in NORMED:
                    after(dve, "rstd", ph, k)
                    rs_ = rs[:, k.slot, :]
                    if ph == L2:
                        V.tensor_tensor(rsd[:, k.slot, :], rs_, dis[:, bass.ds(k.b * A, A)], ALU.mult).then_inc(stage["rstd_dis"], 1)
                        after(dve, "rstd_dis", ph, k)
                        rs_ = rsd[:, k.slot, :]
                    shift(ph, k, mv, rs_, nb)
                else:
                    after(dve, "gelued", ph, k)
                if ph in SEED:
                    after(dve, "seeded", ph, k.back(S))
                if ph == L0:
                    after(dve, "summed", ph, k.back(S))
                after_stores(dve, ph, k.back(S))
                for a in range(A):
                    if ph in NORMED:
                        last = V.tensor_scalar(sub(result[:, k.s3, :], a), sub(res[:, k.s3, :], a), rs_[:, a:a + 1],
                                               nb[:, k.slot, a:a + 1], ALU.mult, ALU.add)
                    else:
                        last = V.tensor_scalar(sub(result[:, k.s3, :], a), sub(r[:, k.s3, :], a), col(dis, k, a), None, ALU.mult)
                last.then_inc(stage["result"], 1)

            def dense(ph):
                def step(k):
                    if ph == L0 and k.exists():
                        after_loads(dve, ph, k)
                        for a in range(A):
                            last = V.scalar_tensor_tensor(out=sub(sm[:, k.s3, :], a), in0=sub(own[:, k.slot, :], a),
                                                          scalar=col(own_n, k, a), in1=sub(sm[:, k.s3, :], a),
                                                          op0=ALU.mult, op1=ALU.add)
                        last.then_inc(stage["own_added"], 1)
                    if k.back(5).exists():
                        finish(ph, k.back(5))
                    if k.back(4).exists():
                        residual(ph, k.back(4))
                    j = k.back(2)
                    if ph in NORM_EPS and j.exists():
                        after(dve, "product", ph, j)
                        after(dve, "relued" if ph == L0 else "squared", ph, j.back(S))
                        V.tensor_tensor(v3(u[:, j.s3, :]), v3(bank[4 + j.two][:, :]), each(BIAS[ph]),
                                        ALU.add).then_inc(stage["biased"], 1)

                if ph == L2:
                    dve.wait_ge(s_roots, 1)
                steps(dve, step, FINAL[ph] + 1)

            def dense_gru(k):
                j = k.back(8)
                if j.exists():
                    finish(L1, j)
                j = k.back(7)
                if j.exists():
                    after(dve, "rstd1", L1, j)
                    shift(L1, j, mv_1, rs_1[:, j.slot, :], nb_1, "1")
                    for a in range(A):
                        last = V.tensor_scalar(sub(res[:, j.s3, :], a), sub(state[:, j.s3, :], a), rs_1[:, j.slot, a:a + 1],
                                               nb_1[:, j.slot, a:a + 1], ALU.mult, ALU.add)
                    last.then_inc(stage["normed1"], 1)
                    after(dve, "normed1", L1, j)
                    V.tensor_tensor(v3(res[:, j.s3, :]), v3(res[:, j.s3, :]), each(gamma_), ALU.mult).then_inc(stage["scaled1"], 1)
                    after(dve, "scaled1", L1, j)
                    after(dve, "own_ready", L1, j)
                    V.tensor_tensor(res[:, j.s3, :], res[:, j.s3, :], extra[:, j.slot, :], ALU.add).then_inc(stage["residual"], 1)
                    after(dve, "residual", L1, j)
                    statistics(L1, j, res[:, j.s3, :], bn6, mv, ve)
                j = k.back(6)
                if j.exists():
                    after(dve, "state_out", L1, j)
                    statistics(L1, j, state[:, j.s3, :], bn6_1, mv_1, ve_1, "1")
                j = k.back(5)
                if j.exists():
                    after(dve, "kept", L1, j)
                    after(dve, "candidate", L1, j)
                    V.tensor_tensor(kept[:, j.s3, :], kept[:, j.s3, :], new[:, j.s3, :], ALU.add).then_inc(stage["state"], 1)
                j = k.back(1)
                if j.exists():
                    after(dve, "product", L1, j)
                    after(dve, "own_message", L1, j.back(S))
                    after(dve, "msg_turned", L1, j.back(S))
                    for a in range(A):
                        last = V.scalar_tensor_tensor(out=sub(scaled[:, j.s3, :], a), in0=rows_bc[:, bmsg_, :],
                                                      scalar=col(deg_d, j, a), in1=sub(bank[2], a), op0=ALU.mult, op1=ALU.add)
                    last.then_inc(stage["message"], 1)
                j = k.back(3)
                if j.exists():
                    after(dve, "gates_rh", L1, j)
                    after(dve, "reset", L1, j)
                    after(dve, "candidate", L1, j.back(S))
                    V.scalar_tensor_tensor(out=cand[:, j.s3, :], in0=bank[5][:, :], scalar=gate_b[:, 1, 2:3],
                                           in1=r[:, j.s3, :], op0=ALU.add, op1=ALU.mult).then_inc(stage["reset_hidden"], 1)
                    after(dve, "gates_zn", L1, j)
                    after(dve, "reset_hidden", L1, j)
                    V.tensor_tensor(cand[:, j.s3, :], cand[:, j.s3, :], bank[7][:, :], ALU.add).then_inc(stage["candidate_in"], 1)

            for ph in range(PHASES):
                if ph == L1:
                    dve.wait_ge(stage["summed"], NB)
                    V.tensor_copy(mean_col[:, :], bank[6][:, 0:1]).then_inc(s_mean, 1)
                aggregate(ph)
                if ph == L1:
                    dve.wait_ge(s_gate_mm, 1)
                    link(V.tensor_tensor(gate_c[:, :], bank[7][:, 0:3], gate_b[:, 0, :], ALU.add))
                    V.tensor_tensor(gate_c[:, 0:2], gate_c[:, 0:2], gate_b[:, 1, 0:2], ALU.add).then_inc(s_gate_c, 1)
                    steps(dve, dense_gru, FINAL[ph] + 1)
                else:
                    dense(ph)


_INS = ['x', 'src', 'dst', 'L0_gnn_Wl', 'L0_gnn_bl', 'L0_gnn_Wr', 'L0_gnn_br', 'L1_gnn_W_msg', 'L1_gnn_b_msg',
        'L1_gnn_w_ih', 'L1_gnn_w_hh', 'L1_gnn_b_ih', 'L1_gnn_b_hh', 'L1_gnn_ln_gamma', 'L1_gnn_ln_beta',
        'L2_gnn_w_self', 'L2_gnn_b_self', 'L2_gnn_w_neigh', 'L2_gnn_b_neigh', 'L3_gnn_W1', 'L3_gnn_b1',
        'L3_gnn_W2', 'L3_gnn_b2', 'L3_gnn_W3', 'L3_gnn_b3']


def kernel(**inputs):
    import numpy as _np
    import concourse.bacc as _bacc
    from concourse import mybir as _mybir
    from concourse.bass_utils import run_bass_kernel_spmd as _run

    nc = _bacc.Bacc("TRN2", target_bir_lowering=False, num_devices=1)
    arrays, args = {}, []
    for name in _INS:
        a = _np.ascontiguousarray(inputs[name])
        arrays[f"in_{name}_dram"] = a
        args.append(nc.dram_tensor(f"in_{name}_dram", a.shape, _mybir.dt.from_np(a.dtype), kind="ExternalInput").ap())
    args.append(nc.dram_tensor("out_0_dram", (N, D), _mybir.dt.float32, kind="ExternalOutput").ap())
    build(nc, *args)
    r = _run(nc, [arrays], core_ids=[0])
    return r.results[0]["out_0_dram"]
```

```python
from contextlib import ExitStack

import concourse.bass as bass
from concourse import mybir

ALU = mybir.AluOpType
ACT = mybir.ActivationFunctionType
AX = mybir.AxisListType
F32 = mybir.dt.float32
F16 = mybir.dt.float16
BF16 = mybir.dt.bfloat16
I32 = mybir.dt.int32

P = 128
D = 128
N = 50000
E = 62500
A = 4
BLK = P * A
NB = -(-N // BLK)
LAST = N - BLK
SHIFT = ((NB - 1) * BLK - LAST) // A
COLS = NB * A
R = 6
S = 3

EP = 125
EJ = E // EP
C = 4
G2 = 2 * C
MAXT = -(-EJ // G2)
KC = MAXT * G2
TRASH = N
ZROWS = 6
ROWS = 396 * P
BIG = float(1 << 24)
FILL = -2.0 * BIG
HOT = 5
HJ = 10

L0, L1, L2, CV1, CV2, CV3 = range(6)
PHASES = 6

LN_EPS = 1e-5
NORM_EPS = {L0: 1e-6, CV1: 1e-8, CV2: 1e-8}

STAGES = {
    "own_added": (L0,),
    "prescaled": (L0, L2, CV1, CV2, CV3),
    "own_ready": (L1, CV1, CV3),
    "turned": tuple(range(6)),
    "turned_out": tuple(range(6)),
    "product": tuple(range(6)),
    "relued": (L0,),
    "squared": (L0, CV1, CV2),
    "norm": (L0, CV1, CV2),
    "norm_eps": (L0, CV1, CV2),
    "norm_inv": (L0, CV1, CV2),
    "residual": tuple(range(6)),
    "stats": (L0, L1, L2, CV3),
    "aggr": (L0, L1, L2, CV3),
    "var_eps": (L0, L1, L2, CV3),
    "rstd": (L0, L1, L2, CV3),
    "rstd_dis": (L2,),
    "shifted": (L0, L1, L2, CV3),
    "gelued": (CV1, CV2),
    "result": tuple(range(6)),
    "seeded": (L0, L1, L2, CV1, CV2),
    "summed": (L0,),
    "message": (L1,),
    "own_message": (L1,),
    "msg_turned": (L1,),
    "msg_out": (L1,),
    "gates_rh": (L1,),
    "gates_zn": (L1,),
    "reset": (L1,),
    "update": (L1,),
    "reset_hidden": (L1,),
    "candidate_in": (L1,),
    "candidate": (L1,),
    "old_less_new": (L1,),
    "kept": (L1,),
    "state": (L1,),
    "state_turned": (L1,),
    "state_out": (L1,),
    "stats1": (L1,), "aggr1": (L1,), "var_eps1": (L1,),
    "rstd1": (L1,),
    "shifted1": (L1,), "scaled1": (L1,),
    "normed1": (L1,),
}


def base(stage, ph):
    return NB * sum(q < ph for q in STAGES[stage])


STORES = {L0: 2, L1: 2, L2: 2, CV1: 3, CV2: 2, CV3: 1}
NORMED = (L0, L1, L2, CV3)
FINAL = {L0: 6, L1: 9, L2: 5, CV1: 5, CV2: 5, CV3: 5}
DEPTH = 3


def stores_before(ph, slot):
    return 16 * sum(STORES[q] for q in range(ph)) * len(range(slot, NB, R))


def build(nc, x, src, dst, Wl, bl, Wr, br, W_msg, b_msg, w_ih, w_hh, b_ih, b_hh, gamma, beta,
          w_self, b_self, w_neigh, b_neigh, W1, b1, W2, b2, W3, b3, out):
    with ExitStack() as ctx:
        def sb(name, shape, dt=F32):
            return ctx.enter_context(nc.sbuf_tensor(name, shape, dt))

        def sem(name):
            return ctx.enter_context(nc.semaphore(name))

        def table(name, rows):
            return nc.dram_tensor(name, [rows, D], F32, kind="Internal").ap()

        x1, x2, y3, h1, y4, y5 = (table(n, N) for n in ("x1", "x2", "y3", "h1", "y4", "y5"))
        sums = [table("sum_even", ROWS), table("sum_odd", ROWS)]
        OWN = [x, x1, x2, y3, h1, y3]
        SOURCE = [x, x1, x2, y3, y4, y5]
        RESULT = [x1, x2, y3, y4, y5, out]

        ident = sb("ident", [P, P])
        zeros = sb("zeros", [P, ZROWS * D])
        ones = sb("ones", [P, P])
        inv_n = sb("inv_n", [P, 2])
        powers = sb("powers", [P, 2, A])
        earlier = sb("earlier", [P, C, C * P])
        lane_f = sb("lane_f", [P, P], F16)
        col_f = sb("col_f", [P, COLS], F16)
        trash_f = sb("trash_f", [P, C])

        weights_T = sb("weights_T", [P, 9, D])
        straight = sb("straight", [P, 5, D])
        rows_bc = sb("rows_bc", [P, 10, D])
        bl_, br_, bmsg_, gamma_, beta_, bself_, bneigh_, bc1_, bc2_, bc3_ = range(10)
        gate_b = sb("gate_b", [P, 2, 3])
        gate_c = sb("gate_c", [P, 3])
        mean_col = sb("mean_col", [P, 1])
        BIAS = {L0: bl_, L2: bself_, CV1: bc1_, CV2: bc2_, CV3: bc3_}

        own_n = sb("own_n", [P, COLS])
        own_n1 = sb("own_n1", [P, COLS])
        deg_s = sb("deg_s", [P, COLS])
        deg_d = sb("deg_d", [P, COLS])
        inv_s = sb("inv_s", [P, COLS])
        inv_d = sb("inv_d", [P, COLS])
        dis = sb("dis", [P, COLS])
        dis_inv = sb("dis_inv", [P, COLS])
        deg_gcn = sb("deg_gcn", [P, COLS])
        SCALE = {L0: inv_s, L2: inv_d, CV1: dis, CV2: dis, CV3: dis}
        SEED = {L0: own_n, L1: own_n, L2: own_n1, CV1: own_n1, CV2: own_n1}

        key_f = sb("key_f", [P, 2, KC])
        gidx = sb("gidx", [P, 2, KC], I32)
        trips = sb("trips", [1, 4], I32)
        trips_f = sb("trips_f", [1, 4])

        ROOMS = 3 * R + 13 * S
        arena = sb("arena", [P, ROOMS, BLK])
        at = [0]

        def ring(n):
            at[0] += n
            return arena[:, at[0] - n:at[0], :]

        own, own_T, extra = ring(R), ring(R), ring(R)
        sm, scaled, gT = ring(S), ring(S), ring(S)
        u, r, res = ring(S), ring(S), ring(S)
        result, seed, update = ring(S), ring(S), ring(S)
        new, kept, state, cand = ring(S), ring(S), ring(S), ring(S)
        at[0] = 0

        def prep(k):
            at[0] += 1
            assert at[0] <= ROOMS
            return arena[:, at[0] - 1, 0:k]

        raw = arena[:, ROOMS - 3:ROOMS, :].rearrange("p a k -> p (a k)")[:, 0:9 * D].rearrange("p (i d) -> p i d", d=D)
        src_i, dst_i = prep(EJ).bitcast(I32), prep(EJ).bitcast(I32)
        src_f, dst_f, differ, place_f = prep(EJ), prep(EJ), prep(EJ), prep(EJ)
        pack = [prep(EJ), prep(EJ)]
        packed = [prep(KC), prep(KC)]
        packed_i = [prep(KC).bitcast(I32), prep(KC).bitcast(I32)]
        empty, trash_kf, trash_k, place_i = prep(KC), prep(KC), prep(KC).bitcast(I32), prep(EJ).bitcast(I32)
        own_lane, own_col = prep(EJ), prep(EJ)
        own_i = [prep(EJ).bitcast(I32), prep(EJ).bitcast(I32), prep(EJ).bitcast(I32)]
        key_lane = [prep(KC), prep(KC)]
        key_col = [prep(KC), prep(KC)]
        key_i = [prep(KC).bitcast(I32) for _ in range(3)]
        hist = [prep(COLS), prep(COLS), prep(COLS)]
        top8 = sb("top8", [P, 2, 8])
        row_n = sb("row_n", [P, 1])
        hot_lane = sb("hot_lane", [P, HOT, P], F16)
        hot_col = sb("hot_col", [P, HOT, COLS], F16)

        idx_now = sb("idx_now", [P, 2, C], I32)
        key_now = sb("key_now", [P, 2, C])
        to_now = sb("to_now", [P, 2, C], I32)
        rows_in = sb("rows_in", [P, 2, C, D])
        rows_sum = sb("rows_sum", [P, 2, C, D])
        equal = sb("equal", [P, 2, C, C * P])
        junk = sb("junk", [P, C, C * P], BF16)
        pass_mark = sb("pass_mark", [P, 1])
        pass_mark_dve = sb("pass_mark_dve", [P, 1])
        n_earlier = sb("n_earlier", [P, 2, C])
        pick = sb("pick", [P, 2, 3, C])

        ss = sb("ss", [P, R, A])
        nrm = sb("nrm", [P, R, A])
        nrm_e = sb("nrm_e", [P, R, A])
        nrm_inv = sb("nrm_inv", [P, R, A])
        bn6 = sb("bn6", [P, R, A, 6])
        mv = sb("mv", [P, R, A, 2])
        ve = sb("ve", [P, R, A])
        rs = sb("rs", [P, R, A])
        rsd = sb("rsd", [P, R, A])
        nb = sb("nb", [P, R, A])
        bn6_1 = sb("bn6_1", [P, R, A, 6])
        mv_1 = sb("mv_1", [P, R, A, 2])
        ve_1 = sb("ve_1", [P, R, A])
        rs_1 = sb("rs_1", [P, R, A])
        nb_1 = sb("nb_1", [P, R, A])
        junk_sq = sb("junk_sq", [P, S, A, D], BF16)

        bank = [ctx.enter_context(nc.psum_tensor(f"bank{i}", [P, BLK], F32)) for i in range(8)]

        stage = {n: sem(n) for n in STAGES}
        loaded = [sem(f"loaded{i}") for i in range(R)]
        stored = [sem(f"stored{i}") for i in range(R)]
        (s_edges, s_weights, s_zero_tile, s_zeroed, s_shift, s_const, s_dve, s_pool, s_row_n, s_row_turned, s_trips,
         s_weights_turned, s_weights_out, s_top, s_own_hot, s_own_hist, s_key_hot, s_key_hist, s_hist_out, s_nodes,
         s_roots, s_biases, s_mean, s_gate_mm, s_gate_c, s_pass_done, s_alone) = (sem(n) for n in (
             "edges_loaded", "weights_loaded", "zero_tile", "sums_zeroed", "last_block_shifted", "constants",
             "dve_step", "pool_step", "rows_counted", "row_counts_turned", "trips_known", "weights_turned",
             "weights_out", "top8_step", "own_hot", "own_hist", "key_hot", "key_hist", "hist_out", "degrees",
             "roots", "biases", "mean_column", "gate_product", "gate_constants", "pass_done", "wait_alone"))
        staged, keys_turned, matched, counted, picked, to_ready, summed_eq, rows_out, added = (
            [sem(f"{n}{ph}") for ph in range(PHASES)] for n in
            ("staged", "keys_turned", "matched", "counted", "picked", "to_ready",
             "summed_eq", "rows_out", "added"))

        class Blk:

            def __init__(self, b, slot, turn):
                self.b, self.slot, self.turn = b, slot % R, turn
                self.s3 = self.slot % S
                self.two = self.slot % 2

            def back(self, n):
                return Blk(self.b - n, self.slot - n, self.turn + (self.slot - n) // R)

            def exists(self):
                return not isinstance(self.b, int) or 0 <= self.b < NB

            def last(self):
                return isinstance(self.b, int) and self.b == NB - 1

        landed = [[sem(f"landed{ph}_{g}") for g in range(2)] for ph in range(PHASES)]

        def after(eng, name, ph, k):
            if k.exists():
                eng.wait_ge(stage[name], k.b + (base(name, ph) + 1))

        def after_stores(eng, ph, k):
            if k.exists():
                eng.wait_ge(stored[k.slot], (k.turn + 1) * (16 * STORES[ph]) + stores_before(ph, k.slot))

        def after_loads(eng, ph, k):
            eng.wait_ge(loaded[k.slot], (k.turn + 1) * 32 + 32 * ph * len(range(k.slot, NB, R)))

        def alone(eng):
            eng.sem_inc(s_alone, 1)

        def rows_of(t, k):
            first = LAST if k.last() else k.b * BLK
            return t[bass.ds(first, BLK), :].rearrange("(p a) d -> p (a d)", a=A)

        def col(t, k, a):
            return t[:, bass.ds(k.b * A + a, 1)]

        def cols(t, k):
            return t[:, bass.ds(k.b * A, A)].unsqueeze(2).to_broadcast([P, A, D])

        def each(i):
            return rows_bc[:, i, :].unsqueeze(1).to_broadcast([P, A, D])

        def sub(t, a):
            return t[:, a * D:(a + 1) * D]

        def v3(t):
            return t.rearrange("p (a d) -> p a d", a=A)

        def product_bank(ph, k):
            return bank[4 + (k.s3 if ph in (CV1, CV2) else k.two)]

        def steps(eng, body, depth):
            first = -(-(depth + S) // R)
            whole = (NB - 2) // R
            for n in range(first * R):
                body(Blk(n, n, n // R))
            with eng.Fori(first, whole) as q:
                for slot in range(R):
                    body(Blk(q * R + slot, slot, q))
            for n in range(whole * R, NB + depth):
                body(Blk(n, n, n // R))

        block = ctx.enter_context(nc.Block())

        @block.sync
        def _(sp):
            sp.dma_start(src_i[0:EP, :], src.rearrange("(p j) -> p j", j=EJ)).then_inc(s_edges, 16)
            sp.dma_start(dst_i[0:EP, :], dst.rearrange("(p j) -> p j", j=EJ)).then_inc(s_edges, 16)
            sp.dma_start(raw[:, 0, :], W_msg).then_inc(s_weights, 16)
            sp.dma_start(raw[:, 1:4, :], w_ih.rearrange("(g p) d -> p g d", p=P)).then_inc(s_weights, 16)
            sp.dma_start(raw[:, 4:7, :], w_hh.rearrange("(g p) d -> p g d", p=P)).then_inc(s_weights, 16)
            sp.dma_start(raw[:, 7, :], w_self).then_inc(s_weights, 16)
            sp.dma_start(raw[:, 8, :], w_neigh).then_inc(s_weights, 16)
            for i, w in enumerate((Wl, Wr, W1, W2, W3)):
                sp.dma_start(straight[:, i, :], w).then_inc(s_weights, 16)
            for i, v in enumerate((bl, br, b_msg, gamma, beta, b_self, b_neigh, b1, b2, b3)):
                sp.dma_start(rows_bc[:, i, :], v.rearrange("(o d) -> o d", o=1).to_broadcast([P, D])).then_inc(s_weights, 16)
            with nc.allow_non_contiguous_dma(reason="three numbers a partition, once"):
                sp.dma_start(gate_b[:, 0, :], b_ih.rearrange("(g p) -> p g", p=P)).then_inc(s_weights, 16)
                sp.dma_start(gate_b[:, 1, :], b_hh.rearrange("(g p) -> p g", p=P)).then_inc(s_weights, 16)
            sp.wait_ge(s_zero_tile, 1)
            sp.dma_start(sums[0].rearrange("(p c r) d -> p c (r d)", p=P, r=ZROWS),
                         zeros[:, :].unsqueeze(1).to_broadcast([P, ROWS // P // ZROWS, ZROWS * D])).then_inc(s_zeroed, 16)
            sp.dma_start(sums[1][TRASH:TRASH + BLK, :].rearrange("(p a) d -> p (a d)", a=A),
                         zeros[:, 0:A * D]).then_inc(s_zeroed, 16)
            sp.wait_ge(s_hist_out, 1)
            for t, h in ((own_n, hist[0]), (deg_s, hist[1]), (deg_d, hist[2])):
                sp.dma_start(t[0:SHIFT, COLS - A:COLS], h[P - SHIFT:P, COLS - 2 * A:COLS - A]).then_inc(s_shift, 16)
                sp.dma_start(t[SHIFT:P, COLS - A:COLS], h[0:P - SHIFT, COLS - A:COLS]).then_inc(s_shift, 16)

            def load(ph, k):
                for name in {L0: ("residual",), L1: ("turned", "own_message"), L2: ("residual",),
                             CV1: ("own_ready",), CV2: ("residual",), CV3: ("own_ready",)}[ph]:
                    after(sp, name, ph, k.back(R))
                    alone(sp)
                sp.dma_start(own[:, k.slot, :], rows_of(OWN[ph], k)).then_inc(loaded[k.slot], 16)
                after(sp, "turned" if ph == L1 else "prescaled", ph, k.back(S))
                alone(sp)
                sp.dma_start(sm[:, k.s3, :], rows_of(sums[ph % 2], k)).then_inc(loaded[k.slot], 16)

            def store_h1(k):
                after(sp, "residual", CV1, k)
                alone(sp)
                sp.dma_start(rows_of(h1, k), res[:, k.s3, :]).then_inc(stored[k.slot], 16)

            def store_result(ph, k):
                if k.last():
                    after_stores(sp, ph, k.back(1))
                    if ph == CV1:
                        store_h1(k)
                after(sp, "result", ph, k)
                alone(sp)
                sp.dma_start(rows_of(RESULT[ph], k), result[:, k.s3, :]).then_inc(stored[k.slot], 16)

            def store_seed(ph, k):
                after(sp, "seeded", ph, k)
                alone(sp)
                sp.dma_start(rows_of(sums[(ph + 1) % 2], k), seed[:, k.s3, :]).then_inc(stored[k.slot], 16)

            def dense(ph):
                sp.wait_ge(s_pass_done, ph + 1)
                load(ph, Blk(0, 0, 0))

                def step(k):
                    if not isinstance(k.b, int) or k.b + 1 < NB:
                        load(ph, k.back(-1))
                    if ph in SEED and k.back(FINAL[ph] + 2).exists():
                        store_seed(ph, k.back(FINAL[ph] + 2))
                    if k.back(FINAL[ph] + 1).exists():
                        store_result(ph, k.back(FINAL[ph] + 1))
                    if ph == CV1 and k.back(FINAL[ph]).exists() and not k.back(FINAL[ph]).last():
                        store_h1(k.back(FINAL[ph]))

                steps(sp, step, FINAL[ph] + DEPTH)

            for ph in range(PHASES):
                dense(ph)
            for slot in range(R):
                sp.wait_ge(stored[slot], stores_before(PHASES, slot))

        @block.gpsimd
        def _(pool):
            pool.memset(zeros[:, :], 0.0).then_inc(s_zero_tile, 1)
            pool.memset(ones[:, :], 1.0)
            pool.memset(ident[:, :], 0.0)
            pool.memset(earlier[:, :, :], 0.0)
            pool.memset(inv_n[:, :], 1.0 / N)
            pool.memset(powers[:, 0, :], -0.5)
            pool.memset(powers[:, 1, :], 0.5)
            pool.iota(lane_f[:, :], [[1, P]], base=0, channel_multiplier=0, allow_small_or_imprecise_dtypes=True)
            pool.iota(col_f[:, :], [[1, COLS]], base=0, channel_multiplier=0, allow_small_or_imprecise_dtypes=True)
            pool.iota(place_i[:, :], [[1, EJ]], base=0, channel_multiplier=0)
            pool.iota(trash_k[:, :], [[0, KC // C], [P, C]], base=TRASH, channel_multiplier=1).then_inc(s_pool, 1)
            pool.wait_ge(s_pool, 1)
            pool.affine_select(out=ident[:, :], in_=ident[:, :], compare_op=ALU.not_equal, fill=1.0, base=0,
                               pattern=[[-1, P]], channel_multiplier=1)
            pool.affine_select(out=inv_n[:, 1:2], in_=inv_n[:, 1:2], compare_op=ALU.is_ge, fill=0.0, base=-SHIFT,
                               pattern=[[0, 1]], channel_multiplier=1)
            for c in range(C):
                if c:
                    pool.memset(earlier[:, c, 0:c * P], 1.0)
                pool.affine_select(out=earlier[:, c, c * P:(c + 1) * P], in_=ones[:, :], compare_op=ALU.is_ge, fill=0.0,
                                   base=-1, pattern=[[-1, P]], channel_multiplier=1)
            pool.tensor_copy(trash_f[:, :], trash_k[:, 0:C]).then_inc(s_const, 1)
            pool.wait_ge(s_nodes, 1)
            pool.tensor_tensor(dis[:, :], deg_gcn[:, :], powers[:, 0, 0:1].to_broadcast([P, COLS]), ALU.pow)
            pool.tensor_tensor(dis_inv[:, :], deg_gcn[:, :], powers[:, 1, 0:1].to_broadcast([P, COLS]), ALU.pow).then_inc(s_roots, 1)
            pool.wait_ge(s_trips, 1)
            turns = pool.value_load(trips[0:1, 0:1], min_val=3, max_val=MAXT)
            last_turn = pool.value_load(trips[0:1, 1:2], min_val=2, max_val=MAXT - 1)

            def gather(ph, q, g):
                pool.wait_ge(staged[ph], q * 2 + (g + 1))
                alone(pool)
                if not (isinstance(q, int) and q == 0):
                    pool.wait_ge(summed_eq[ph], q * 2 + (g - 1))
                    alone(pool)
                for c in range(C):
                    pool.indirect_dma_start(rows_in[:, g, c, :], None, SOURCE[ph],
                                            bass.IndirectOffsetOnAxis(ap=idx_now[:, g, c:c + 1], axis=0)
                                            ).then_inc(landed[ph][g], 16)

            def add(ph, q, g, first=False):
                room = g % 2
                pool.wait_ge(rows_out[ph], q * 2 + (g + 1))
                alone(pool)
                pool.wait_ge(to_ready[ph], q * 2 + (g + 1))
                alone(pool)
                if not first:
                    pool.wait_ge(added[ph], q * (32 * C) + 16 * C * g)
                    alone(pool)
                for c in range(C):
                    pool.indirect_dma_start(sums[ph % 2], bass.IndirectOffsetOnAxis(ap=to_now[:, room, c:c + 1], axis=0),
                                            rows_sum[:, room, c, :], None, compute_op=ALU.add).then_inc(added[ph], 16)

            def aggregate(ph):
                if ph == L0:
                    pool.wait_ge(s_zeroed, 32)
                else:
                    for slot in range(R):
                        pool.wait_ge(stored[slot], stores_before(ph, slot))
                gather(ph, 0, 0)
                gather(ph, 0, 1)
                add(ph, 0, 0, first=True)
                with pool.Fori(1, turns) as q:
                    gather(ph, q, 0)
                    add(ph, q, -1)
                    gather(ph, q, 1)
                    add(ph, q, 0)
                add(ph, last_turn, 1)
                pool.wait_ge(added[ph], turns * (32 * C))
                alone(pool)
                pool.memset(pass_mark[:, :], 0.0).then_inc(s_pass_done, 1)

            def power(ph, k, out_, in_, i, needs, gives):
                after(pool, needs, ph, k)
                pool.tensor_tensor(out_[:, k.slot, :], in_[:, k.slot, :], powers[:, i, :], ALU.pow).then_inc(stage[gives], 1)

            def prescale(k):
                after(pool, "own_added", L0, k)
                after(pool, "turned", L0, k.back(S))
                pool.tensor_tensor(v3(scaled[:, k.s3, :]), v3(sm[:, k.s3, :]), cols(SCALE[L0], k),
                                   ALU.mult).then_inc(stage["prescaled"], 1)

            def operand(ph, k):
                after_loads(pool, ph, k)
                after(pool, "residual", ph, k.back(R))
                pool.tensor_tensor(v3(extra[:, k.slot, :]), v3(own[:, k.slot, :]), cols(dis_inv, k),
                                   ALU.mult).then_inc(stage["own_ready"], 1)

            def seeds(ph, k):
                after(pool, "result", ph, k)
                after_stores(pool, ph, k.back(S))
                pool.tensor_tensor(v3(seed[:, k.s3, :]), v3(result[:, k.s3, :]), cols(SEED[ph], k),
                                   ALU.mult).then_inc(stage["seeded"], 1)

            def dense(ph):
                def step(k):
                    j = k.back(FINAL[ph] - 1)
                    if ph in NORMED and j.exists():
                        power(ph, j, rs, ve, 0, "var_eps", "rstd")
                    if k.exists():
                        if ph == L0:
                            prescale(k)
                        if ph in (CV1, CV3):
                            operand(ph, k)
                    if ph in SEED and k.back(FINAL[ph] + 1).exists():
                        seeds(ph, k.back(FINAL[ph] + 1))
                    if ph in NORM_EPS and k.back(3).exists():
                        power(ph, k.back(3), nrm, ss, 1, "squared", "norm")

                steps(pool, step, FINAL[ph] + DEPTH)

            def dense_gru(k):
                if k.back(7).exists():
                    power(L1, k.back(7), rs_1, ve_1, 0, "var_eps1", "rstd1")
                j = k.back(3)
                if j.exists():
                    after_loads(pool, L1, j)
                    after(pool, "message", L1, j)
                    after(pool, "residual", L1, j.back(R))
                    pool.tensor_tensor(extra[:, j.slot, :], own[:, j.slot, :], scaled[:, j.s3, :],
                                       ALU.add).then_inc(stage["own_message"], 1)
                    after(pool, "own_message", L1, j)
                    pool.tensor_tensor(v3(extra[:, j.slot, :]), v3(extra[:, j.slot, :]), each(beta_),
                                       ALU.add).then_inc(stage["own_ready"], 1)
                j = k.back(4)
                if j.exists():
                    after(pool, "candidate", L1, j)
                    after(pool, "update", L1, j)
                    after(pool, "turned_out", L1, j)
                    after(pool, "state_turned", L1, j.back(S))
                    pool.tensor_tensor(kept[:, j.s3, :], own_T[:, j.slot, :], new[:, j.s3, :],
                                       ALU.subtract).then_inc(stage["old_less_new"], 1)
                    after(pool, "old_less_new", L1, j)
                    pool.tensor_tensor(kept[:, j.s3, :], kept[:, j.s3, :], update[:, j.s3, :],
                                       ALU.mult).then_inc(stage["kept"], 1)
                if k.back(8).exists():
                    power(L1, k.back(8), rs, ve, 0, "var_eps", "rstd")

            for ph in range(PHASES):
                aggregate(ph)
                if ph == L1:
                    steps(pool, dense_gru, FINAL[ph] + DEPTH)
                else:
                    dense(ph)

        @block.tensor
        def _(pe):
            pe.wait_ge(s_const, 1)
            pe.wait_ge(s_row_n, 1)
            nc.tensor.transpose(bank[3][0:1, 0:P], row_n[:, :], ident[:, :]).then_inc(s_row_turned, 1)
            pe.wait_ge(s_weights, 16 * 22)
            for i in range(9):
                last = nc.tensor.transpose(bank[4 + i // 4][:, i % 4 * D:(i % 4 + 1) * D], raw[:, i, :], ident[:, :])
            last.then_inc(s_weights_turned, 1)

            def own_hist(j, slot, first=False):
                pe.wait_ge(s_own_hot, j + 1)
                nc.tensor.matmul(bank[0][:, 0:COLS], hot_lane[:, slot, :], hot_col[:, slot, :], start=first, stop=True,
                                 skip_group_check=True).then_inc(s_own_hist, 1)

            for j in range(HJ):
                own_hist(j, j % HOT, first=j == 0)
            with pe.Fori(1, EJ // HJ) as q:
                for j in range(HJ):
                    own_hist(q * HJ + j, j % HOT)

            def key_hist(c, slot, first=False):
                pe.wait_ge(s_key_hot, c + 1)
                for d in range(2):
                    last = nc.tensor.matmul(bank[1 + d][:, 0:COLS], hot_lane[:, 2 * slot + d, :], hot_col[:, 2 * slot + d, :],
                                            start=first, stop=True, skip_group_check=True)
                last.then_inc(s_key_hist, 1)

            pe.wait_ge(s_trips, 1)
            turns = pe.value_load(trips[0:1, 0:1], min_val=3, max_val=MAXT)
            last_turn = pe.value_load(trips[0:1, 1:2], min_val=2, max_val=MAXT - 1)
            for c in range(G2):
                key_hist(c, c % 2, first=c == 0)
            with pe.Fori(1, turns) as q:
                for c in range(G2):
                    key_hist(q * G2 + c, c % 2)

            def keys(ph, q, g, first=False):
                pe.wait_ge(staged[ph], q * 2 + (g + 1))
                if not first:
                    pe.wait_ge(matched[ph], q * 2 + g)
                for c in range(C):
                    last = nc.tensor.transpose(sub(bank[0], c), key_now[:, g, c:c + 1].to_broadcast([P, P]), ident[:, :])
                last.then_inc(keys_turned[ph], 1)

            def sum_equal(ph, q, g, first=False):
                room = g % 2
                pe.wait_ge(matched[ph], q * 2 + (g + 1))
                pe.wait_ge(landed[ph][room], q * (16 * C) + (16 * C if g >= 0 else 0))
                if not first:
                    pe.wait_ge(rows_out[ph], q * 2 + (g - 1))
                for c in range(C):
                    for e in range(C):
                        last = nc.tensor.matmul(sub(bank[1 + room], c), equal[:, room, e, c * P:(c + 1) * P],
                                                rows_in[:, room, e, :], start=e == 0, stop=e == C - 1)
                last.then_inc(summed_eq[ph], 1)

            def aggregate(ph):
                keys(ph, 0, 0, first=True)
                keys(ph, 0, 1)
                sum_equal(ph, 0, 0, first=True)
                keys(ph, 1, 0)
                sum_equal(ph, 1, -1, first=True)
                keys(ph, 1, 1)
                sum_equal(ph, 1, 0)
                with pe.Fori(2, turns) as q:
                    keys(ph, q, 0)
                    sum_equal(ph, q, -1)
                    keys(ph, q, 1)
                    sum_equal(ph, q, 0)
                sum_equal(ph, last_turn, 1)

            def turn(ph, k):
                after_loads(pe, ph, k)
                after(pe, "prescaled", ph, k)
                after(pe, "turned_out", ph, k.back(2))
                for a in range(A):
                    if ph in (L0, L2):
                        nc.tensor.transpose(sub(bank[k.two], a), sub(own[:, k.slot, :], a), ident[:, :])
                    last = nc.tensor.transpose(sub(bank[2 + k.two], a), sub(scaled[:, k.s3, :], a), ident[:, :])
                last.then_inc(stage["turned"], 1)

            def multiply(ph, k):
                after(pe, "turned_out", ph, k)
                if ph == L0:
                    after(pe, "relued", ph, k.back(2))
                else:
                    after(pe, "residual", ph, k.back(3 if ph in (CV1, CV2) else 2))
                into = product_bank(ph, k)
                w_sum = {L0: straight[:, 1, :], L2: weights_T[:, 8, :], CV1: straight[:, 2, :], CV2: straight[:, 3, :],
                         CV3: straight[:, 4, :]}[ph]
                w_own = {L0: straight[:, 0, :], L2: weights_T[:, 7, :]}.get(ph)
                for a in range(A):
                    nc.tensor.matmul(sub(into, a), ident[:, :], rows_bc[:, BIAS[ph], :], start=True, stop=False)
                    if w_own is not None:
                        nc.tensor.matmul(sub(into, a), sub(own_T[:, k.slot, :], a), w_own, start=False, stop=False)
                    last = nc.tensor.matmul(sub(into, a), sub(gT[:, k.s3, :], a), w_sum, start=False, stop=True)
                last.then_inc(stage["product"], 1)

            def column_sums(k):
                after(pe, "result", L0, k)
                w = inv_n[:, 1:2] if k.last() else inv_n[:, 0:1]
                for a in range(A):
                    last = nc.tensor.matmul(bank[6][:, 0:1], sub(result[:, k.s3, :], a), w,
                                            start=isinstance(k.b, int) and k.b == 0 and a == 0, stop=True,
                                            skip_group_check=True)
                last.then_inc(stage["summed"], 1)

            def dense(ph):
                def step(k):
                    if k.back(1).exists():
                        turn(ph, k.back(1))
                    if k.back(2).exists():
                        multiply(ph, k.back(2))
                    if ph == L0 and k.back(6).exists():
                        column_sums(k.back(6))

                steps(pe, step, FINAL[ph] + DEPTH)

            def dense_gru(k):
                if k.exists():
                    after_loads(pe, L1, k)
                    after(pe, "turned_out", L1, k.back(1))
                    for a in range(A):
                        nc.tensor.transpose(sub(bank[0], a), sub(own[:, k.slot, :], a), ident[:, :])
                        last = nc.tensor.transpose(sub(bank[1], a), sub(sm[:, k.s3, :], a), ident[:, :])
                    last.then_inc(stage["turned"], 1)
                j = k.back(6)
                if j.exists():
                    after(pe, "state", L1, j)
                    after(pe, "state_out", L1, j.back(1))
                    ahead = j.back(-3)
                    after(pe, "msg_out", L1, ahead if ahead.exists() else Blk(NB - 1, NB - 1, (NB - 1) // R))
                    for a in range(A):
                        last = nc.tensor.transpose(sub(bank[3], a), sub(kept[:, j.s3, :], a), ident[:, :])
                    last.then_inc(stage["state_turned"], 1)
                j = k.back(1)
                if j.exists():
                    after(pe, "turned_out", L1, j)
                    after(pe, "message", L1, j.back(1))
                    for a in range(A):
                        last = nc.tensor.matmul(sub(bank[2], a), sub(gT[:, j.s3, :], a), weights_T[:, 0, :],
                                                start=True, stop=True)
                    last.then_inc(stage["product"], 1)
                j = k.back(3)
                if j.exists():
                    after(pe, "msg_out", L1, j)
                    x_T, m_T = own_T[:, j.slot, :], u[:, j.s3, :]
                    after(pe, "reset", L1, j.back(1))
                    nc.tensor.matmul(bank[4][:, :], weights_T[:, 1, :], m_T, start=True, stop=False)
                    nc.tensor.matmul(bank[4][:, :], weights_T[:, 4, :], x_T, start=False, stop=True)
                    after(pe, "reset_hidden", L1, j.back(1))
                    nc.tensor.matmul(bank[5][:, :], weights_T[:, 6, :], x_T, start=True, stop=True
                                     ).then_inc(stage["gates_rh"], 1)
                    after(pe, "candidate_in", L1, j.back(1))
                    nc.tensor.matmul(bank[7][:, :], weights_T[:, 3, :], m_T, start=True, stop=True)
                    after(pe, "update", L1, j.back(1))
                    nc.tensor.matmul(bank[6][:, :], weights_T[:, 2, :], m_T, start=True, stop=False)
                    nc.tensor.matmul(bank[6][:, :], weights_T[:, 5, :], x_T, start=False, stop=True
                                     ).then_inc(stage["gates_zn"], 1)
                j = k.back(2)
                if j.exists():
                    after(pe, "message", L1, j)
                    after(pe, "state_out", L1, j.back(4))
                    for a in range(A):
                        last = nc.tensor.transpose(sub(bank[3], a), sub(scaled[:, j.s3, :], a), ident[:, :])
                    last.then_inc(stage["msg_turned"], 1)

            for ph in range(PHASES):
                aggregate(ph)
                if ph == L1:
                    pe.wait_ge(s_mean, 1)
                    for g in range(3):
                        last = nc.tensor.matmul(bank[7][:, g:g + 1], weights_T[:, 1 + g, :], mean_col[:, :], start=True,
                                                stop=True, skip_group_check=True)
                    last.then_inc(s_gate_mm, 1)
                    pe.wait_ge(s_gate_c, 1)
                    steps(pe, dense_gru, FINAL[ph] + DEPTH)
                else:
                    dense(ph)

        @block.scalar
        def _(act):
            act.wait_ge(s_weights_turned, 1)
            for i in range(3):
                n = min(4, 9 - 4 * i) * D
                last = nc.scalar.copy(weights_T[:, 4 * i:4 * i + n // D, :].rearrange("p i d -> p (i d)"), bank[4 + i][:, 0:n])
            last.then_inc(s_weights_out, 1)
            act.wait_ge(s_trips, 1)
            turns = act.value_load(trips[0:1, 0:1], min_val=3, max_val=MAXT)

            def group(ph, q, g, first=False):
                act.wait_ge(summed_eq[ph], q * 2 + (g + 1))
                if not first:
                    act.wait_ge(added[ph], q * (32 * C) + 16 * C * (g - 1))
                nc.scalar.copy(rows_sum[:, g, :, :].rearrange("p c d -> p (c d)"), bank[1 + g][:, :]).then_inc(rows_out[ph], 1)

            def aggregate(ph):
                group(ph, 0, 0, first=True)
                group(ph, 0, 1, first=True)
                with act.Fori(1, turns) as q:
                    group(ph, q, 0)
                    group(ph, q, 1)

            def turned_out(ph, k):
                after(act, "turned", ph, k)
                if ph in (L0, L2):
                    after(act, "product", ph, k.back(R))
                    nc.scalar.copy(own_T[:, k.slot, :], bank[k.two][:, :])
                after(act, "product", ph, k.back(S))
                nc.scalar.copy(gT[:, k.s3, :], bank[2 + k.two][:, :]).then_inc(stage["turned_out"], 1)

            def prescale(ph, k):
                after_loads(act, ph, k)
                after(act, "turned", ph, k.back(S))
                for a in range(A):
                    last = nc.scalar.activation(sub(scaled[:, k.s3, :], a), sub(sm[:, k.s3, :], a), ACT.Copy,
                                                scale=col(SCALE[ph], k, a))
                last.then_inc(stage["prescaled"], 1)

            def squares(ph, k):
                after(act, "product", ph, k)
                rows = product_bank(ph, k)
                if ph == L0:
                    after(act, "residual", ph, k.back(S))
                    nc.scalar.activation(r[:, k.s3, :], rows[:, :], ACT.Relu).then_inc(stage["relued"], 1)
                    after(act, "relued", ph, k)
                    rows = r[:, k.s3, :]
                for a in range(A):
                    last = nc.scalar.activation(junk_sq[:, k.s3, a, :], sub(rows, a), ACT.Square,
                                                accum_out=ss[:, k.slot, a:a + 1])
                last.then_inc(stage["squared"], 1)

            def gelu(ph, k):
                after(act, "residual", ph, k)
                after(act, "result", ph, k.back(S))
                nc.scalar.activation(r[:, k.s3, :], res[:, k.s3, :], ACT.Gelu).then_inc(stage["gelued"], 1)

            def dense(ph):
                def step(k):
                    if k.back(1).exists():
                        turned_out(ph, k.back(1))
                    if ph in NORM_EPS and k.back(3).exists():
                        squares(ph, k.back(3))
                    if ph in (CV1, CV2) and k.back(4).exists():
                        gelu(ph, k.back(4))
                    if ph in (L2, CV3) and k.exists():
                        prescale(ph, k)

                if ph in (CV1, CV2):
                    nc.scalar.preload_act_table(ACT.Gelu)
                steps(act, step, FINAL[ph] + DEPTH)

            def dense_gru(k):
                if k.exists():
                    after(act, "turned", L1, k)
                    after(act, "gates_zn", L1, k.back(R))
                    after(act, "old_less_new", L1, k.back(R))
                    nc.scalar.copy(own_T[:, k.slot, :], bank[0][:, :])
                    after(act, "product", L1, k.back(S))
                    nc.scalar.copy(gT[:, k.s3, :], bank[1][:, :]).then_inc(stage["turned_out"], 1)
                j = k.back(6)
                if j.exists():
                    after(act, "state_turned", L1, j)
                    after(act, "stats1", L1, j.back(S))
                    after(act, "normed1", L1, j.back(S))
                    nc.scalar.copy(state[:, j.s3, :], bank[3][:, :]).then_inc(stage["state_out"], 1)
                j = k.back(4)
                if j.exists():
                    after(act, "candidate_in", L1, j)
                    after(act, "state", L1, j.back(S))
                    nc.scalar.activation(new[:, j.s3, :], cand[:, j.s3, :], ACT.Tanh, bias=gate_c[:, 2:3]
                                         ).then_inc(stage["candidate"], 1)
                j = k.back(7)
                if j.exists():
                    after(act, "shifted1", L1, j)
                    after(act, "state_out", L1, j)
                    after(act, "result", L1, j.back(S))
                    for a in range(A):
                        last = nc.scalar.activation(sub(res[:, j.s3, :], a), sub(state[:, j.s3, :], a), ACT.Identity,
                                                    bias=nb_1[:, j.slot, a:a + 1], scale=rs_1[:, j.slot, a:a + 1])
                    last.then_inc(stage["normed1"], 1)
                j = k.back(3)
                if j.exists():
                    after(act, "gates_rh", L1, j)
                    after(act, "reset_hidden", L1, j.back(S))
                    nc.scalar.activation(r[:, j.s3, :], bank[4][:, :], ACT.Sigmoid, bias=gate_c[:, 0:1]
                                         ).then_inc(stage["reset"], 1)
                    after(act, "gates_zn", L1, j)
                    after(act, "kept", L1, j.back(S))
                    nc.scalar.activation(update[:, j.s3, :], bank[6][:, :], ACT.Sigmoid, bias=gate_c[:, 1:2]
                                         ).then_inc(stage["update"], 1)
                j = k.back(FINAL[L1] + 1)
                if j.exists():
                    after(act, "result", L1, j)
                    after_stores(act, L1, j.back(S))
                    for a in range(A):
                        last = nc.scalar.activation(sub(seed[:, j.s3, :], a), sub(result[:, j.s3, :], a), ACT.Copy,
                                                    scale=col(SEED[L1], j, a))
                    last.then_inc(stage["seeded"], 1)
                j = k.back(2)
                if j.exists():
                    after(act, "msg_turned", L1, j)
                    after(act, "gates_zn", L1, j.back(S))
                    nc.scalar.copy(u[:, j.s3, :], bank[3][:, :]).then_inc(stage["msg_out"], 1)

            for ph in range(PHASES):
                aggregate(ph)
                if ph == L1:
                    act.wait_ge(s_gate_c, 1)
                    nc.scalar.preload_act_table(ACT.Sigmoid)
                    steps(act, dense_gru, FINAL[ph] + DEPTH)
                else:
                    dense(ph)

        @block.vector
        def _(dve):
            done = [0]

            def link(ins):
                done[0] += 1
                ins.then_inc(s_dve, 1)
                dve.wait_ge(s_dve, done[0])

            V = nc.vector
            V.memset(row_n[:, :], 0.0)
            for i in range(2):
                V.memset(pack[i], FILL)
                V.memset(packed[i], FILL)
            V.memset(own_col, 0.0)
            link(V.memset(own_lane, -1.0))
            dve.wait_ge(s_edges, 32)
            ends_i, ends_f = (src_i, dst_i), (src_f, dst_f)
            for i in range(2):
                last = V.tensor_copy(ends_f[i][0:EP, :], ends_i[i][0:EP, :])
            link(last)
            link(V.tensor_tensor(differ[0:EP, :], src_f[0:EP, :], dst_f[0:EP, :], ALU.not_equal))
            V.reduce_sum(row_n[0:EP, :], differ[0:EP, :], AX.X).then_inc(s_row_n, 1)
            dve.wait_ge(s_row_turned, 1)
            link(V.reduce_max(trips_f[:, 0:1], bank[3][0:1, 0:P], AX.X))
            link(V.tensor_scalar(trips_f[:, 1:2], trips_f[:, 0:1], float(G2 - 1), float(3 * G2), ALU.add, ALU.max))
            link(V.tensor_copy(trips[:, 2:3], trips_f[:, 1:2]))
            link(V.tensor_scalar(trips[:, 0:1], trips[:, 2:3], G2.bit_length() - 1, None, ALU.logical_shift_right))
            V.tensor_scalar(trips[:, 1:2], trips[:, 0:1], -1.0, None, ALU.add).then_inc(s_trips, 1)
            dve.wait_ge(s_const, 1)
            link(V.tensor_scalar(place_f[0:EP, :], place_i[0:EP, :], 65536.0, -BIG, ALU.mult, ALU.add))
            for i in range(2):
                last = V.tensor_tensor(pack[i][0:EP, :], place_f[0:EP, :], ends_f[i][0:EP, :], ALU.add)
            link(last)
            for i in range(2):
                last = V.tensor_tensor(pack[i][0:EP, :], pack[i][0:EP, :], differ[0:EP, :], ALU.mult)
            link(last)
            link(V.tensor_scalar(place_f[0:EP, :], differ[0:EP, :], -FILL, FILL, ALU.mult, ALU.add))
            for i in range(2):
                last = V.tensor_tensor(pack[i][0:EP, :], pack[i][0:EP, :], place_f[0:EP, :], ALU.add)
            link(last)
            dve.wait_ge(s_trips, 1)
            turns = dve.value_load(trips[0:1, 0:1], min_val=3, max_val=MAXT)
            last_turn = dve.value_load(trips[0:1, 1:2], min_val=2, max_val=MAXT - 1)
            with dve.Fori(0, turns) as q:
                for i in range(2):
                    last = V.max(top8[:, i, :], pack[i])
                last.then_inc(s_top, 1)
                dve.wait_ge(s_top, q * 2 + 1)
                for i in range(2):
                    V.tensor_copy(packed[i][:, bass.ds(q * G2, G2)], top8[:, i, :])
                for i in range(2):
                    last = V.match_replace(pack[i], top8[:, i, :], pack[i], FILL)
                last.then_inc(s_top, 1)
                dve.wait_ge(s_top, q * 2 + 2)
                alone(dve)
            link(V.tensor_scalar(empty, packed[0], -BIG, None, ALU.is_lt))
            link(V.tensor_copy(trash_kf, trash_k[:, :]))
            link(V.tensor_tensor(empty, empty, trash_kf, ALU.mult))
            for i in range(2):
                last = V.tensor_copy(packed_i[i], packed[i])
            link(last)
            for i in range(2):
                last = V.tensor_scalar(gidx[:, 1 - i, :], packed_i[i], 0xFFFF, None, ALU.bitwise_and)
            link(last)
            for i in range(2):
                last = V.tensor_copy(packed[i], gidx[:, 1 - i, :])
            link(last)
            for i in range(2):
                last = V.tensor_tensor(key_f[:, i, :], packed[i], empty, ALU.add)
            link(last)

            def grid(lane, column, nodes, t1, t2, t3):
                V.tensor_scalar(t1, nodes, 2, P - 1, ALU.logical_shift_right, ALU.bitwise_and)
                V.tensor_scalar(t2, nodes, 9, 2, ALU.logical_shift_right, ALU.logical_shift_left)
                link(V.tensor_scalar(t3, nodes, A - 1, None, ALU.bitwise_and))
                V.tensor_copy(lane, t1)
                link(V.tensor_tensor(column, t2, t3, ALU.add))

            for i in range(2):
                link(V.tensor_copy(packed_i[i], key_f[:, i, :]))
                grid(key_lane[i], key_col[i], packed_i[i], *key_i)
            grid(own_lane[0:EP, :], own_col[0:EP, :], src_i[0:EP, :], *(t[0:EP, :] for t in own_i))
            link(V.tensor_scalar(place_f[0:EP, :], differ[0:EP, :], -1.0, 1.0, ALU.mult, ALU.add))
            link(V.tensor_tensor(own_lane[0:EP, :], own_lane[0:EP, :], place_f[0:EP, :], ALU.mult))
            link(V.tensor_tensor(own_lane[0:EP, :], own_lane[0:EP, :], differ[0:EP, :], ALU.subtract))

            def own_hot(j, slot, first=False):
                if not first:
                    dve.wait_ge(s_own_hist, j - (HOT - 1))
                V.tensor_scalar(hot_lane[:, slot, :], lane_f[:, :], own_lane[:, bass.ds(j, 1)], None, ALU.is_equal)
                V.tensor_scalar(hot_col[:, slot, :], col_f[:, :], own_col[:, bass.ds(j, 1)], None,
                                ALU.is_equal).then_inc(s_own_hot, 1)

            for j in range(HJ):
                own_hot(j, j % HOT, first=j < HOT)
            with dve.Fori(1, EJ // HJ) as q:
                for j in range(HJ):
                    own_hot(q * HJ + j, j % HOT)
            dve.wait_ge(s_own_hist, EJ)

            def key_hot(c, slot, first=False):
                if not first:
                    dve.wait_ge(s_key_hist, c - 1)
                for d in range(2):
                    V.tensor_scalar(hot_lane[:, 2 * slot + d, :], lane_f[:, :], key_lane[d][:, bass.ds(c, 1)], None, ALU.is_equal)
                    last = V.tensor_scalar(hot_col[:, 2 * slot + d, :], col_f[:, :], key_col[d][:, bass.ds(c, 1)], None,
                                           ALU.is_equal)
                last.then_inc(s_key_hot, 1)

            for c in range(G2):
                key_hot(c, c % 2, first=c < 2)
            with dve.Fori(1, turns) as q:
                for c in range(G2):
                    key_hot(q * G2 + c, c % 2)
            dve.wait_ge(s_key_hist, turns * G2)
            link(V.tensor_copy(hist[0], bank[0][:, 0:COLS]))
            V.tensor_tensor(hist[1], bank[1][:, 0:COLS], hist[0], ALU.add)
            link(V.tensor_tensor(hist[2], bank[2][:, 0:COLS], hist[0], ALU.add))
            on_grid = COLS - A
            V.tensor_copy(own_n[:, 0:on_grid], hist[0][:, 0:on_grid])
            V.tensor_copy(deg_s[:, 0:on_grid], hist[1][:, 0:on_grid])
            V.tensor_copy(deg_d[:, 0:on_grid], hist[2][:, 0:on_grid]).then_inc(s_hist_out, 1)
            dve.wait_ge(s_hist_out, 1)
            dve.wait_ge(s_shift, 96)
            V.tensor_scalar(own_n1[:, :], own_n[:, :], 1.0, None, ALU.add)
            V.tensor_scalar(deg_gcn[:, :], deg_d[:, :], 1.0, None, ALU.add).then_inc(s_nodes, 1)
            V.tensor_scalar(inv_s[:, :], deg_s[:, :], 1.0, None, ALU.max)
            link(V.tensor_scalar(inv_d[:, :], deg_d[:, :], 1.0, None, ALU.max))
            V.reciprocal(inv_s[:, :], inv_s[:, :])
            link(V.reciprocal(inv_d[:, :], inv_d[:, :]))
            dve.wait_ge(s_weights, 16 * 22)
            V.tensor_tensor(rows_bc[:, bl_, :], rows_bc[:, bl_, :], rows_bc[:, br_, :], ALU.add)
            link(V.tensor_tensor(rows_bc[:, bself_, :], rows_bc[:, bself_, :], rows_bc[:, bneigh_, :], ALU.add))
            V.memset(pass_mark_dve[:, :], 0.0).then_inc(s_biases, 1)

            def stage_in(ph, q, g, first=False):
                key = 0 if ph == L0 else 1
                at_ = bass.ds(q * G2 + g * C, C)
                if not first:
                    dve.wait_ge(landed[ph][g], q * (16 * C))
                V.tensor_copy(idx_now[:, g, :], gidx[:, key, at_])
                V.tensor_copy(key_now[:, g, :], key_f[:, key, at_]).then_inc(staged[ph], 1)

            def match(ph, q, g, first=False):
                room = g % 2
                dve.wait_ge(keys_turned[ph], q * 2 + (g + 1))
                if not first:
                    dve.wait_ge(summed_eq[ph], q * 2 + (g - 1))
                for c in range(C):
                    last = V.tensor_scalar(equal[:, room, c, :], bank[0][:, :], key_now[:, room, c:c + 1], None, ALU.is_equal)
                last.then_inc(matched[ph], 1)
                dve.wait_ge(matched[ph], q * 2 + (g + 1))
                for c in range(C):
                    n = (c + 1) * P
                    last = V.scalar_tensor_tensor(out=junk[:, c, 0:n], in0=equal[:, room, c, 0:n], scalar=1.0,
                                                  in1=earlier[:, c, 0:n], op0=ALU.mult, op1=ALU.mult,
                                                  accum_out=n_earlier[:, room, c:c + 1])
                last.then_inc(counted[ph], 1)
                V.tensor_tensor(pick[:, room, 0, :], trash_f[:, :], key_now[:, room, :], ALU.subtract)
                dve.wait_ge(counted[ph], q * 2 + (g + 1))
                V.tensor_scalar(pick[:, room, 1, :], n_earlier[:, room, :], 1.0, None, ALU.min).then_inc(picked[ph], 1)
                dve.wait_ge(picked[ph], q * 6 + (3 * g + 1))
                V.tensor_tensor(pick[:, room, 2, :], pick[:, room, 0, :], pick[:, room, 1, :], ALU.mult).then_inc(picked[ph], 1)
                dve.wait_ge(picked[ph], q * 6 + (3 * g + 2))
                V.tensor_tensor(pick[:, room, 0, :], pick[:, room, 2, :], key_now[:, room, :], ALU.add).then_inc(picked[ph], 1)
                dve.wait_ge(picked[ph], q * 6 + (3 * g + 3))
                if not first:
                    dve.wait_ge(added[ph], q * (32 * C) + 16 * C * (g - 1))
                V.tensor_copy(to_now[:, room, :], pick[:, room, 0, :]).then_inc(to_ready[ph], 1)

            def aggregate(ph):
                stage_in(ph, 0, 0, first=True)
                stage_in(ph, 0, 1, first=True)
                match(ph, 0, 0, first=True)
                stage_in(ph, 1, 0)
                match(ph, 1, -1, first=True)
                stage_in(ph, 1, 1)
                match(ph, 1, 0)
                with dve.Fori(2, turns) as q:
                    stage_in(ph, q, 0)
                    match(ph, q, -1)
                    stage_in(ph, q, 1)
                    match(ph, q, 0)
                match(ph, last_turn, 1)

            def row_stats(ph, k, rows, bn6, tag=""):
                for a in range(A):
                    last = V.bn_stats(bn6[:, k.slot, a, :], sub(rows, a))
                last.then_inc(stage["stats" + tag], 1)

            def mean_variance(ph, k, bn6, mv, tag=""):
                after(dve, "stats" + tag, ph, k)
                alone(dve)
                for a in range(A):
                    last = V.bn_aggr(mv[:, k.slot, a, :], bn6[:, k.slot, a, :])
                last.then_inc(stage["aggr" + tag], 1)

            def variance_eps(ph, k, mv, ve, tag=""):
                after(dve, "aggr" + tag, ph, k)
                V.tensor_scalar(ve[:, k.slot, :], mv[:, k.slot, :, 1], LN_EPS, None, ALU.add).then_inc(stage["var_eps" + tag], 1)

            def shift(ph, k, mv, rs, nb, tag=""):
                V.scalar_tensor_tensor(out=nb[:, k.slot, :], in0=mv[:, k.slot, :, 0], scalar=-1.0, in1=rs[:, k.slot, :],
                                       op0=ALU.mult, op1=ALU.mult).then_inc(stage["shifted" + tag], 1)

            def norm_eps(ph, k):
                after(dve, "norm", ph, k)
                V.tensor_scalar(nrm_e[:, k.slot, :], nrm[:, k.slot, :], NORM_EPS[ph], None, ALU.add).then_inc(stage["norm_eps"], 1)

            def norm_inv(ph, k):
                after(dve, "norm_eps", ph, k)
                V.reciprocal(nrm_inv[:, k.slot, :], nrm_e[:, k.slot, :]).then_inc(stage["norm_inv"], 1)

            def residual_scaled(ph, k):
                x_ = extra[:, k.slot, :] if ph == CV1 else own[:, k.slot, :]
                after(dve, "norm_inv", ph, k)
                if ph == L0:
                    after(dve, "squared", ph, k)
                    rows = r[:, k.s3, :]
                else:
                    after(dve, "product", ph, k)
                    after(dve, "gelued", ph, k.back(S))
                    rows = product_bank(ph, k)
                if ph == CV1:
                    after(dve, "own_ready", ph, k)
                    after_stores(dve, ph, k.back(S))
                for a in range(A):
                    last = V.scalar_tensor_tensor(out=sub(res[:, k.s3, :], a), in0=sub(rows, a),
                                                  scalar=nrm_inv[:, k.slot, a:a + 1], in1=sub(x_, a),
                                                  op0=ALU.mult, op1=ALU.add)
                last.then_inc(stage["residual"], 1)

            def residual(ph, k):
                after(dve, "product", ph, k)
                if ph == CV3:
                    after(dve, "own_ready", ph, k)
                x_ = extra[:, k.slot, :] if ph == CV3 else own[:, k.slot, :]
                V.tensor_tensor(res[:, k.s3, :], product_bank(ph, k)[:, :], x_, ALU.add).then_inc(stage["residual"], 1)

            def finish(ph, k):
                if ph in NORMED:
                    after(dve, "shifted", ph, k)
                else:
                    after(dve, "gelued", ph, k)
                if ph in SEED:
                    after(dve, "seeded", ph, k.back(S))
                if ph == L0:
                    after(dve, "summed", ph, k.back(S))
                after_stores(dve, ph, k.back(S))
                rs_ = (rsd if ph == L2 else rs)[:, k.slot, :]
                for a in range(A):
                    if ph in NORMED:
                        last = V.tensor_scalar(sub(result[:, k.s3, :], a), sub(res[:, k.s3, :], a), rs_[:, a:a + 1],
                                               nb[:, k.slot, a:a + 1], ALU.mult, ALU.add)
                    else:
                        last = V.tensor_scalar(sub(result[:, k.s3, :], a), sub(r[:, k.s3, :], a), col(dis, k, a), None, ALU.mult)
                last.then_inc(stage["result"], 1)

            def own_added(k):
                after_loads(dve, L0, k)
                for a in range(A):
                    last = V.scalar_tensor_tensor(out=sub(sm[:, k.s3, :], a), in0=sub(own[:, k.slot, :], a),
                                                  scalar=col(own_n, k, a), in1=sub(sm[:, k.s3, :], a),
                                                  op0=ALU.mult, op1=ALU.add)
                last.then_inc(stage["own_added"], 1)

            def prescale(ph, k):
                after_loads(dve, ph, k)
                after(dve, "turned", ph, k.back(S))
                for a in range(A):
                    last = V.tensor_scalar(sub(scaled[:, k.s3, :], a), sub(sm[:, k.s3, :], a), col(dis, k, a), None, ALU.mult)
                last.then_inc(stage["prescaled"], 1)

            def dense_normed(ph):
                end = FINAL[ph]

                def step(k):
                    if ph == L0 and k.back(end - 2).exists():
                        norm_eps(ph, k.back(end - 2))
                    if k.back(end - 1).exists():
                        mean_variance(ph, k.back(end - 1), bn6, mv)
                    if ph == L0 and k.back(end - 2).exists():
                        norm_inv(ph, k.back(end - 2))
                    j = k.back(end)
                    if j.exists():
                        after(dve, "rstd", ph, j)
                        if ph == L2:
                            V.tensor_tensor(rsd[:, j.slot, :], rs[:, j.slot, :], dis[:, bass.ds(j.b * A, A)],
                                            ALU.mult).then_inc(stage["rstd_dis"], 1)
                        else:
                            shift(ph, j, mv, rs, nb)
                    if k.back(end - 1).exists():
                        variance_eps(ph, k.back(end - 1), mv, ve)
                    if ph == L0 and k.exists():
                        own_added(k)
                    if ph == L2 and j.exists():
                        after(dve, "rstd_dis", ph, j)
                        shift(ph, j, mv, rsd, nb)
                    if k.back(end - 2).exists():
                        if ph == L0:
                            residual_scaled(ph, k.back(end - 2))
                        else:
                            residual(ph, k.back(end - 2))
                    if j.exists():
                        finish(ph, j)
                    if k.back(end - 2).exists():
                        after(dve, "residual", ph, k.back(end - 2))
                        row_stats(ph, k.back(end - 2), res[:, k.back(end - 2).s3, :], bn6)

                if ph == L2:
                    dve.wait_ge(s_roots, 1)
                steps(dve, step, end + DEPTH)

            def dense_gelu(ph):
                def step(k):
                    if k.back(4).exists():
                        norm_eps(ph, k.back(4))
                    if k.exists():
                        prescale(ph, k)
                    if k.back(4).exists():
                        norm_inv(ph, k.back(4))
                    if k.back(5).exists():
                        finish(ph, k.back(5))
                    if k.back(4).exists():
                        residual_scaled(ph, k.back(4))

                steps(dve, step, FINAL[ph] + DEPTH)

            def dense_gru(k):
                hidden, inner, outer, end = k.back(4), k.back(7), k.back(8), k.back(9)
                if hidden.exists():
                    j = hidden
                    after(dve, "gates_rh", L1, j)
                    after(dve, "reset", L1, j)
                    after(dve, "candidate", L1, j.back(S))
                    V.scalar_tensor_tensor(out=cand[:, j.s3, :], in0=bank[5][:, :], scalar=gate_b[:, 1, 2:3],
                                           in1=r[:, j.s3, :], op0=ALU.add, op1=ALU.mult).then_inc(stage["reset_hidden"], 1)
                if inner.exists():
                    mean_variance(L1, inner, bn6_1, mv_1, "1")
                if hidden.exists():
                    j = hidden
                    after(dve, "gates_zn", L1, j)
                    after(dve, "reset_hidden", L1, j)
                    V.tensor_tensor(cand[:, j.s3, :], cand[:, j.s3, :], bank[7][:, :], ALU.add).then_inc(stage["candidate_in"], 1)
                if inner.exists():
                    variance_eps(L1, inner, mv_1, ve_1, "1")
                if outer.exists():
                    j = outer
                    after(dve, "normed1", L1, j)
                    V.tensor_tensor(v3(res[:, j.s3, :]), v3(res[:, j.s3, :]), each(gamma_), ALU.mult).then_inc(stage["scaled1"], 1)
                j = k.back(1)
                if j.exists():
                    after(dve, "product", L1, j)
                    after(dve, "own_message", L1, j.back(S))
                    after(dve, "msg_turned", L1, j.back(S))
                    for a in range(A):
                        last = V.scalar_tensor_tensor(out=sub(scaled[:, j.s3, :], a), in0=rows_bc[:, bmsg_, :],
                                                      scalar=col(deg_d, j, a), in1=sub(bank[2], a), op0=ALU.mult, op1=ALU.add)
                    last.then_inc(stage["message"], 1)
                if outer.exists():
                    j = outer
                    after(dve, "scaled1", L1, j)
                    after(dve, "own_ready", L1, j)
                    V.tensor_tensor(res[:, j.s3, :], res[:, j.s3, :], extra[:, j.slot, :], ALU.add).then_inc(stage["residual"], 1)
                if end.exists():
                    after(dve, "rstd", L1, end)
                    shift(L1, end, mv, rs, nb)
                if inner.exists():
                    after(dve, "rstd1", L1, inner)
                    shift(L1, inner, mv_1, rs_1, nb_1, "1")
                if outer.exists():
                    after(dve, "residual", L1, outer)
                    row_stats(L1, outer, res[:, outer.s3, :], bn6)
                j = k.back(5)
                if j.exists():
                    after(dve, "kept", L1, j)
                    after(dve, "candidate", L1, j)
                    V.tensor_tensor(kept[:, j.s3, :], kept[:, j.s3, :], new[:, j.s3, :], ALU.add).then_inc(stage["state"], 1)
                if outer.exists():
                    mean_variance(L1, outer, bn6, mv)
                if end.exists():
                    finish(L1, end)
                if outer.exists():
                    variance_eps(L1, outer, mv, ve)
                j = k.back(6)
                if j.exists():
                    after(dve, "state_out", L1, j)
                    row_stats(L1, j, state[:, j.s3, :], bn6_1, "1")

            for ph in range(PHASES):
                if ph == L1:
                    dve.wait_ge(stage["summed"], NB)
                    V.tensor_copy(mean_col[:, :], bank[6][:, 0:1]).then_inc(s_mean, 1)
                aggregate(ph)
                if ph == L1:
                    dve.wait_ge(s_gate_mm, 1)
                    link(V.tensor_tensor(gate_c[:, :], bank[7][:, 0:3], gate_b[:, 0, :], ALU.add))
                    V.tensor_tensor(gate_c[:, 0:2], gate_c[:, 0:2], gate_b[:, 1, 0:2], ALU.add).then_inc(s_gate_c, 1)
                    steps(dve, dense_gru, FINAL[ph] + DEPTH)
                elif ph in NORMED:
                    dense_normed(ph)
                else:
                    dense_gelu(ph)


_INS = ['x', 'src', 'dst', 'L0_gnn_Wl', 'L0_gnn_bl', 'L0_gnn_Wr', 'L0_gnn_br', 'L1_gnn_W_msg', 'L1_gnn_b_msg',
        'L1_gnn_w_ih', 'L1_gnn_w_hh', 'L1_gnn_b_ih', 'L1_gnn_b_hh', 'L1_gnn_ln_gamma', 'L1_gnn_ln_beta',
        'L2_gnn_w_self', 'L2_gnn_b_self', 'L2_gnn_w_neigh', 'L2_gnn_b_neigh', 'L3_gnn_W1', 'L3_gnn_b1',
        'L3_gnn_W2', 'L3_gnn_b2', 'L3_gnn_W3', 'L3_gnn_b3']


def kernel(**inputs):
    import numpy as _np
    import concourse.bacc as _bacc
    from concourse import mybir as _mybir
    from concourse.bass_utils import run_bass_kernel_spmd as _run

    nc = _bacc.Bacc("TRN2", target_bir_lowering=False, num_devices=1)
    arrays, args = {}, []
    for name in _INS:
        a = _np.ascontiguousarray(inputs[name])
        arrays[f"in_{name}_dram"] = a
        args.append(nc.dram_tensor(f"in_{name}_dram", a.shape, _mybir.dt.from_np(a.dtype), kind="ExternalInput").ap())
    args.append(nc.dram_tensor("out_0_dram", (N, D), _mybir.dt.float32, kind="ExternalOutput").ap())
    build(nc, *args)
    r = _run(nc, [arrays], core_ids=[0])
    return r.results[0]["out_0_dram"]
```

```python
from contextlib import ExitStack

import concourse.bass as bass
from concourse import mybir

ALU = mybir.AluOpType
ACT = mybir.ActivationFunctionType
AX = mybir.AxisListType
F32 = mybir.dt.float32
F16 = mybir.dt.float16
BF16 = mybir.dt.bfloat16
I32 = mybir.dt.int32

P = 128
D = 128
N = 50000
E = 62500
A = 4
BLK = P * A
NB = -(-N // BLK)
LAST = N - BLK
SHIFT = ((NB - 1) * BLK - LAST) // A
COLS = NB * A
R = 6
S = 3

EP = 125
EJ = E // EP
C = 4
G2 = 2 * C
PR = 8
MAXR = -(-EJ // (2 * PR))
KP = MAXR * 2 * PR
MAXT = -(-E // (P * G2))
KC = MAXT * G2
TRASH = N
ZROWS = 6
ROWS = 396 * P
BIG = float(1 << 24)
FILL = -2.0 * BIG
HOT = 5
HJ = 25

L0, L1, L2, CV1, CV2, CV3 = range(6)
PHASES = 6

LN_EPS = 1e-5
NORM_EPS = {L0: 1e-6, CV1: 1e-8, CV2: 1e-8}

STAGES = {
    "own_added": (L0,),
    "prescaled": (L0, L2, CV1, CV2, CV3),
    "own_ready": (L1, L2, CV1, CV3),
    "turned": tuple(range(6)),
    "turned_out": tuple(range(6)),
    "product": tuple(range(6)),
    "relued": (L0,),
    "squared": (L0, CV1, CV2),
    "norm": (L0, CV1, CV2),
    "norm_eps": (L0, CV1, CV2),
    "norm_inv": (L0, CV1, CV2),
    "residual": tuple(range(6)),
    "stats": (L0, L1, L2, CV3),
    "aggr": (L0, L1, L2, CV3),
    "var_eps": (L0, L1, L2, CV3),
    "rstd": (L0, L1, L2, CV3),
    "rstd_dis": (L2,),
    "shifted": (L0, L1, L2, CV3),
    "gelued": (CV1, CV2),
    "result": tuple(range(6)),
    "seeded": (L0, L1, L2, CV1, CV2),
    "summed": (L0,),
    "message": (L1,),
    "own_message": (L1,),
    "msg_turned": (L1,),
    "msg_out": (L1,),
    "gates_rh": (L1,),
    "gates_zn": (L1,),
    "reset": (L1,),
    "update": (L1,),
    "reset_hidden": (L1,),
    "candidate_in": (L1,),
    "candidate": (L1,),
    "old_less_new": (L1,),
    "kept": (L1,),
    "state": (L1,),
    "state_turned": (L1,),
    "state_out": (L1,),
    "stats1": (L1,), "aggr1": (L1,), "var_eps1": (L1,),
    "rstd1": (L1,),
    "shifted1": (L1,), "scaled1": (L1,),
    "normed1": (L1,),
}


def base(stage, ph):
    return NB * sum(q < ph for q in STAGES[stage])


STORES = {L0: 2, L1: 2, L2: 2, CV1: 3, CV2: 2, CV3: 1}
NORMED = (L0, L1, L2, CV3)
FINAL = {L0: 6, L1: 9, L2: 5, CV1: 5, CV2: 5, CV3: 5}
DEPTH = 3


def stores_before(ph, slot):
    return 16 * sum(STORES[q] for q in range(ph)) * len(range(slot, NB, R))


def build(nc, x, src, dst, Wl, bl, Wr, br, W_msg, b_msg, w_ih, w_hh, b_ih, b_hh, gamma, beta,
          w_self, b_self, w_neigh, b_neigh, W1, b1, W2, b2, W3, b3, out):
    with ExitStack() as ctx:
        def sb(name, shape, dt=F32):
            return ctx.enter_context(nc.sbuf_tensor(name, shape, dt))

        def sem(name):
            return ctx.enter_context(nc.semaphore(name))

        def table(name, rows):
            return nc.dram_tensor(name, [rows, D], F32, kind="Internal").ap()

        x1, x2, y3, h1, y4, y5 = (table(n, N) for n in ("x1", "x2", "y3", "h1", "y4", "y5"))
        sums = [table("sum_even", ROWS), table("sum_odd", ROWS)]
        lists = nc.dram_tensor("lists", [P * KC + P * KP, 2], I32, kind="Internal").ap()
        OWN = [x, x1, x2, y3, h1, y3]
        SOURCE = [x, x1, x2, y3, y4, y5]
        RESULT = [x1, x2, y3, y4, y5, out]

        ident = sb("ident", [P, P])
        zeros = sb("zeros", [P, ZROWS * D])
        ones = sb("ones", [P, P])
        inv_n = sb("inv_n", [P, 2])
        powers = sb("powers", [P, 2, A])
        earlier = sb("earlier", [P, C, C * P])
        lane_f = sb("lane_f", [P, P], F16)
        col_f = sb("col_f", [P, COLS], F16)
        trash_f = sb("trash_f", [P, C])

        weights_T = sb("weights_T", [P, 9, D])
        straight = sb("straight", [P, 5, D])
        rows_bc = sb("rows_bc", [P, 10, D])
        bl_, br_, bmsg_, gamma_, beta_, bself_, bneigh_, bc1_, bc2_, bc3_ = range(10)
        gate_b = sb("gate_b", [P, 2, 3])
        gate_c = sb("gate_c", [P, 3])
        mean_col = sb("mean_col", [P, 1])
        BIAS = {L0: bl_, L2: bself_, CV1: bc1_, CV2: bc2_, CV3: bc3_}

        own_n = sb("own_n", [P, COLS])
        own_n1 = sb("own_n1", [P, COLS])
        deg_s = sb("deg_s", [P, COLS])
        deg_d = sb("deg_d", [P, COLS])
        inv_s = sb("inv_s", [P, COLS])
        inv_d = sb("inv_d", [P, COLS])
        dis = sb("dis", [P, COLS])
        dis_inv = sb("dis_inv", [P, COLS])
        deg_gcn = sb("deg_gcn", [P, COLS])
        SCALE = {L0: inv_s, L2: inv_d, CV1: dis, CV2: dis, CV3: dis}
        SEED = {L0: own_n, L1: own_n, L2: own_n1, CV1: own_n1, CV2: own_n1}

        key_f = sb("key_f", [P, 2, KC])
        gidx = sb("gidx", [P, 2, KC], I32)
        trips = sb("trips", [1, 6], I32)
        trips_f = sb("trips_f", [1, 4])
        deal_n = sb("deal_n", [P, 2])
        before = sb("before", [P, P])

        ROOMS = 3 * R + 13 * S
        arena = sb("arena", [P, ROOMS, BLK])
        at = [0]

        def ring(n):
            at[0] += n
            return arena[:, at[0] - n:at[0], :]

        own, own_T, extra = ring(R), ring(R), ring(R)
        sm, scaled, gT = ring(S), ring(S), ring(S)
        r, u, res = ring(S), ring(S), ring(S)
        result, seed, update = ring(S), ring(S), ring(S)
        new, kept, state, cand = ring(S), ring(S), ring(S), ring(S)
        first_u, first_new = 3 * R + 4 * S, 3 * R + 9 * S
        res_long = arena[:, first_u:first_u + R, :]
        result_long, seed_long = arena[:, first_new:first_new + R, :], arena[:, first_new + R:first_new + 2 * R, :]
        at[0] = 0

        def prep(k):
            at[0] += 1
            assert at[0] <= ROOMS
            return arena[:, at[0] - 1, 0:k]

        def prep2(k):
            at[0] += 2
            assert at[0] <= ROOMS
            return arena[:, at[0] - 2:at[0], :].rearrange("p a k -> p (a k)")[:, 0:k]

        raw = arena[:, ROOMS - 3:ROOMS, :].rearrange("p a k -> p (a k)")[:, 0:9 * D].rearrange("p (i d) -> p i d", d=D)
        src_i, dst_i = prep(EJ).bitcast(I32), prep(EJ).bitcast(I32)
        src_f, dst_f, differ, place_f = prep(EJ), prep(EJ), prep(EJ), prep(EJ)
        pack = [prep(EJ), prep(EJ)]
        packed = [prep(KP), prep(KP)]
        packed_i = [prep(KP).bitcast(I32), prep(KP).bitcast(I32)]
        empty, place_i = prep(KP), prep(KP).bitcast(I32)
        rank, rank_i, slot_i, lane_i = prep(KP), prep(KP).bitcast(I32), prep(KP).bitcast(I32), prep(KP).bitcast(I32)
        spare_i, spare_f = prep(KP).bitcast(I32), prep(KP)
        deal_to, deal_i = prep(KP), prep(KP).bitcast(I32)
        pairs = prep2(2 * KP).bitcast(I32).rearrange("p (k two) -> p k two", two=2)
        dealt = prep2(2 * KC).bitcast(I32).rearrange("p (k two) -> p k two", two=2)
        trash_k, trash_kf, empty_k = prep(KC).bitcast(I32), prep(KC), prep(KC)
        own_lane, own_col = prep(EJ), prep(EJ)
        own_i = [prep(EJ).bitcast(I32), prep(EJ).bitcast(I32), prep(EJ).bitcast(I32)]
        key_lane = [prep(KC), prep(KC)]
        key_col = [prep(KC), prep(KC)]
        key_i = [prep(KC).bitcast(I32) for _ in range(4)]
        hist = [prep(COLS), prep(COLS), prep(COLS)]
        top8 = sb("top8", [P, 2, PR])
        row_n = sb("row_n", [P, 1])
        hot_lane = sb("hot_lane", [P, HOT, P], F16)
        hot_col = sb("hot_col", [P, HOT, COLS], F16)
        deal_now = sb("deal_now", [P, 2, PR], I32)
        pairs_now = sb("pairs_now", [P, 2, PR, 2], I32)

        idx_now = sb("idx_now", [P, 2, C], I32)
        key_now = sb("key_now", [P, 2, C])
        to_now = sb("to_now", [P, 2, C], I32)
        rows_in = sb("rows_in", [P, 2, C, D])
        rows_sum = sb("rows_sum", [P, 2, C, D])
        equal = sb("equal", [P, 2, C, C * P])
        junk = sb("junk", [P, C, C * P], BF16)
        pass_mark = sb("pass_mark", [P, 1])
        pass_mark_dve = sb("pass_mark_dve", [P, 1])
        n_earlier = sb("n_earlier", [P, 2, C])
        pick = sb("pick", [P, 2, 3, C])

        ss = sb("ss", [P, R, A])
        nrm = sb("nrm", [P, R, A])
        nrm_e = sb("nrm_e", [P, R, A])
        nrm_inv = sb("nrm_inv", [P, R, A])
        bn6 = sb("bn6", [P, R, A, 6])
        mv = sb("mv", [P, R, A, 2])
        ve = sb("ve", [P, R, A])
        rs = sb("rs", [P, R, A])
        rsd = sb("rsd", [P, R, A])
        nb = sb("nb", [P, R, A])
        bn6_1 = sb("bn6_1", [P, R, A, 6])
        mv_1 = sb("mv_1", [P, R, A, 2])
        ve_1 = sb("ve_1", [P, R, A])
        rs_1 = sb("rs_1", [P, R, A])
        nb_1 = sb("nb_1", [P, R, A])
        junk_sq = sb("junk_sq", [P, S, A, D], BF16)

        bank = [ctx.enter_context(nc.psum_tensor(f"bank{i}", [P, BLK], F32)) for i in range(8)]

        stage = {n: sem(n) for n in STAGES}
        loaded = [sem(f"loaded{i}") for i in range(R)]
        stored = [sem(f"stored{i}") for i in range(R)]
        (s_edges, s_weights, s_zero_tile, s_zeroed, s_shift, s_const, s_dve, s_pool, s_row_n, s_row_turned, s_trips,
         s_weights_turned, s_weights_out, s_top, s_own_hot, s_own_hist, s_key_hot, s_key_hist, s_hist_out, s_nodes,
         s_roots, s_ranked, s_deal_staged, s_dealt0, s_dealt1, s_lists_empty, s_lists_full, s_lists_in, s_base, s_sqrt,
         s_biases, s_mean, s_gate_mm, s_gate_c, s_pass_done, s_alone) = (sem(n) for n in (
             "edges_loaded", "weights_loaded", "zero_tile", "sums_zeroed", "last_block_shifted", "constants",
             "dve_step", "pool_step", "rows_counted", "row_counts_turned", "trips_known", "weights_turned",
             "weights_out", "top8_step", "own_hot", "own_hist", "key_hot", "key_hist", "hist_out", "degrees",
             "roots", "edges_ranked", "deal_staged", "dealt0", "dealt1", "lists_empty", "lists_full", "lists_in", "row_starts",
             "square_roots", "biases", "mean_column", "gate_product", "gate_constants", "pass_done", "wait_alone"))
        staged, keys_turned, matched, picked, to_ready, summed_eq, rows_out, added = (
            [sem(f"{n}{ph}") for ph in range(PHASES)] for n in
            ("staged", "keys_turned", "matched", "picked", "to_ready",
             "summed_eq", "rows_out", "added"))

        class Blk:

            def __init__(self, b, slot, turn):
                self.b, self.slot, self.turn = b, slot % R, turn
                self.s3 = self.slot % S
                self.two = self.slot % 2

            def back(self, n):
                return Blk(self.b - n, self.slot - n, self.turn + (self.slot - n) // R)

            def exists(self):
                return not isinstance(self.b, int) or 0 <= self.b < NB

            def last(self):
                return isinstance(self.b, int) and self.b == NB - 1

        landed = [[sem(f"landed{ph}_{g}") for g in range(2)] for ph in range(PHASES)]

        def after(eng, name, ph, k):
            if k.exists():
                eng.wait_ge(stage[name], k.b + (base(name, ph) + 1))

        def after_stores(eng, ph, k):
            if k.exists():
                eng.wait_ge(stored[k.slot], (k.turn + 1) * (16 * STORES[ph]) + stores_before(ph, k.slot))

        def after_loads(eng, ph, k):
            eng.wait_ge(loaded[k.slot], (k.turn + 1) * 32 + 32 * ph * len(range(k.slot, NB, R)))

        def alone(eng):
            eng.sem_inc(s_alone, 1)

        def rows_of(t, k):
            first = LAST if k.last() else k.b * BLK
            return t[bass.ds(first, BLK), :].rearrange("(p a) d -> p (a d)", a=A)

        def col(t, k, a):
            return t[:, bass.ds(k.b * A + a, 1)]

        def cols(t, k):
            return t[:, bass.ds(k.b * A, A)].unsqueeze(2).to_broadcast([P, A, D])

        def each(i):
            return rows_bc[:, i, :].unsqueeze(1).to_broadcast([P, A, D])

        def sub(t, a):
            return t[:, a * D:(a + 1) * D]

        def v3(t):
            return t.rearrange("p (a d) -> p a d", a=A)

        def span(ph):
            return S if ph == L1 else R

        def res_of(ph, k):
            return res[:, k.s3, :] if ph == L1 else res_long[:, k.slot, :]

        def result_of(ph, k):
            return result[:, k.s3, :] if ph == L1 else result_long[:, k.slot, :]

        def seed_of(ph, k):
            return seed[:, k.s3, :] if ph == L1 else seed_long[:, k.slot, :]

        def product_bank(ph, k):
            return bank[4 + (k.s3 if ph in (CV1, CV2) else k.two)]

        def steps(eng, body, depth):
            first = -(-(depth + S) // R)
            whole = (NB - 2) // R
            for n in range(first * R):
                body(Blk(n, n, n // R))
            with eng.Fori(first, whole) as q:
                for slot in range(R):
                    body(Blk(q * R + slot, slot, q))
            for n in range(whole * R, NB + depth):
                body(Blk(n, n, n // R))

        block = ctx.enter_context(nc.Block())

        @block.sync
        def _(sp):
            sp.dma_start(src_i[0:EP, :], src.rearrange("(p j) -> p j", j=EJ)).then_inc(s_edges, 16)
            sp.dma_start(dst_i[0:EP, :], dst.rearrange("(p j) -> p j", j=EJ)).then_inc(s_edges, 16)
            sp.wait_ge(s_pool, 1)
            sp.dma_start(lists[0:P * KC, :].rearrange("(p k) two -> p (k two)", p=P),
                         dealt.rearrange("p k two -> p (k two)")
                         ).then_inc(s_lists_empty, 16)
            sp.dma_start(raw[:, 0, :], W_msg).then_inc(s_weights, 16)
            sp.dma_start(raw[:, 1:4, :], w_ih.rearrange("(g p) d -> p g d", p=P)).then_inc(s_weights, 16)
            sp.dma_start(raw[:, 4:7, :], w_hh.rearrange("(g p) d -> p g d", p=P)).then_inc(s_weights, 16)
            sp.dma_start(raw[:, 7, :], w_self).then_inc(s_weights, 16)
            sp.dma_start(raw[:, 8, :], w_neigh).then_inc(s_weights, 16)
            for i, w in enumerate((Wl, Wr, W1, W2, W3)):
                sp.dma_start(straight[:, i, :], w).then_inc(s_weights, 16)
            for i, v in enumerate((bl, br, b_msg, gamma, beta, b_self, b_neigh, b1, b2, b3)):
                sp.dma_start(rows_bc[:, i, :], v.rearrange("(o d) -> o d", o=1).to_broadcast([P, D])).then_inc(s_weights, 16)
            with nc.allow_non_contiguous_dma(reason="three numbers a partition, once"):
                sp.dma_start(gate_b[:, 0, :], b_ih.rearrange("(g p) -> p g", p=P)).then_inc(s_weights, 16)
                sp.dma_start(gate_b[:, 1, :], b_hh.rearrange("(g p) -> p g", p=P)).then_inc(s_weights, 16)
            sp.wait_ge(s_zero_tile, 1)
            sp.dma_start(sums[0].rearrange("(p c r) d -> p c (r d)", p=P, r=ZROWS),
                         zeros[:, :].unsqueeze(1).to_broadcast([P, ROWS // P // ZROWS, ZROWS * D])).then_inc(s_zeroed, 16)
            sp.dma_start(sums[1][TRASH:TRASH + BLK, :].rearrange("(p a) d -> p (a d)", a=A),
                         zeros[:, 0:A * D]).then_inc(s_zeroed, 16)
            sp.wait_ge(s_lists_full, 1)
            sp.dma_start(dealt.rearrange("p k two -> p (k two)"),
                         lists[0:P * KC, :].rearrange("(p k) two -> p (k two)", p=P)).then_inc(s_lists_in, 16)
            sp.wait_ge(s_hist_out, 1)
            for t, h in ((own_n, hist[0]), (deg_s, hist[1]), (deg_d, hist[2])):
                sp.dma_start(t[0:SHIFT, COLS - A:COLS], h[P - SHIFT:P, COLS - 2 * A:COLS - A]).then_inc(s_shift, 16)
                sp.dma_start(t[SHIFT:P, COLS - A:COLS], h[0:P - SHIFT, COLS - A:COLS]).then_inc(s_shift, 16)

            def load(ph, k):
                for name in {L0: ("residual",), L1: ("turned", "own_message"), L2: ("turned", "own_ready"),
                             CV1: ("own_ready",), CV2: ("residual",), CV3: ("own_ready",)}[ph]:
                    after(sp, name, ph, k.back(R))
                    alone(sp)
                sp.dma_start(own[:, k.slot, :], rows_of(OWN[ph], k)).then_inc(loaded[k.slot], 16)
                after(sp, "turned" if ph == L1 else "prescaled", ph, k.back(S))
                alone(sp)
                sp.dma_start(sm[:, k.s3, :], rows_of(sums[ph % 2], k)).then_inc(loaded[k.slot], 16)

            def store_h1(k):
                after(sp, "residual", CV1, k)
                alone(sp)
                sp.dma_start(rows_of(h1, k), res_of(CV1, k)).then_inc(stored[k.slot], 16)

            def store_result(ph, k):
                if k.last():
                    after_stores(sp, ph, k.back(1))
                    if ph == CV1:
                        store_h1(k)
                after(sp, "result", ph, k)
                alone(sp)
                sp.dma_start(rows_of(RESULT[ph], k), result_of(ph, k)).then_inc(stored[k.slot], 16)

            def store_seed(ph, k):
                after(sp, "seeded", ph, k)
                alone(sp)
                sp.dma_start(rows_of(sums[(ph + 1) % 2], k), seed_of(ph, k)).then_inc(stored[k.slot], 16)

            def dense(ph):
                sp.wait_ge(s_pass_done, ph + 1)
                if ph == L0:
                    sp.wait_ge(s_roots, 1)
                load(ph, Blk(0, 0, 0))

                def step(k):
                    if not isinstance(k.b, int) or k.b + 1 < NB:
                        load(ph, k.back(-1))
                    if ph in SEED and k.back(FINAL[ph] + 2).exists():
                        store_seed(ph, k.back(FINAL[ph] + 2))
                    if k.back(FINAL[ph] + 1).exists():
                        store_result(ph, k.back(FINAL[ph] + 1))
                    if ph == CV1 and k.back(FINAL[ph]).exists() and not k.back(FINAL[ph]).last():
                        store_h1(k.back(FINAL[ph]))

                steps(sp, step, FINAL[ph] + DEPTH)

            for ph in range(PHASES):
                dense(ph)
            for slot in range(R):
                sp.wait_ge(stored[slot], stores_before(PHASES, slot))

        @block.gpsimd
        def _(pool):
            pool.memset(zeros[:, :], 0.0).then_inc(s_zero_tile, 1)
            pool.memset(ones[:, :], 1.0)
            pool.memset(ident[:, :], 0.0)
            pool.memset(earlier[:, :, :], 0.0)
            pool.memset(inv_n[:, :], 1.0 / N)
            pool.memset(powers[:, 0, :], -0.5)
            pool.memset(powers[:, 1, :], 0.5)
            pool.iota(lane_f[:, :], [[1, P]], base=0, channel_multiplier=0, allow_small_or_imprecise_dtypes=True)
            pool.iota(col_f[:, :], [[1, COLS]], base=0, channel_multiplier=0, allow_small_or_imprecise_dtypes=True)
            pool.iota(place_i[:, :], [[1, KP]], base=0, channel_multiplier=0)
            pool.iota(spare_i[:, :], [[1, KP]], base=P * KC, channel_multiplier=KP)
            pool.memset(dealt, -1)
            pool.iota(trash_k[:, :], [[0, KC // C], [P, C]], base=TRASH, channel_multiplier=1).then_inc(s_pool, 1)
            pool.wait_ge(s_pool, 1)
            pool.affine_select(out=ident[:, :], in_=ident[:, :], compare_op=ALU.not_equal, fill=1.0, base=0,
                               pattern=[[-1, P]], channel_multiplier=1)
            pool.affine_select(out=inv_n[:, 1:2], in_=inv_n[:, 1:2], compare_op=ALU.is_ge, fill=0.0, base=-SHIFT,
                               pattern=[[0, 1]], channel_multiplier=1)
            pool.affine_select(out=before[:, :], in_=ones[:, :], compare_op=ALU.is_ge, fill=0.0, base=-1,
                               pattern=[[1, P]], channel_multiplier=-1)
            for c in range(C):
                if c:
                    pool.memset(earlier[:, c, 0:c * P], 1.0)
                pool.affine_select(out=earlier[:, c, c * P:(c + 1) * P], in_=ones[:, :], compare_op=ALU.is_ge, fill=0.0,
                                   base=-1, pattern=[[-1, P]], channel_multiplier=1)
            pool.tensor_copy(trash_f[:, :], trash_k[:, 0:C]).then_inc(s_const, 1)
            pool.wait_ge(s_trips, 1)
            deals = pool.value_load(trips[0:1, 0:1], min_val=2, max_val=MAXR)
            turns = pool.value_load(trips[0:1, 1:2], min_val=3, max_val=MAXT)
            last_turn = pool.value_load(trips[0:1, 2:3], min_val=2, max_val=MAXT - 1)
            s_dealt = (s_dealt0, s_dealt1)
            pool.wait_ge(s_lists_empty, 16)
            pool.wait_ge(s_ranked, 1)

            def deal(q, g, first=False):
                if not first:
                    pool.wait_ge(s_dealt[g], q * (16 * PR))
                    alone(pool)
                at_ = bass.ds(q * (2 * PR) + g * PR, PR)
                pool.tensor_copy(deal_now[:, g, :], deal_i[:, at_])
                pool.tensor_copy(pairs_now[:, g, :, :], pairs[:, at_, :]).then_inc(s_deal_staged, 1)
                pool.wait_ge(s_deal_staged, q * 2 + (g + 1))
                alone(pool)
                for j in range(PR):
                    pool.indirect_dma_start(lists, bass.IndirectOffsetOnAxis(ap=deal_now[:, g, j:j + 1], axis=0),
                                            pairs_now[:, g, j, :], None).then_inc(s_dealt[g], 16)

            deal(0, 0, first=True)
            deal(0, 1, first=True)
            with pool.Fori(1, deals) as q:
                deal(q, 0)
                deal(q, 1)
            for g in range(2):
                pool.wait_ge(s_dealt[g], deals * (16 * PR))
                alone(pool)
            pool.memset(pass_mark[:, :], 0.0).then_inc(s_lists_full, 1)

            def gather(ph, q, g):
                pool.wait_ge(staged[ph], q * 2 + (g + 1))
                alone(pool)
                if not (isinstance(q, int) and q == 0):
                    pool.wait_ge(summed_eq[ph], q * 2 + (g - 1))
                    alone(pool)
                for c in range(C):
                    pool.indirect_dma_start(rows_in[:, g, c, :], None, SOURCE[ph],
                                            bass.IndirectOffsetOnAxis(ap=idx_now[:, g, c:c + 1], axis=0)
                                            ).then_inc(landed[ph][g], 16)

            def add(ph, q, g, first=False):
                room = g % 2
                pool.wait_ge(rows_out[ph], q * 2 + (g + 1))
                alone(pool)
                pool.wait_ge(to_ready[ph], q * 2 + (g + 1))
                alone(pool)
                if not first:
                    pool.wait_ge(added[ph], q * (32 * C) + 16 * C * g)
                    alone(pool)
                for c in range(C):
                    pool.indirect_dma_start(sums[ph % 2], bass.IndirectOffsetOnAxis(ap=to_now[:, room, c:c + 1], axis=0),
                                            rows_sum[:, room, c, :], None, compute_op=ALU.add).then_inc(added[ph], 16)

            def aggregate(ph):
                if ph == L0:
                    pool.wait_ge(s_zeroed, 32)
                else:
                    for slot in range(R):
                        pool.wait_ge(stored[slot], stores_before(ph, slot))
                gather(ph, 0, 0)
                gather(ph, 0, 1)
                add(ph, 0, 0, first=True)
                with pool.Fori(1, turns) as q:
                    gather(ph, q, 0)
                    add(ph, q, -1)
                    gather(ph, q, 1)
                    add(ph, q, 0)
                add(ph, last_turn, 1)
                pool.wait_ge(added[ph], turns * (32 * C))
                alone(pool)
                pool.memset(pass_mark[:, :], 0.0).then_inc(s_pass_done, 1)

            def power(ph, k, out_, in_, i, needs, gives):
                after(pool, needs, ph, k)
                pool.tensor_tensor(out_[:, k.slot, :], in_[:, k.slot, :], powers[:, i, :], ALU.pow).then_inc(stage[gives], 1)

            def prescale(k):
                after(pool, "own_added", L0, k)
                after(pool, "turned", L0, k.back(S))
                pool.tensor_tensor(v3(scaled[:, k.s3, :]), v3(sm[:, k.s3, :]), cols(SCALE[L0], k),
                                   ALU.mult).then_inc(stage["prescaled"], 1)

            def operand(ph, k):
                after_loads(pool, ph, k)
                after(pool, "residual", ph, k.back(R))
                if ph == L2:
                    pool.tensor_tensor(v3(extra[:, k.slot, :]), v3(own[:, k.slot, :]), each(BIAS[L2]),
                                       ALU.add).then_inc(stage["own_ready"], 1)
                    return
                pool.tensor_tensor(v3(extra[:, k.slot, :]), v3(own[:, k.slot, :]), cols(dis_inv, k),
                                   ALU.mult).then_inc(stage["own_ready"], 1)

            def seeds(ph, k):
                after(pool, "result", ph, k)
                pool.tensor_tensor(v3(seed_of(ph, k)), v3(result_of(ph, k)), cols(SEED[ph], k),
                                   ALU.mult).then_inc(stage["seeded"], 1)

            def dense(ph):
                def step(k):
                    j = k.back(FINAL[ph] - 1)
                    if ph in NORMED and j.exists():
                        power(ph, j, rs, ve, 0, "var_eps", "rstd")
                    if k.exists():
                        if ph == L0:
                            prescale(k)
                        if ph in (L2, CV1, CV3):
                            operand(ph, k)
                    if ph == L0 and k.back(3).exists():
                        power(ph, k.back(3), nrm, ss, 1, "squared", "norm")
                    if ph in SEED and k.back(FINAL[ph] + 1).exists():
                        seeds(ph, k.back(FINAL[ph] + 1))
                    if ph in (CV1, CV2) and k.back(3).exists():
                        power(ph, k.back(3), nrm, ss, 1, "squared", "norm")

                steps(pool, step, FINAL[ph] + DEPTH)

            def dense_gru(k):
                if k.back(7).exists():
                    power(L1, k.back(7), rs_1, ve_1, 0, "var_eps1", "rstd1")
                j = k.back(3)
                if j.exists():
                    after(pool, "message", L1, j)
                    after(pool, "residual", L1, j.back(R))
                    pool.tensor_tensor(extra[:, j.slot, :], own[:, j.slot, :], scaled[:, j.s3, :],
                                       ALU.add).then_inc(stage["own_message"], 1)
                    after(pool, "own_message", L1, j)
                    pool.tensor_tensor(v3(extra[:, j.slot, :]), v3(extra[:, j.slot, :]), each(beta_),
                                       ALU.add).then_inc(stage["own_ready"], 1)
                j = k.back(4)
                if j.exists():
                    after(pool, "candidate", L1, j)
                    after(pool, "state_turned", L1, j.back(S))
                    pool.tensor_tensor(kept[:, j.s3, :], own_T[:, j.slot, :], new[:, j.s3, :],
                                       ALU.subtract).then_inc(stage["old_less_new"], 1)
                    after(pool, "old_less_new", L1, j)
                    pool.tensor_tensor(kept[:, j.s3, :], kept[:, j.s3, :], update[:, j.s3, :],
                                       ALU.mult).then_inc(stage["kept"], 1)
                if k.back(8).exists():
                    power(L1, k.back(8), rs, ve, 0, "var_eps", "rstd")

            for ph in range(PHASES):
                aggregate(ph)
                if ph == L0:
                    pool.wait_ge(s_roots, 1)
                if ph == L1:
                    steps(pool, dense_gru, FINAL[ph] + DEPTH)
                else:
                    dense(ph)

        @block.tensor
        def _(pe):
            pe.wait_ge(s_const, 1)
            pe.wait_ge(s_row_n, 1)
            nc.tensor.transpose(bank[3][0:1, 0:P], row_n[:, :], ident[:, :]).then_inc(s_row_turned, 1)
            nc.tensor.matmul(bank[7][:, 0:1], before[:, :], row_n[:, :], start=True, stop=True, skip_group_check=True)
            nc.tensor.matmul(bank[7][:, 1:2], ones[:, :], row_n[:, :], start=True, stop=True,
                             skip_group_check=True).then_inc(s_base, 1)
            pe.wait_ge(s_weights, 16 * 22)
            for i in range(9):
                last = nc.tensor.transpose(bank[4 + i // 4][:, i % 4 * D:(i % 4 + 1) * D], raw[:, i, :], ident[:, :])
            last.then_inc(s_weights_turned, 1)

            def own_hist(j, slot, first=False):
                pe.wait_ge(s_own_hot, j + 1)
                nc.tensor.matmul(bank[3][:, 0:COLS], hot_lane[:, slot, :], hot_col[:, slot, :], start=first, stop=True,
                                 skip_group_check=True).then_inc(s_own_hist, 1)

            pe.wait_ge(s_trips, 1)
            for j in range(HJ):
                own_hist(j, j % HOT, first=j == 0)
            with pe.Fori(1, EJ // HJ) as q:
                for j in range(HJ):
                    own_hist(q * HJ + j, j % HOT)

            def key_hist(c, slot, first=False):
                pe.wait_ge(s_key_hot, c + 1)
                for d in range(2):
                    last = nc.tensor.matmul(bank[4 + d][:, 0:COLS], hot_lane[:, 2 * slot + d, :], hot_col[:, 2 * slot + d, :],
                                            start=first, stop=True, skip_group_check=True)
                last.then_inc(s_key_hist, 1)

            turns = pe.value_load(trips[0:1, 1:2], min_val=3, max_val=MAXT)
            last_turn = pe.value_load(trips[0:1, 2:3], min_val=2, max_val=MAXT - 1)
            pe.wait_ge(s_weights_out, 1)

            def keys(ph, q, g, first=False):
                pe.wait_ge(staged[ph], q * 2 + (g + 1))
                if not first:
                    pe.wait_ge(matched[ph], q * 2 + g)
                for c in range(C):
                    last = nc.tensor.transpose(sub(bank[0], c), key_now[:, g, c:c + 1].to_broadcast([P, P]), ident[:, :])
                last.then_inc(keys_turned[ph], 1)

            def sum_equal(ph, q, g, first=False):
                room = g % 2
                pe.wait_ge(matched[ph], q * 2 + (g + 1))
                pe.wait_ge(landed[ph][room], q * (16 * C) + (16 * C if g >= 0 else 0))
                if not first:
                    pe.wait_ge(rows_out[ph], q * 2 + (g - 1))
                for c in range(C):
                    for e in range(C):
                        last = nc.tensor.matmul(sub(bank[1 + room], c), equal[:, room, e, c * P:(c + 1) * P],
                                                rows_in[:, room, e, :], start=e == 0, stop=e == C - 1)
                last.then_inc(summed_eq[ph], 1)

            def count_keys(ph, q, g, first=False):
                if ph == L0:
                    for c in range(C):
                        key_hist(q * G2 + (g * C + c), c % 2, first=first and c == 0)

            def aggregate(ph):
                keys(ph, 0, 0, first=True)
                keys(ph, 0, 1)
                count_keys(ph, 0, 0, first=True)
                count_keys(ph, 0, 1)
                sum_equal(ph, 0, 0, first=True)
                keys(ph, 1, 0)
                count_keys(ph, 1, 0)
                sum_equal(ph, 1, -1, first=True)
                keys(ph, 1, 1)
                count_keys(ph, 1, 1)
                sum_equal(ph, 1, 0)
                with pe.Fori(2, turns) as q:
                    keys(ph, q, 0)
                    count_keys(ph, q, 0)
                    sum_equal(ph, q, -1)
                    keys(ph, q, 1)
                    count_keys(ph, q, 1)
                    sum_equal(ph, q, 0)
                sum_equal(ph, last_turn, 1)

            def turn(ph, k):
                after(pe, "prescaled", ph, k)
                after(pe, "turned_out", ph, k.back(2))
                for a in range(A):
                    if ph in (L0, L2):
                        nc.tensor.transpose(sub(bank[k.two], a), sub(own[:, k.slot, :], a), ident[:, :])
                    last = nc.tensor.transpose(sub(bank[2 + k.two], a), sub(scaled[:, k.s3, :], a), ident[:, :])
                last.then_inc(stage["turned"], 1)

            def multiply(ph, k):
                after(pe, "turned_out", ph, k)
                if ph == L0:
                    after(pe, "relued", ph, k.back(2))
                else:
                    after(pe, "residual", ph, k.back(3 if ph in (CV1, CV2) else 2))
                into = product_bank(ph, k)
                w_sum = {L0: straight[:, 1, :], L2: weights_T[:, 8, :], CV1: straight[:, 2, :], CV2: straight[:, 3, :],
                         CV3: straight[:, 4, :]}[ph]
                w_own = {L0: straight[:, 0, :], L2: weights_T[:, 7, :]}.get(ph)
                for a in range(A):
                    if ph != L2:
                        nc.tensor.matmul(sub(into, a), ident[:, :], rows_bc[:, BIAS[ph], :], start=True, stop=False)
                    if w_own is not None:
                        nc.tensor.matmul(sub(into, a), sub(own_T[:, k.slot, :], a), w_own, start=ph == L2, stop=False)
                    last = nc.tensor.matmul(sub(into, a), sub(gT[:, k.s3, :], a), w_sum, start=False, stop=True)
                last.then_inc(stage["product"], 1)

            def column_sums(k):
                after(pe, "result", L0, k)
                w = inv_n[:, 1:2] if k.last() else inv_n[:, 0:1]
                for a in range(A):
                    last = nc.tensor.matmul(bank[6][:, 0:1], sub(result_of(L0, k), a), w,
                                            start=isinstance(k.b, int) and k.b == 0 and a == 0, stop=True,
                                            skip_group_check=True)
                last.then_inc(stage["summed"], 1)

            def dense(ph):
                def step(k):
                    if k.back(1).exists():
                        turn(ph, k.back(1))
                    if k.back(2).exists():
                        multiply(ph, k.back(2))
                    if ph == L0 and k.back(6).exists():
                        column_sums(k.back(6))

                steps(pe, step, FINAL[ph] + DEPTH)

            def dense_gru(k):
                if k.exists():
                    after_loads(pe, L1, k)
                    after(pe, "turned_out", L1, k.back(1))
                    for a in range(A):
                        nc.tensor.transpose(sub(bank[0], a), sub(own[:, k.slot, :], a), ident[:, :])
                        last = nc.tensor.transpose(sub(bank[1], a), sub(sm[:, k.s3, :], a), ident[:, :])
                    last.then_inc(stage["turned"], 1)
                j = k.back(6)
                if j.exists():
                    after(pe, "state", L1, j)
                    after(pe, "state_out", L1, j.back(1))
                    ahead = j.back(-3)
                    after(pe, "msg_out", L1, ahead if ahead.exists() else Blk(NB - 1, NB - 1, (NB - 1) // R))
                    for a in range(A):
                        last = nc.tensor.transpose(sub(bank[3], a), sub(kept[:, j.s3, :], a), ident[:, :])
                    last.then_inc(stage["state_turned"], 1)
                j = k.back(1)
                if j.exists():
                    after(pe, "turned_out", L1, j)
                    after(pe, "message", L1, j.back(1))
                    for a in range(A):
                        last = nc.tensor.matmul(sub(bank[2], a), sub(gT[:, j.s3, :], a), weights_T[:, 0, :],
                                                start=True, stop=True)
                    last.then_inc(stage["product"], 1)
                j = k.back(3)
                if j.exists():
                    after(pe, "msg_out", L1, j)
                    x_T, m_T = own_T[:, j.slot, :], u[:, j.s3, :]
                    after(pe, "reset", L1, j.back(1))
                    nc.tensor.matmul(bank[4][:, :], weights_T[:, 1, :], m_T, start=True, stop=False)
                    nc.tensor.matmul(bank[4][:, :], weights_T[:, 4, :], x_T, start=False, stop=True)
                    after(pe, "reset_hidden", L1, j.back(1))
                    nc.tensor.matmul(bank[5][:, :], weights_T[:, 6, :], x_T, start=True, stop=True
                                     ).then_inc(stage["gates_rh"], 1)
                    after(pe, "candidate_in", L1, j.back(1))
                    nc.tensor.matmul(bank[7][:, :], weights_T[:, 3, :], m_T, start=True, stop=True)
                    after(pe, "update", L1, j.back(1))
                    nc.tensor.matmul(bank[6][:, :], weights_T[:, 2, :], m_T, start=True, stop=False)
                    nc.tensor.matmul(bank[6][:, :], weights_T[:, 5, :], x_T, start=False, stop=True
                                     ).then_inc(stage["gates_zn"], 1)
                j = k.back(2)
                if j.exists():
                    after(pe, "message", L1, j)
                    after(pe, "state_out", L1, j.back(4))
                    for a in range(A):
                        last = nc.tensor.transpose(sub(bank[3], a), sub(scaled[:, j.s3, :], a), ident[:, :])
                    last.then_inc(stage["msg_turned"], 1)

            for ph in range(PHASES):
                aggregate(ph)
                if ph == L1:
                    pe.wait_ge(s_mean, 1)
                    for g in range(3):
                        last = nc.tensor.matmul(bank[7][:, g:g + 1], weights_T[:, 1 + g, :], mean_col[:, :], start=True,
                                                stop=True, skip_group_check=True)
                    last.then_inc(s_gate_mm, 1)
                    pe.wait_ge(s_gate_c, 1)
                    steps(pe, dense_gru, FINAL[ph] + DEPTH)
                else:
                    dense(ph)

        @block.scalar
        def _(act):
            act.wait_ge(s_weights_turned, 1)
            for i in range(3):
                n = min(4, 9 - 4 * i) * D
                last = nc.scalar.copy(weights_T[:, 4 * i:4 * i + n // D, :].rearrange("p i d -> p (i d)"), bank[4 + i][:, 0:n])
            last.then_inc(s_weights_out, 1)
            act.wait_ge(s_trips, 1)
            turns = act.value_load(trips[0:1, 1:2], min_val=3, max_val=MAXT)

            def group(ph, q, g, first=False):
                act.wait_ge(summed_eq[ph], q * 2 + (g + 1))
                if not first:
                    act.wait_ge(added[ph], q * (32 * C) + 16 * C * (g - 1))
                nc.scalar.copy(rows_sum[:, g, :, :].rearrange("p c d -> p (c d)"), bank[1 + g][:, :]).then_inc(rows_out[ph], 1)

            def aggregate(ph):
                group(ph, 0, 0, first=True)
                group(ph, 0, 1, first=True)
                with act.Fori(1, turns) as q:
                    group(ph, q, 0)
                    group(ph, q, 1)

            def turned_out(ph, k):
                after(act, "turned", ph, k)
                after(act, "product", ph, k.back(S))
                if ph in (L0, L2):
                    nc.scalar.copy(own_T[:, k.slot, :], bank[k.two][:, :])
                nc.scalar.copy(gT[:, k.s3, :], bank[2 + k.two][:, :]).then_inc(stage["turned_out"], 1)

            def prescale(ph, k):
                after_loads(act, ph, k)
                after(act, "turned", ph, k.back(S))
                for a in range(A):
                    last = nc.scalar.activation(sub(scaled[:, k.s3, :], a), sub(sm[:, k.s3, :], a), ACT.Copy,
                                                scale=col(SCALE[ph], k, a))
                last.then_inc(stage["prescaled"], 1)

            def squares(ph, k):
                after(act, "product", ph, k)
                rows = product_bank(ph, k)
                if ph == L0:
                    after(act, "residual", ph, k.back(S))
                    nc.scalar.activation(r[:, k.s3, :], rows[:, :], ACT.Relu).then_inc(stage["relued"], 1)
                    after(act, "relued", ph, k)
                    rows = r[:, k.s3, :]
                for a in range(A):
                    last = nc.scalar.activation(junk_sq[:, k.s3, a, :], sub(rows, a), ACT.Square,
                                                accum_out=ss[:, k.slot, a:a + 1])
                last.then_inc(stage["squared"], 1)

            def gelu(ph, k):
                after(act, "residual", ph, k)
                after(act, "result", ph, k.back(S))
                nc.scalar.activation(r[:, k.s3, :], res_of(ph, k), ACT.Gelu).then_inc(stage["gelued"], 1)

            def dense(ph):
                def step(k):
                    if ph == L0 and k.back(3).exists():
                        squares(ph, k.back(3))
                    if k.back(1).exists():
                        turned_out(ph, k.back(1))
                    if ph in (CV1, CV2) and k.back(3).exists():
                        squares(ph, k.back(3))
                    if ph in (CV1, CV2) and k.back(4).exists():
                        gelu(ph, k.back(4))
                    if ph in (L2, CV3) and k.exists():
                        prescale(ph, k)

                if ph in (CV1, CV2):
                    nc.scalar.preload_act_table(ACT.Gelu)
                steps(act, step, FINAL[ph] + DEPTH)

            def dense_gru(k):
                if k.exists():
                    after(act, "turned", L1, k)
                    after(act, "old_less_new", L1, k.back(R))
                    nc.scalar.copy(own_T[:, k.slot, :], bank[0][:, :])
                    after(act, "product", L1, k.back(S))
                    nc.scalar.copy(gT[:, k.s3, :], bank[1][:, :]).then_inc(stage["turned_out"], 1)
                j = k.back(6)
                if j.exists():
                    after(act, "state_turned", L1, j)
                    after(act, "stats1", L1, j.back(S))
                    after(act, "normed1", L1, j.back(S))
                    nc.scalar.copy(state[:, j.s3, :], bank[3][:, :]).then_inc(stage["state_out"], 1)
                j = k.back(4)
                if j.exists():
                    after(act, "candidate_in", L1, j)
                    after(act, "state", L1, j.back(S))
                    nc.scalar.activation(new[:, j.s3, :], cand[:, j.s3, :], ACT.Tanh, bias=gate_c[:, 2:3]
                                         ).then_inc(stage["candidate"], 1)
                j = k.back(7)
                if j.exists():
                    after(act, "shifted1", L1, j)
                    after(act, "state_out", L1, j)
                    after(act, "result", L1, j.back(S))
                    for a in range(A):
                        last = nc.scalar.activation(sub(res[:, j.s3, :], a), sub(state[:, j.s3, :], a), ACT.Identity,
                                                    bias=nb_1[:, j.slot, a:a + 1], scale=rs_1[:, j.slot, a:a + 1])
                    last.then_inc(stage["normed1"], 1)
                j = k.back(FINAL[L1] + 1)
                if j.exists():
                    after(act, "result", L1, j)
                    for a in range(A):
                        last = nc.scalar.activation(sub(seed[:, j.s3, :], a), sub(result[:, j.s3, :], a), ACT.Copy,
                                                    scale=col(SEED[L1], j, a))
                    last.then_inc(stage["seeded"], 1)
                j = k.back(3)
                if j.exists():
                    after(act, "gates_rh", L1, j)
                    after(act, "reset_hidden", L1, j.back(S))
                    nc.scalar.activation(r[:, j.s3, :], bank[4][:, :], ACT.Sigmoid, bias=gate_c[:, 0:1]
                                         ).then_inc(stage["reset"], 1)
                    after(act, "gates_zn", L1, j)
                    after(act, "kept", L1, j.back(S))
                    nc.scalar.activation(update[:, j.s3, :], bank[6][:, :], ACT.Sigmoid, bias=gate_c[:, 1:2]
                                         ).then_inc(stage["update"], 1)
                j = k.back(2)
                if j.exists():
                    after(act, "msg_turned", L1, j)
                    after(act, "gates_zn", L1, j.back(S))
                    nc.scalar.copy(u[:, j.s3, :], bank[3][:, :]).then_inc(stage["msg_out"], 1)

            for ph in range(PHASES):
                aggregate(ph)
                if ph == L0:
                    act.wait_ge(s_nodes, 1)
                    nc.scalar.activation(dis_inv[:, :], deg_gcn[:, :], ACT.Sqrt).then_inc(s_sqrt, 1)
                    act.wait_ge(s_roots, 1)
                if ph == L1:
                    act.wait_ge(s_gate_c, 1)
                    nc.scalar.preload_act_table(ACT.Sigmoid)
                    steps(act, dense_gru, FINAL[ph] + DEPTH)
                else:
                    dense(ph)

        @block.vector
        def _(dve):
            done = [0]

            def link(ins):
                done[0] += 1
                ins.then_inc(s_dve, 1)
                dve.wait_ge(s_dve, done[0])

            V = nc.vector
            V.memset(row_n[:, :], 0.0)
            for i in range(2):
                V.memset(pack[i], FILL)
                V.memset(packed[i], FILL)
            V.memset(own_col, 0.0)
            link(V.memset(own_lane, -1.0))
            dve.wait_ge(s_edges, 32)
            ends_i, ends_f = (src_i, dst_i), (src_f, dst_f)
            for i in range(2):
                last = V.tensor_copy(ends_f[i][0:EP, :], ends_i[i][0:EP, :])
            link(last)
            link(V.tensor_tensor(differ[0:EP, :], src_f[0:EP, :], dst_f[0:EP, :], ALU.not_equal))
            V.reduce_sum(row_n[0:EP, :], differ[0:EP, :], AX.X).then_inc(s_row_n, 1)
            dve.wait_ge(s_row_turned, 1)
            dve.wait_ge(s_base, 1)
            V.tensor_copy(deal_n[:, :], bank[7][:, 0:2])
            link(V.reduce_max(trips_f[:, 0:1], bank[3][0:1, 0:P], AX.X))
            V.tensor_scalar(trips_f[:, 1:2], trips_f[:, 0:1], float(2 * PR - 1), float(4 * PR), ALU.add, ALU.max)
            link(V.tensor_scalar(trips_f[:, 2:3], deal_n[0:1, 1:2], float(P * G2 - 1), float(3 * P * G2), ALU.add, ALU.max))
            link(V.tensor_copy(trips[:, 3:5], trips_f[:, 1:3]))
            V.tensor_scalar(trips[:, 0:1], trips[:, 3:4], (2 * PR).bit_length() - 1, None, ALU.logical_shift_right)
            link(V.tensor_scalar(trips[:, 1:2], trips[:, 4:5], (P * G2).bit_length() - 1, None, ALU.logical_shift_right))
            V.tensor_scalar(trips[:, 2:3], trips[:, 1:2], -1.0, None, ALU.add).then_inc(s_trips, 1)
            dve.wait_ge(s_const, 1)
            link(V.tensor_copy(rank, place_i))
            link(V.tensor_scalar(place_f[0:EP, :], rank[0:EP, 0:EJ], 65536.0, -BIG, ALU.mult, ALU.add))
            for i in range(2):
                last = V.tensor_tensor(pack[i][0:EP, :], place_f[0:EP, :], ends_f[i][0:EP, :], ALU.add)
            link(last)
            for i in range(2):
                last = V.tensor_tensor(pack[i][0:EP, :], pack[i][0:EP, :], differ[0:EP, :], ALU.mult)
            link(last)
            link(V.tensor_scalar(place_f[0:EP, :], differ[0:EP, :], -FILL, FILL, ALU.mult, ALU.add))
            for i in range(2):
                last = V.tensor_tensor(pack[i][0:EP, :], pack[i][0:EP, :], place_f[0:EP, :], ALU.add)
            link(last)
            dve.wait_ge(s_trips, 1)
            deals = dve.value_load(trips[0:1, 0:1], min_val=2, max_val=MAXR)
            turns = dve.value_load(trips[0:1, 1:2], min_val=3, max_val=MAXT)
            last_turn = dve.value_load(trips[0:1, 2:3], min_val=2, max_val=MAXT - 1)
            with dve.Fori(0, deals) as q:
                for h in range(2):
                    for i in range(2):
                        last = V.max(top8[:, i, :], pack[i])
                    last.then_inc(s_top, 1)
                    dve.wait_ge(s_top, q * 4 + (2 * h + 1))
                    for i in range(2):
                        V.tensor_copy(packed[i][:, bass.ds(q * (2 * PR) + h * PR, PR)], top8[:, i, :])
                    for i in range(2):
                        last = V.match_replace(pack[i], top8[:, i, :], pack[i], FILL)
                    last.then_inc(s_top, 1)
                    dve.wait_ge(s_top, q * 4 + (2 * h + 2))
                    alone(dve)
            V.tensor_scalar(empty, packed[0], -BIG, None, ALU.is_lt)
            for i in range(2):
                V.tensor_copy(packed_i[i], packed[i])
            V.tensor_scalar(rank, rank, deal_n[:, 0:1], None, ALU.add)
            link(V.tensor_copy(spare_f, spare_i))
            for i in range(2):
                V.tensor_scalar(pairs[:, :, i], packed_i[i], 0xFFFF, None, ALU.bitwise_and)
            link(V.tensor_copy(rank_i, rank))
            V.tensor_scalar(lane_i, rank_i, P - 1, None, ALU.bitwise_and)
            link(V.tensor_scalar(slot_i, rank_i, P.bit_length() - 1, None, ALU.logical_shift_right))
            V.tensor_copy(rank, lane_i)
            link(V.tensor_copy(deal_to, slot_i))
            link(V.scalar_tensor_tensor(out=deal_to, in0=rank, scalar=float(KC), in1=deal_to, op0=ALU.mult, op1=ALU.add))
            link(V.tensor_tensor(spare_f, spare_f, deal_to, ALU.subtract))
            link(V.tensor_tensor(spare_f, spare_f, empty, ALU.mult))
            link(V.tensor_tensor(deal_to, deal_to, spare_f, ALU.add))
            V.tensor_copy(deal_i, deal_to).then_inc(s_ranked, 1)

            def grid(lane, column, nodes, t1, t2, t3):
                V.tensor_scalar(t1, nodes, 2, P - 1, ALU.logical_shift_right, ALU.bitwise_and)
                V.tensor_scalar(t2, nodes, 9, 2, ALU.logical_shift_right, ALU.logical_shift_left)
                link(V.tensor_scalar(t3, nodes, A - 1, None, ALU.bitwise_and))
                V.tensor_copy(lane, t1)
                link(V.tensor_tensor(column, t2, t3, ALU.add))

            grid(own_lane[0:EP, :], own_col[0:EP, :], src_i[0:EP, :], *(t[0:EP, :] for t in own_i))
            link(V.tensor_scalar(place_f[0:EP, :], differ[0:EP, :], -1.0, 1.0, ALU.mult, ALU.add))
            link(V.tensor_tensor(own_lane[0:EP, :], own_lane[0:EP, :], place_f[0:EP, :], ALU.mult))
            link(V.tensor_tensor(own_lane[0:EP, :], own_lane[0:EP, :], differ[0:EP, :], ALU.subtract))
            dve.wait_ge(s_weights, 16 * 22)
            V.tensor_tensor(rows_bc[:, bl_, :], rows_bc[:, bl_, :], rows_bc[:, br_, :], ALU.add)
            link(V.tensor_tensor(rows_bc[:, bself_, :], rows_bc[:, bself_, :], rows_bc[:, bneigh_, :], ALU.add))
            V.memset(pass_mark_dve[:, :], 0.0).then_inc(s_biases, 1)

            def own_hot(j, slot, first=False):
                if not first:
                    dve.wait_ge(s_own_hist, j - (HOT - 1))
                V.tensor_scalar(hot_lane[:, slot, :], lane_f[:, :], own_lane[:, bass.ds(j, 1)], None, ALU.is_equal)
                V.tensor_scalar(hot_col[:, slot, :], col_f[:, :], own_col[:, bass.ds(j, 1)], None,
                                ALU.is_equal).then_inc(s_own_hot, 1)

            for j in range(HJ):
                own_hot(j, j % HOT, first=j < HOT)
            with dve.Fori(1, EJ // HJ) as q:
                for j in range(HJ):
                    own_hot(q * HJ + j, j % HOT)
            dve.wait_ge(s_own_hist, EJ)

            dve.wait_ge(s_lists_in, 16)
            V.tensor_copy(trash_kf, trash_k)
            ends = [packed[i][:, 0:KC] for i in range(2)]
            for i in range(2):
                last = V.tensor_copy(ends[i], dealt[:, :, i])
            link(last)
            link(V.tensor_scalar(empty_k, ends[0], 0.0, None, ALU.is_lt))
            V.tensor_tensor(empty_k, empty_k, trash_kf, ALU.mult)
            for i in range(2):
                last = V.tensor_scalar(ends[i], ends[i], 0.0, None, ALU.max)
            link(last)
            for i in range(2):
                V.tensor_copy(gidx[:, 1 - i, :], ends[i])
                last = V.tensor_tensor(key_f[:, i, :], ends[i], empty_k, ALU.add)
            link(last)
            for i in range(2):
                link(V.tensor_copy(key_i[3], key_f[:, i, :]))
                grid(key_lane[i], key_col[i], key_i[3], *key_i[0:3])

            def key_hot(c, slot, first=False):
                if not first:
                    dve.wait_ge(s_key_hist, c - 1)
                for d in range(2):
                    V.tensor_scalar(hot_lane[:, 2 * slot + d, :], lane_f[:, :], key_lane[d][:, bass.ds(c, 1)], None, ALU.is_equal)
                    last = V.tensor_scalar(hot_col[:, 2 * slot + d, :], col_f[:, :], key_col[d][:, bass.ds(c, 1)], None,
                                           ALU.is_equal)
                last.then_inc(s_key_hot, 1)

            def count_keys(ph, q, g, first=False):
                if ph == L0:
                    for c in range(C):
                        key_hot(q * G2 + (g * C + c), c % 2, first=first and c < 2)

            def numbers():
                dve.wait_ge(s_key_hist, turns * G2)
                link(V.tensor_copy(hist[0], bank[3][:, 0:COLS]))
                V.tensor_tensor(hist[1], bank[4][:, 0:COLS], hist[0], ALU.add)
                link(V.tensor_tensor(hist[2], bank[5][:, 0:COLS], hist[0], ALU.add))
                on_grid = COLS - A
                V.tensor_copy(own_n[:, 0:on_grid], hist[0][:, 0:on_grid])
                V.tensor_copy(deg_s[:, 0:on_grid], hist[1][:, 0:on_grid])
                V.tensor_copy(deg_d[:, 0:on_grid], hist[2][:, 0:on_grid]).then_inc(s_hist_out, 1)
                dve.wait_ge(s_hist_out, 1)
                dve.wait_ge(s_shift, 96)
                V.tensor_scalar(own_n1[:, :], own_n[:, :], 1.0, None, ALU.add)
                link(V.tensor_scalar(deg_gcn[:, :], deg_d[:, :], 1.0, None, ALU.add))
                V.tensor_scalar(inv_s[:, :], deg_s[:, :], 1.0, None, ALU.max).then_inc(s_nodes, 1)
                link(V.tensor_scalar(inv_d[:, :], deg_d[:, :], 1.0, None, ALU.max))
                V.reciprocal(inv_s[:, :], inv_s[:, :])
                link(V.reciprocal(inv_d[:, :], inv_d[:, :]))
                dve.wait_ge(s_sqrt, 1)
                link(V.reciprocal(dis[:, :], dis_inv[:, :]))
                link(V.tensor_tensor(dis[:, :], dis[:, :], deg_gcn[:, :], ALU.mult))
                link(V.tensor_tensor(dis_inv[:, :], dis_inv[:, :], dis[:, :], ALU.add))
                link(V.tensor_scalar(dis_inv[:, :], dis_inv[:, :], 0.5, None, ALU.mult))
                V.reciprocal(dis[:, :], dis_inv[:, :]).then_inc(s_roots, 1)

            def stage_in(ph, q, g, first=False):
                key = 0 if ph == L0 else 1
                at_ = bass.ds(q * G2 + g * C, C)
                if not first:
                    dve.wait_ge(landed[ph][g], q * (16 * C))
                V.tensor_copy(idx_now[:, g, :], gidx[:, key, at_])
                V.tensor_copy(key_now[:, g, :], key_f[:, key, at_]).then_inc(staged[ph], 1)

            def match(ph, q, g, first=False):
                room = g % 2
                dve.wait_ge(keys_turned[ph], q * 2 + (g + 1))
                if not first:
                    dve.wait_ge(summed_eq[ph], q * 2 + (g - 1))
                for c in range(C):
                    last = V.tensor_scalar(equal[:, room, c, :], bank[0][:, :], key_now[:, room, c:c + 1], None, ALU.is_equal)
                last.then_inc(matched[ph], 1)
                dve.wait_ge(matched[ph], q * 2 + (g + 1))
                for c in range(C):
                    n = (c + 1) * P
                    last = V.scalar_tensor_tensor(out=junk[:, c, 0:n], in0=equal[:, room, c, 0:n], scalar=1.0,
                                                  in1=earlier[:, c, 0:n], op0=ALU.mult, op1=ALU.mult,
                                                  accum_out=n_earlier[:, room, c:c + 1])
                last.then_inc(picked[ph], 1)
                V.tensor_tensor(pick[:, room, 0, :], trash_f[:, :], key_now[:, room, :], ALU.subtract)
                dve.wait_ge(picked[ph], q * 8 + (4 * g + 1))
                V.tensor_scalar(pick[:, room, 1, :], n_earlier[:, room, :], 1.0, None, ALU.min).then_inc(picked[ph], 1)
                dve.wait_ge(picked[ph], q * 8 + (4 * g + 2))
                V.tensor_tensor(pick[:, room, 2, :], pick[:, room, 0, :], pick[:, room, 1, :], ALU.mult).then_inc(picked[ph], 1)
                dve.wait_ge(picked[ph], q * 8 + (4 * g + 3))
                V.tensor_tensor(pick[:, room, 0, :], pick[:, room, 2, :], key_now[:, room, :], ALU.add).then_inc(picked[ph], 1)
                dve.wait_ge(picked[ph], q * 8 + (4 * g + 4))
                if not first:
                    dve.wait_ge(added[ph], q * (32 * C) + 16 * C * (g - 1))
                V.tensor_copy(to_now[:, room, :], pick[:, room, 0, :]).then_inc(to_ready[ph], 1)

            def aggregate(ph):
                stage_in(ph, 0, 0, first=True)
                stage_in(ph, 0, 1, first=True)
                match(ph, 0, 0, first=True)
                count_keys(ph, 0, 0, first=True)
                count_keys(ph, 0, 1)
                stage_in(ph, 1, 0)
                match(ph, 1, -1, first=True)
                count_keys(ph, 1, 0)
                stage_in(ph, 1, 1)
                match(ph, 1, 0)
                count_keys(ph, 1, 1)
                with dve.Fori(2, turns) as q:
                    stage_in(ph, q, 0)
                    match(ph, q, -1)
                    count_keys(ph, q, 0)
                    stage_in(ph, q, 1)
                    match(ph, q, 0)
                    count_keys(ph, q, 1)
                match(ph, last_turn, 1)
                if ph == L0:
                    numbers()

            def row_stats(ph, k, rows, bn6, tag=""):
                for a in range(A):
                    last = V.bn_stats(bn6[:, k.slot, a, :], sub(rows, a))
                last.then_inc(stage["stats" + tag], 1)

            def mean_variance(ph, k, bn6, mv, tag=""):
                after(dve, "stats" + tag, ph, k)
                alone(dve)
                for a in range(A):
                    last = V.bn_aggr(mv[:, k.slot, a, :], bn6[:, k.slot, a, :])
                last.then_inc(stage["aggr" + tag], 1)

            def variance_eps(ph, k, mv, ve, tag=""):
                after(dve, "aggr" + tag, ph, k)
                V.tensor_scalar(ve[:, k.slot, :], mv[:, k.slot, :, 1], LN_EPS, None, ALU.add).then_inc(stage["var_eps" + tag], 1)

            def shift(ph, k, mv, rs, nb, tag=""):
                V.scalar_tensor_tensor(out=nb[:, k.slot, :], in0=mv[:, k.slot, :, 0], scalar=-1.0, in1=rs[:, k.slot, :],
                                       op0=ALU.mult, op1=ALU.mult).then_inc(stage["shifted" + tag], 1)

            def norm_eps(ph, k):
                after(dve, "norm", ph, k)
                V.tensor_scalar(nrm_e[:, k.slot, :], nrm[:, k.slot, :], NORM_EPS[ph], None, ALU.add).then_inc(stage["norm_eps"], 1)

            def norm_inv(ph, k):
                after(dve, "norm_eps", ph, k)
                V.reciprocal(nrm_inv[:, k.slot, :], nrm_e[:, k.slot, :]).then_inc(stage["norm_inv"], 1)

            def residual_scaled(ph, k):
                x_ = extra[:, k.slot, :] if ph == CV1 else own[:, k.slot, :]
                after(dve, "norm_inv", ph, k)
                if ph == L0:
                    after(dve, "squared", ph, k)
                    rows = r[:, k.s3, :]
                else:
                    after(dve, "product", ph, k)
                    rows = product_bank(ph, k)
                if ph == CV1:
                    after(dve, "own_ready", ph, k)
                    after_stores(dve, ph, k.back(R))
                for a in range(A):
                    last = V.scalar_tensor_tensor(out=sub(res_of(ph, k), a), in0=sub(rows, a),
                                                  scalar=nrm_inv[:, k.slot, a:a + 1], in1=sub(x_, a),
                                                  op0=ALU.mult, op1=ALU.add)
                last.then_inc(stage["residual"], 1)

            def residual(ph, k):
                after(dve, "product", ph, k)
                after(dve, "own_ready", ph, k)
                V.tensor_tensor(res_of(ph, k), product_bank(ph, k)[:, :], extra[:, k.slot, :],
                                ALU.add).then_inc(stage["residual"], 1)

            def finish(ph, k):
                if ph in NORMED:
                    after(dve, "shifted", ph, k)
                else:
                    after(dve, "gelued", ph, k)
                if ph == L0:
                    after(dve, "summed", ph, k.back(R))
                after_stores(dve, ph, k.back(span(ph)))
                rs_ = (rsd if ph == L2 else rs)[:, k.slot, :]
                for a in range(A):
                    if ph in NORMED:
                        last = V.tensor_scalar(sub(result_of(ph, k), a), sub(res_of(ph, k), a), rs_[:, a:a + 1],
                                               nb[:, k.slot, a:a + 1], ALU.mult, ALU.add)
                    else:
                        last = V.tensor_scalar(sub(result_of(ph, k), a), sub(r[:, k.s3, :], a), col(dis, k, a), None, ALU.mult)
                last.then_inc(stage["result"], 1)

            def own_added(k):
                after_loads(dve, L0, k)
                for a in range(A):
                    last = V.scalar_tensor_tensor(out=sub(sm[:, k.s3, :], a), in0=sub(own[:, k.slot, :], a),
                                                  scalar=col(own_n, k, a), in1=sub(sm[:, k.s3, :], a),
                                                  op0=ALU.mult, op1=ALU.add)
                last.then_inc(stage["own_added"], 1)

            def prescale(ph, k):
                after_loads(dve, ph, k)
                after(dve, "turned", ph, k.back(S))
                for a in range(A):
                    last = V.tensor_scalar(sub(scaled[:, k.s3, :], a), sub(sm[:, k.s3, :], a), col(dis, k, a), None, ALU.mult)
                last.then_inc(stage["prescaled"], 1)

            def dense_normed(ph):
                end = FINAL[ph]

                def step(k):
                    early, late, j = k.back(end - 2), k.back(end - 1), k.back(end)
                    if ph == L0:
                        if early.exists():
                            norm_eps(ph, early)
                        if late.exists():
                            mean_variance(ph, late, bn6, mv)
                        if early.exists():
                            norm_inv(ph, early)
                        if j.exists():
                            after(dve, "rstd", ph, j)
                            shift(ph, j, mv, rs, nb)
                        if late.exists():
                            variance_eps(ph, late, mv, ve)
                        if k.exists():
                            own_added(k)
                        if early.exists():
                            residual_scaled(ph, early)
                    else:
                        if early.exists():
                            residual(ph, early)
                        if late.exists():
                            mean_variance(ph, late, bn6, mv)
                        if j.exists():
                            after(dve, "rstd", ph, j)
                            if ph == L2:
                                V.tensor_tensor(rsd[:, j.slot, :], rs[:, j.slot, :], dis[:, bass.ds(j.b * A, A)],
                                                ALU.mult).then_inc(stage["rstd_dis"], 1)
                            else:
                                shift(ph, j, mv, rs, nb)
                        if late.exists():
                            variance_eps(ph, late, mv, ve)
                        if ph == L2 and j.exists():
                            after(dve, "rstd_dis", ph, j)
                            shift(ph, j, mv, rsd, nb)
                    if j.exists():
                        finish(ph, j)
                    if early.exists():
                        after(dve, "residual", ph, early)
                        row_stats(ph, early, res_of(ph, early), bn6)

                steps(dve, step, end + DEPTH)

            def dense_gelu(ph):
                def step(k):
                    if k.back(4).exists():
                        norm_eps(ph, k.back(4))
                    if k.exists():
                        prescale(ph, k)
                    if k.back(4).exists():
                        norm_inv(ph, k.back(4))
                    if k.back(5).exists():
                        finish(ph, k.back(5))
                    if k.back(4).exists():
                        residual_scaled(ph, k.back(4))

                steps(dve, step, FINAL[ph] + DEPTH)

            def dense_gru(k):
                hidden, inner, outer, end = k.back(4), k.back(7), k.back(8), k.back(9)
                if hidden.exists():
                    j = hidden
                    after(dve, "reset", L1, j)
                    after(dve, "candidate", L1, j.back(S))
                    V.scalar_tensor_tensor(out=cand[:, j.s3, :], in0=bank[5][:, :], scalar=gate_b[:, 1, 2:3],
                                           in1=r[:, j.s3, :], op0=ALU.add, op1=ALU.mult).then_inc(stage["reset_hidden"], 1)
                if inner.exists():
                    mean_variance(L1, inner, bn6_1, mv_1, "1")
                if hidden.exists():
                    j = hidden
                    after(dve, "gates_zn", L1, j)
                    after(dve, "reset_hidden", L1, j)
                    V.tensor_tensor(cand[:, j.s3, :], cand[:, j.s3, :], bank[7][:, :], ALU.add).then_inc(stage["candidate_in"], 1)
                if inner.exists():
                    variance_eps(L1, inner, mv_1, ve_1, "1")
                if outer.exists():
                    j = outer
                    after(dve, "normed1", L1, j)
                    V.tensor_tensor(v3(res[:, j.s3, :]), v3(res[:, j.s3, :]), each(gamma_), ALU.mult).then_inc(stage["scaled1"], 1)
                j = k.back(1)
                if j.exists():
                    after(dve, "product", L1, j)
                    after(dve, "own_message", L1, j.back(S))
                    after(dve, "msg_turned", L1, j.back(S))
                    for a in range(A):
                        last = V.scalar_tensor_tensor(out=sub(scaled[:, j.s3, :], a), in0=rows_bc[:, bmsg_, :],
                                                      scalar=col(deg_d, j, a), in1=sub(bank[2], a), op0=ALU.mult, op1=ALU.add)
                    last.then_inc(stage["message"], 1)
                if outer.exists():
                    j = outer
                    after(dve, "scaled1", L1, j)
                    after(dve, "own_ready", L1, j)
                    V.tensor_tensor(res[:, j.s3, :], res[:, j.s3, :], extra[:, j.slot, :], ALU.add).then_inc(stage["residual"], 1)
                if end.exists():
                    after(dve, "rstd", L1, end)
                    shift(L1, end, mv, rs, nb)
                if inner.exists():
                    after(dve, "rstd1", L1, inner)
                    shift(L1, inner, mv_1, rs_1, nb_1, "1")
                if outer.exists():
                    after(dve, "residual", L1, outer)
                    row_stats(L1, outer, res[:, outer.s3, :], bn6)
                j = k.back(5)
                if j.exists():
                    after(dve, "kept", L1, j)
                    V.tensor_tensor(kept[:, j.s3, :], kept[:, j.s3, :], new[:, j.s3, :], ALU.add).then_inc(stage["state"], 1)
                if outer.exists():
                    mean_variance(L1, outer, bn6, mv)
                if end.exists():
                    finish(L1, end)
                if outer.exists():
                    variance_eps(L1, outer, mv, ve)
                j = k.back(6)
                if j.exists():
                    after(dve, "state_out", L1, j)
                    row_stats(L1, j, state[:, j.s3, :], bn6_1, "1")

            for ph in range(PHASES):
                if ph == L1:
                    dve.wait_ge(stage["summed"], NB)
                    V.tensor_copy(mean_col[:, :], bank[6][:, 0:1]).then_inc(s_mean, 1)
                aggregate(ph)
                if ph == L1:
                    dve.wait_ge(s_gate_mm, 1)
                    link(V.tensor_tensor(gate_c[:, :], bank[7][:, 0:3], gate_b[:, 0, :], ALU.add))
                    V.tensor_tensor(gate_c[:, 0:2], gate_c[:, 0:2], gate_b[:, 1, 0:2], ALU.add).then_inc(s_gate_c, 1)
                    steps(dve, dense_gru, FINAL[ph] + DEPTH)
                elif ph in NORMED:
                    dense_normed(ph)
                else:
                    dense_gelu(ph)


_INS = ['x', 'src', 'dst', 'L0_gnn_Wl', 'L0_gnn_bl', 'L0_gnn_Wr', 'L0_gnn_br', 'L1_gnn_W_msg', 'L1_gnn_b_msg',
        'L1_gnn_w_ih', 'L1_gnn_w_hh', 'L1_gnn_b_ih', 'L1_gnn_b_hh', 'L1_gnn_ln_gamma', 'L1_gnn_ln_beta',
        'L2_gnn_w_self', 'L2_gnn_b_self', 'L2_gnn_w_neigh', 'L2_gnn_b_neigh', 'L3_gnn_W1', 'L3_gnn_b1',
        'L3_gnn_W2', 'L3_gnn_b2', 'L3_gnn_W3', 'L3_gnn_b3']


def kernel(**inputs):
    import numpy as _np
    import concourse.bacc as _bacc
    from concourse import mybir as _mybir
    from concourse.bass_utils import run_bass_kernel_spmd as _run

    nc = _bacc.Bacc("TRN2", target_bir_lowering=False, num_devices=1)
    arrays, args = {}, []
    for name in _INS:
        a = _np.ascontiguousarray(inputs[name])
        arrays[f"in_{name}_dram"] = a
        args.append(nc.dram_tensor(f"in_{name}_dram", a.shape, _mybir.dt.from_np(a.dtype), kind="ExternalInput").ap())
    args.append(nc.dram_tensor("out_0_dram", (N, D), _mybir.dt.float32, kind="ExternalOutput").ap())
    build(nc, *args)
    r = _run(nc, [arrays], core_ids=[0])
    return r.results[0]["out_0_dram"]
```
